# Optimizing a Trainium2 kernel written in Bass

```python
import numpy as np
import jax
import jax.numpy as jnp

def _softmax(x, axis=-1):
    return jax.nn.softmax(x, axis=axis)

def _gelu(x):
    return jax.nn.gelu(x, approximate=True)

def _silu(x):
    return jax.nn.silu(x)

def _sigmoid(x):
    return jax.nn.sigmoid(x)

def _layernorm(x, axis=-1, eps=1e-05):
    m = jnp.mean(x, axis=axis, keepdims=True)
    v = jnp.var(x, axis=axis, keepdims=True)
    return (x - m) / jnp.sqrt(v + eps)

def _scatter_add(tgt, idx, src, axis=0):
    return tgt.at[idx].add(src)

def _segment_sum(src, seg, n):
    return jax.ops.segment_sum(src, seg, n)
kernel_name = 'mk_cond_seq_d2_seqx_r8_bf2983'

def setup_inputs(seed: int=0):
    np.random.seed(seed)
    _w = jnp.asarray

    def _rec_inputs():
        import jax
        import jax.numpy as jnp
        _rk = jax.random.key(seed)
        x = 1.648e-05 + 1 * jax.random.normal(jax.random.fold_in(_rk, 1), (8, 256, 144), jnp.float32)
        _lenS = 256 - jax.random.randint(jax.random.fold_in(_rk, 7), (8,), 0, max(1, 256 // 4) + 1, jnp.int32)
        _lenS2 = 256 - jax.random.randint(jax.random.fold_in(_rk, 8), (8,), 0, max(1, 256 // 4) + 1, jnp.int32)
        cond_1152 = 0.00914911 + 1.00357 * jax.random.normal(jax.random.fold_in(_rk, 11), (8, 144), jnp.float32)
        return (x, cond_1152)
    x, cond_1152 = _rec_inputs()

    def _L0_cond_setup():
        import jax, jax.numpy as jnp
        import numpy as np
        B, L, C = (8, 128, 144)
        H = 16
        D = C // H
        FF = int(C * 4.0)
        EPS = 1e-06

        def _layernorm(x):
            mu = jnp.mean(x, axis=-1, keepdims=True)
            var = jnp.mean(jnp.square(x - mu), axis=-1, keepdims=True)
            return (x - mu) * jax.lax.rsqrt(var + EPS)

        def _modulate(x, shift, scale):
            return x * (1.0 + scale) + shift

        def _attention(h, W_qkv, b_qkv, W_proj, b_proj):
            b, l, c = h.shape
            qkv = h @ W_qkv + b_qkv
            qkv = qkv.reshape(b, l, 3, H, D)
            q, k, v = (qkv[:, :, 0], qkv[:, :, 1], qkv[:, :, 2])
            scale = D ** (-0.5)
            scores = jnp.einsum('blhd,bmhd->bhlm', q * scale, k)
            attn = jax.nn.softmax(scores, axis=-1)
            o = jnp.einsum('bhlm,bmhd->blhd', attn, v).reshape(b, l, c)
            return o @ W_proj + b_proj
        key = jax.random.key(seed)
        ks = jax.random.split(key, 12)
        s = 0.02
        return {'x': jax.random.normal(ks[0], (B, L, C), jnp.float32), 'c': jax.random.normal(ks[1], (B, 1, C), jnp.float32), 'W_qkv': jax.random.normal(ks[2], (C, 3 * C), jnp.float32) * s, 'b_qkv': jnp.zeros((3 * C,), jnp.float32), 'W_proj': jax.random.normal(ks[3], (C, C), jnp.float32) * s, 'b_proj': jnp.zeros((C,), jnp.float32), 'W_fc1': jax.random.normal(ks[4], (C, FF), jnp.float32) * s, 'b_fc1': jnp.zeros((FF,), jnp.float32), 'W_fc2': jax.random.normal(ks[5], (FF, C), jnp.float32) * s, 'b_fc2': jnp.zeros((C,), jnp.float32), 'W_ada': jax.random.normal(ks[6], (C, 6 * C), jnp.float32) * s, 'b_ada': jnp.zeros((6 * C,), jnp.float32)}
    _L0_cond_all = _L0_cond_setup()
    _L0_cond_in = {k: v for k, v in _L0_cond_all.items() if k in ('W_qkv', 'b_qkv', 'W_proj', 'b_proj', 'W_fc1', 'b_fc1', 'W_fc2', 'b_fc2', 'W_ada', 'b_ada')}
    del _L0_cond_all

    def _L1_cond_setup():
        import jax, jax.numpy as jnp
        import numpy as np
        from jax.scipy.linalg import expm
        N, D, COND_DIM = (144, 64, 144)
        B, T = (16, 128)

        def _rotation(cond, W, b):
            v = jax.nn.silu(cond) @ W.T + b
            iu, ju = jnp.triu_indices(D, k=1)
            A = jnp.zeros((cond.shape[0], D, D), dtype=v.dtype)
            A = A.at[:, iu, ju].set(v).at[:, ju, iu].set(-v)
            return expm(A)
        key = jax.random.key(seed)
        k1, k2, k3, k4, k5 = jax.random.split(key, 5)
        x = jax.random.normal(k1, (B, T, N), dtype=jnp.float32)
        cond = jax.random.normal(k2, (B, COND_DIM), dtype=jnp.float32)
        P = jax.random.normal(k3, (N, D), dtype=jnp.float32)
        n_skew = D * (D - 1) // 2
        bound = 1.0 / np.sqrt(COND_DIM)
        W = jax.random.uniform(k4, (n_skew, COND_DIM), minval=-bound, maxval=bound, dtype=jnp.float32)
        b = jax.random.uniform(k5, (n_skew,), minval=-bound, maxval=bound, dtype=jnp.float32)
        return {'x': x, 'cond': cond, 'P': P, 'W': W, 'b': b}
    _L1_cond_all = _L1_cond_setup()
    _L1_cond_in = {k: v for k, v in _L1_cond_all.items() if k in ('P', 'W', 'b')}
    del _L1_cond_all
    return {'x': x, 'cond_1152': cond_1152, 'L0_cond_W_qkv': _L0_cond_in['W_qkv'], 'L0_cond_b_qkv': _L0_cond_in['b_qkv'], 'L0_cond_W_proj': _L0_cond_in['W_proj'], 'L0_cond_b_proj': _L0_cond_in['b_proj'], 'L0_cond_W_fc1': _L0_cond_in['W_fc1'], 'L0_cond_b_fc1': _L0_cond_in['b_fc1'], 'L0_cond_W_fc2': _L0_cond_in['W_fc2'], 'L0_cond_b_fc2': _L0_cond_in['b_fc2'], 'L0_cond_W_ada': _L0_cond_in['W_ada'], 'L0_cond_b_ada': _L0_cond_in['b_ada'], 'L1_cond_P': _L1_cond_in['P'], 'L1_cond_W': _L1_cond_in['W'], 'L1_cond_b': _L1_cond_in['b']}

def reference(x, cond_1152, L0_cond_W_qkv, L0_cond_b_qkv, L0_cond_W_proj, L0_cond_b_proj, L0_cond_W_fc1, L0_cond_b_fc1, L0_cond_W_fc2, L0_cond_b_fc2, L0_cond_W_ada, L0_cond_b_ada, L1_cond_P, L1_cond_W, L1_cond_b):
    import jax
    import jax.numpy as jnp

    def _L0_cond_ref(x, c, W_qkv, b_qkv, W_proj, b_proj, W_fc1, b_fc1, W_fc2, b_fc2, W_ada, b_ada):
        import jax, jax.numpy as jnp
        import numpy as np
        B, L, C = (8, 128, 144)
        H = 16
        D = C // H
        FF = int(C * 4.0)
        EPS = 1e-06

        def _layernorm(x):
            mu = jnp.mean(x, axis=-1, keepdims=True)
            var = jnp.mean(jnp.square(x - mu), axis=-1, keepdims=True)
            return (x - mu) * jax.lax.rsqrt(var + EPS)

        def _modulate(x, shift, scale):
            return x * (1.0 + scale) + shift

        def _attention(h, W_qkv, b_qkv, W_proj, b_proj):
            b, l, c = h.shape
            qkv = h @ W_qkv + b_qkv
            qkv = qkv.reshape(b, l, 3, H, D)
            q, k, v = (qkv[:, :, 0], qkv[:, :, 1], qkv[:, :, 2])
            scale = D ** (-0.5)
            scores = jnp.einsum('blhd,bmhd->bhlm', q * scale, k)
            attn = jax.nn.softmax(scores, axis=-1)
            o = jnp.einsum('bhlm,bmhd->blhd', attn, v).reshape(b, l, c)
            return o @ W_proj + b_proj
        ada = jax.nn.silu(c) @ W_ada + b_ada
        shift_msa, scale_msa, gate_msa, shift_mlp, scale_mlp, gate_mlp = jnp.split(ada, 6, axis=-1)
        h = _modulate(_layernorm(x), shift_msa, scale_msa)
        x = x + gate_msa * _attention(h, W_qkv, b_qkv, W_proj, b_proj)
        h = _modulate(_layernorm(x), shift_mlp, scale_mlp)
        mlp = jax.nn.gelu(h @ W_fc1 + b_fc1, approximate=True) @ W_fc2 + b_fc2
        x = x + gate_mlp * mlp
        return x

    def _L1_cond_ref(x, cond, P, W, b):
        import jax, jax.numpy as jnp
        import numpy as np
        from jax.scipy.linalg import expm
        N, D, COND_DIM = (144, 64, 144)
        B, T = (16, 128)

        def _rotation(cond, W, b):
            v = jax.nn.silu(cond) @ W.T + b
            iu, ju = jnp.triu_indices(D, k=1)
            A = jnp.zeros((cond.shape[0], D, D), dtype=v.dtype)
            A = A.at[:, iu, ju].set(v).at[:, ju, iu].set(-v)
            return expm(A)
        U, _ = jnp.linalg.qr(P)
        R = _rotation(cond, W, b)
        z = jnp.einsum('btn,nd->btd', x, U)
        z_rot = jnp.einsum('btd,bde->bte', z, R)
        x_rot = x + jnp.einsum('btd,nd->btn', z_rot - z, U)
        return x_rot
    x = _L0_cond_ref(x, cond_1152[:, None, :], L0_cond_W_qkv, L0_cond_b_qkv, L0_cond_W_proj, L0_cond_b_proj, L0_cond_W_fc1, L0_cond_b_fc1, L0_cond_W_fc2, L0_cond_b_fc2, L0_cond_W_ada, L0_cond_b_ada)
    x = _L1_cond_ref(x, cond_1152, L1_cond_P, L1_cond_W, L1_cond_b)
    return x

_drawn_inputs = setup_inputs


def setup_inputs(seed=0):
    import zlib

    import numpy as np

    out = dict(_drawn_inputs(seed))
    spreads = {'L0_cond_b_qkv': (0.0, 0.8),
     'L0_cond_b_proj': (0.0, 0.503),
     'L0_cond_b_fc1': (0.0, 0.8),
     'L0_cond_b_fc2': (0.0, 0.49),
     'L0_cond_b_ada': (0.0, 0.503)}
    factors = {'L0_cond_W_qkv': 8.0,
     'L0_cond_W_proj': 8.0,
     'L0_cond_W_fc1': 5.329,
     'L0_cond_W_fc2': 4.932,
     'L0_cond_W_ada': 2.719}
    for name, (base, spread) in spreads.items():
        noise = np.random.default_rng([zlib.crc32(name.encode()), seed]).standard_normal(out[name].shape)
        drawn = base * np.exp(spread * noise) if base else spread * noise
        out[name] = jnp.asarray(drawn.astype(out[name].dtype))
    for name, factor in factors.items():
        out[name] = (out[name] * factor).astype(out[name].dtype)
    return out
```

```python
from contextlib import ExitStack

import concourse.bass as bass
from concourse import mybir

F32 = mybir.dt.float32
BF16 = mybir.dt.bfloat16
ACT = mybir.ActivationFunctionType
ALU = mybir.AluOpType
AX = mybir.AxisListType


def cond_seq_program(nc, x, cond, w_qkv, b_qkv, w_proj, b_proj, w_fc1, b_fc1, w_fc2, b_fc2,
                     w_ada, b_ada, p_mat, w_rot, b_rot, out):
    B, L, C = x.shape
    H = 16
    D = C // H
    FF = w_fc1.shape[1]
    R = p_mat.shape[1]
    NV = w_rot.shape[0]
    LT = L // 128
    NT = B * LT
    CB = C - 128
    QC = 96
    NQ = 2 * C // QC
    FC = FF // 96
    G = H // 4
    KS = 96
    ATT_SCALE = float(D) ** -0.5
    ATT_EPS = 1e-6
    SQUARINGS = 14
    VR = 16
    VP = NV // VR

    Q_RUNS = [(0, 1, 3), (1, 1, 2), (2, 1, 1)]
    K_RUNS = [(0, 3, 1), (0, 2, 1), (0, 1, 1)]

    ctx = ExitStack()
    with ctx:
        def sb(name, shape, dt=F32):
            return ctx.enter_context(nc.sbuf_tensor(name, shape, dt))

        def pb(name, shape, dt=F32):
            return ctx.enter_context(nc.psum_tensor(name, shape, dt))

        def sem(name):
            return ctx.enter_context(nc.semaphore(name))

        scr_ada = nc.dram_tensor("scr_ada", [B, 6 * C], F32, kind="Internal").ap()
        scr_qk = nc.dram_tensor("scr_qk", [3, 2 * C, L], BF16, kind="Internal").ap()

        ident = sb("ident", [128, 128])
        identb = sb("identb", [128, 128], BF16)
        half_i = sb("half_i", [R, B, R])
        ones_row = sb("ones_row", [1, 128])
        wqkv_a = sb("wqkv_a", [128, 3 * C])
        wqkv_b = sb("wqkv_b", [CB + 1, 3 * C])
        wqk_a = sb("wqk_a", [128, 2 * C])
        wqk_b = sb("wqk_b", [CB + 1, 2 * C])
        wp_a = sb("wp_a", [128, C])
        wp_b = sb("wp_b", [CB + 1, C])
        wfc1_a = sb("wfc1_a", [128, FF])
        wfc1_b = sb("wfc1_b", [CB + 1, FF])
        wfc2 = sb("wfc2", [97, FC, C])
        wada_a = sb("wada_a", [128, 6 * C])
        wada_b = sb("wada_b", [CB + 1, 6 * C])
        pa = sb("pa", [128, R])
        pbm = sb("pbm", [CB, R])
        wr = sb("wr", [VP, VR, C])
        br = sb("br", [1, NV])
        wrT_a = sb("wrT_a", [128, NV])
        wrT_b = sb("wrT_b", [CB, NV])
        csb = sb("csb", [B, C])
        cexp = sb("cexp", [B, C])
        cden = sb("cden", [B, C])
        crec = sb("crec", [B, C])
        silu = sb("silu", [B, C + 1])
        siluT_a = sb("siluT_a", [128, B])
        siluT_b = sb("siluT_b", [CB + 1, B])
        ada = sb("ada", [B, 6 * C])
        gates = sb("gates", [128, 2, B, C])
        ms = sb("ms", [128, 2, 2 * C])
        vsb = wr[0:B, :, :].rearrange("b r k -> b (r k)")[:, 0:NV]
        up = sb("up", [R, B, R])
        aa = sb("aa", [R, B, 2, R])
        a2 = sb("a2", [R, B, R])
        q0 = sb("q0", [R, B, R])
        qq = sb("qq", [R, B, 2, R])
        ef = sb("ef", [R, B, 2, R])
        efs = sb("efs", [R, B, R])
        fq = sb("fq", [R, B, C])
        gm = sb("gm", [R, 2 * R + 1])
        ew = sb("ew", [R, R])
        rp = sb("rp", [1, 1])
        linv = sb("linv", [R, R])
        linvT = sb("linvT", [R, R])
        pT = sb("pT", [R, C])
        qtu = sb("qtu", [R, C])
        qsq = sb("qsq", [R, C])
        qn = sb("qn", [R, 8])
        qt = sb("qt", [R, C])
        qa = sb("qa", [128, R])
        qb = sb("qb", [CB, R])
        sm = sb("sm", [R, 2, R + 1])
        ew2 = sb("ew2", [R, 2, R])
        sg = sb("sg", [1, R])
        st1 = sb("st1", [1, 4])
        ss = sb("ss", [R, R])
        xin = sb("xin", [128, NT, C])
        bst = sb("bst", [128, NT, 6])
        mv = sb("mv", [128, NT, 2])
        lnv = sb("lnv", [128, NT])
        lns = sb("lns", [128, NT])
        lnr = sb("lnr", [128, NT])
        lnt = sb("lnt", [128, NT])
        lnu = sb("lnu", [128, NT])
        rstd = sb("rstd", [128, NT])
        hb = sb("hb", [128, LT, C])
        hs = sb("hs", [128, LT, C])
        h = sb("h", [128, LT, C + 1])
        hTa = sb("hTa", [128, 2, L])
        hTb = sb("hTb", [CB + 1, 2, L])
        qk32 = sb("qk32", [QC, NQ, L])
        qkr = sb("qkr", [QC, NQ, L])
        parts = sb("parts", [QC, 3, NQ, L], BF16)
        qs = sb("qs", [128, 2, H, L], BF16)
        ks = sb("ks", [128, 2, H, L], BF16)
        ve = sb("ve", [128, 2, LT, H, 32])
        nm = sb("nm", [128, LT, H])
        nmb = sb("nmb", [128, LT, 2, H], BF16)
        nmT = sb("nmT", [2 * H, L], BF16)
        pex = sb("pex", [128, 4, 4, L])
        oT = sb("oT", [128, G, L])
        rden = sb("rden", [128, LT, H])
        otok = sb("otok", [128, LT, C + 1])
        oTa = sb("oTa", [128, L])
        oTb = sb("oTb", [CB + 1, L])
        res = sb("res", [128, LT, C])
        gT = pex[0:97, :, :, :].rearrange("p a b l -> p (a b) l")[:, 0:12, :].rearrange("p (s c) l -> p s c l", s=2)
        x2Ta = sb("x2Ta", [128, L])
        x2Tb = sb("x2Tb", [CB, L])
        zT = sb("zT", [R, L])
        x2c = sb("x2c", [128, 2, LT, C])
        osb = sb("osb", [128, 2, LT, C])

        ps = [pb(f"ps{i}", [128, 512]) for i in range(2)]
        pst = [pb(f"pst{i}", [128, 4, L]) for i in range(2)]
        m6 = pb("m6", [128, 512])
        m7 = pb("m7", [128, 512])
        misc = {6: m6, 7: m7}

        S = {}

        def s(name):
            if name not in S:
                S[name] = sem(name)
            return S[name]

        A_STAGES = {"P": -1, "X": 0, "M": 1, "F": 2, "N": 3}
        A_USES = {6: [("qk01", "F"), ("tt0", "P"), ("qk2", "F"), ("oc", "P"), ("hT", "N"), ("nmT", "M")],
                  7: [("tt1", "P"), ("v", "M"), ("proj", "P"), ("oT0", "X"), ("oT1", "X"), ("oT2", "X"), ("oT3", "X")]}
        A_FIRST, A_LAST = -3, B
        B_STAGES = {"R": -1, "D": 0, "U": 1, "N": 2}
        B_USES = {6: [("x2T", "R"), ("hT", "N"), ("w", "R")], 7: [("fc2", "D"), ("z", "R")]}
        B_FIRST, B_LAST = -2, B

        class Shared:

            def __init__(self, stages, uses, first, base):
                self.where = {n: (bank, i, stages[st]) for bank, names in uses.items() for i, (n, st) in enumerate(names)}
                self.n = {bank: len(names) for bank, names in uses.items()}
                self.first, self.base = first, base

            def at(self, name, b):
                bank, i, offset = self.where[name]
                return bank, (b - offset - self.first) * self.n[bank] + self.base[bank] + i

            def claim(self, pe, name, b):
                bank, k = self.at(name, b)
                if not (isinstance(k, int) and k == 0):
                    pe.wait_ge(s(f"bank{bank}_drained"), k)
                return misc[bank]

            def filled(self, ins, name):
                ins.then_inc(s(f"bank{self.where[name][0]}_filled"), 1)

            def skip(self, pe, name, b):
                self.claim(pe, name, b)
                pe.sem_inc(s(f"bank{self.where[name][0]}_filled"), 1)
                pe.sem_inc(s(f"bank{self.where[name][0]}_drained"), 1)

            def await_fill(self, eng, name, b):
                bank, k = self.at(name, b)
                eng.wait_ge(s(f"bank{bank}_filled"), k + 1)
                return misc[bank]

            def drained(self, ins, name):
                ins.then_inc(s(f"bank{self.where[name][0]}_drained"), 1)

            def await_drain(self, eng, name, b):
                bank, k = self.at(name, b)
                eng.wait_ge(s(f"bank{bank}_drained"), k + 1)

        def settled(eng, name):
            eng.sem_inc(s(f"{name}_passed"), 1)

        UA = Shared(A_STAGES, A_USES, A_FIRST, {6: 0, 7: 0})
        UB = Shared(B_STAGES, B_USES, B_FIRST, {bank: (A_LAST - A_FIRST + 1) * len(names) for bank, names in A_USES.items()})

        def real(b):
            return not isinstance(b, int) or 0 <= b < B

        def later(b):
            return not isinstance(b, int) or b > 0

        def run(eng, first, last, lo, hi, turn):
            for t in range(first, lo):
                turn(t, t % 2)
            with eng.Fori(0, (hi - lo) // 2) as i:
                for u in range(2):
                    turn(i * 2 + (lo + u), (lo + u) % 2)
            for t in range(hi, last + 1):
                turn(t, t % 2)

        A_TURNS = (A_FIRST, A_LAST, 1, 5)
        B_TURNS = (B_FIRST, B_LAST, 1, 5)

        block = ctx.enter_context(nc.Block())

        @block.sync
        def _(sp):
            sp.sem_inc(s("out_written"), 16)
            sp.dma_start(csb[:, :], cond).then_inc(s("cond_loaded"), 16)
            sp.dma_start(pa[:, :], p_mat[0:128, :]).then_inc(s("p_loaded"), 16)
            sp.dma_start(pbm[:, :], p_mat[128:C, :]).then_inc(s("p_loaded"), 16)
            sp.dma_start(wada_a[:, :], w_ada[0:128, :]).then_inc(s("wada_loaded"), 16)
            sp.dma_start(wada_b[0:CB, :], w_ada[128:C, :]).then_inc(s("wada_loaded"), 16)
            sp.dma_start(wada_b[CB:CB + 1, :], b_ada.rearrange("(a n) -> a n", a=1)).then_inc(s("wada_loaded"), 16)
            sp.dma_start(wr[:, :, :], w_rot.rearrange("(p r) k -> p r k", r=VR)).then_inc(s("wr_loaded"), 16)
            sp.dma_start(br[:, :], b_rot.rearrange("(a n) -> a n", a=1)).then_inc(s("wr_loaded"), 16)
            xv = x.rearrange("b (t p) c -> p (b t) c", p=128)
            for q in range(2):
                sp.dma_start(xin[:, 8 * q:8 * q + 8, :], xv[:, 8 * q:8 * q + 8, :]).then_inc(s("x_loaded"), 16)
            sp.dma_start(wqkv_a[:, :], w_qkv[0:128, :]).then_inc(s("wqkv_loaded"), 16)
            sp.dma_start(wqkv_b[0:CB, :], w_qkv[128:C, :]).then_inc(s("wqkv_loaded"), 16)
            sp.dma_start(wqkv_b[CB:CB + 1, :], b_qkv.rearrange("(a n) -> a n", a=1)).then_inc(s("wqkv_loaded"), 16)
            sp.dma_start(wp_a[:, :], w_proj[0:128, :]).then_inc(s("wp_loaded"), 16)
            sp.dma_start(wp_b[0:CB, :], w_proj[128:C, :]).then_inc(s("wp_loaded"), 16)
            sp.dma_start(wp_b[CB:CB + 1, :], b_proj.rearrange("(a n) -> a n", a=1)).then_inc(s("wp_loaded"), 16)
            sp.dma_start(wfc1_a[:, :], w_fc1[0:128, :]).then_inc(s("mlp_loaded"), 16)
            sp.dma_start(wfc1_b[0:CB, :], w_fc1[128:C, :]).then_inc(s("mlp_loaded"), 16)
            sp.dma_start(wfc1_b[CB:CB + 1, :], b_fc1.rearrange("(a n) -> a n", a=1)).then_inc(s("mlp_loaded"), 16)
            sp.dma_start(wfc2[0:96, :, :], w_fc2.rearrange("(c p) n -> p c n", p=96)).then_inc(s("mlp_loaded"), 16)
            sp.dma_start(wfc2[96:97, FC - 1, :], b_fc2.rearrange("(a n) -> a n", a=1)).then_inc(s("mlp_loaded"), 16)
            sp.wait_ge(s("ada_ready"), 2)
            sp.dma_start(scr_ada, ada[:, :]).then_inc(s("ada_written"), 16)
            sp.wait_ge(s("ada_written"), 16)
            for i, at in enumerate((2, 5)):
                sp.dma_start(gates[:, i, :, :], scr_ada[:, at * C:at * C + C].partition_broadcast(128)).then_inc(s("gates_loaded"), 16)
            sp.wait_ge(s("v_ready"), 4)
            sp.wait_ge(s("up_zeroed"), 1)
            at = 0
            for i in range(R - 1):
                n = R - 1 - i
                sp.dma_start(up[i:i + 1, :, i + 1:R], vsb[:, at:at + n], allow_slow_non_contiguous=(n == 1)).then_inc(s("up_loaded"), 16)
                at += n

            def modulation(b, slot, at, n):
                if later(n):
                    sp.wait_ge(s("ms_loaded"), n * 16)
                    settled(sp, "sp")
                if not isinstance(n, int) or n >= 2:
                    sp.wait_ge(s("h_ready"), n - 1)
                settled(sp, "sp")
                sp.dma_start(ms[:, slot, :], scr_ada[bass.ds(b, 1), at:at + 2 * C].rearrange("a n -> (a n)").partition_broadcast(128)
                             ).then_inc(s("ms_loaded"), 16)

            def turn_a(t, par):
                if real(t + 3):
                    modulation(t + 3, (par + 1) % 2, 0, t + 3)
                if real(t + 2):
                    b = t + 2
                    UA.await_drain(sp, "qk2", b)
                    settled(sp, "sp")
                    if later(b):
                        sp.wait_ge(s("stacks_loaded"), b * 96)
                        settled(sp, "sp")
                    sp.dma_start(scr_qk[0].rearrange("(c p) n -> p c n", p=QC), parts[:, 0, :, :]).then_inc(s("parts_written"), 16)
                    for i, name in enumerate(("mid_ready", "low_ready")):
                        sp.wait_ge(s(name), b + 1)
                        settled(sp, "sp")
                        sp.dma_start(scr_qk[i + 1].rearrange("(c p) n -> p c n", p=QC), parts[:, i + 1, :, :]).then_inc(s("parts_written"), 16)
                    sp.wait_ge(s("parts_written"), b * 48 + 48)
                    settled(sp, "sp")
                    if real(t):
                        sp.wait_ge(s("exp_done"), t * 8 + 10)
                        settled(sp, "sp")
                    qkv = scr_qk.rearrange("t (k d h) n -> t k d (h n)", k=2, d=D)
                    for stack, which, runs in ((qs, 0, Q_RUNS), (ks, 1, K_RUNS)):
                        row = 0
                        for part, n, repeat in runs:
                            src = qkv[part:part + n, which]
                            if repeat > 1:
                                src = src.to_broadcast([repeat, D, H * L])
                            rows = D * n * repeat
                            sp.dma_start(stack[row:row + rows, par, :, :].rearrange("p h l -> p (h l)"), src).then_inc(s("stacks_loaded"), 16)
                            row += rows
                if real(t + 1):
                    b = t + 1
                    UA.await_drain(sp, "nmT", b)
                    settled(sp, "sp")
                    sp.dma_start(qs[KS:KS + 2, (par + 1) % 2, :, :].rearrange("t h l -> t (h l)"), nmT[:, :]).then_inc(s("shift_loaded"), 16)

            def turn_b(t, par):
                if real(t + 2):
                    modulation(t + 2, par, 3 * C, t + 2 + B)
                if real(t - 1):
                    sp.wait_ge(s("out_ready"), t)
                    settled(sp, "sp")
                    if not isinstance(t, int) or t >= 2:
                        sp.wait_ge(s("out_written"), t * 16)
                    sp.dma_start(out[bass.ds(t - 1, 1)].rearrange("a (t p) c -> p (a t) c", p=128), osb[:, (par + 1) % 2, :, :]).then_inc(s("out_written"), 16)

            run(sp, *A_TURNS, turn_a)
            run(sp, *B_TURNS, turn_b)
            sp.wait_ge(s("out_written"), 16 * B + 16)

        @block.gpsimd
        def _(pool):
            def zero_then_select(t, view, pattern, base, fill, name):
                nc.gpsimd.memset(t, 0.0).then_inc(s(name), 1)
                pool.wait_ge(s(name), 1)
                nc.gpsimd.affine_select(out=view, in_=view, compare_op=ALU.not_equal, fill=fill, base=base,
                                        pattern=pattern, channel_multiplier=1).then_inc(s(name), 1)

            zero_then_select(ident[:, :], ident[:, :], [[-1, 128]], 0, 1.0, "ident_ready")
            nc.gpsimd.memset(silu[:, C:C + 1], 1.0).then_inc(s("ones_ready"), 1)
            nc.gpsimd.memset(ones_row[:, :], 1.0).then_inc(s("ones_ready"), 1)
            nc.gpsimd.memset(up[:, :, :], 0.0).then_inc(s("up_zeroed"), 1)
            zero_then_select(gm[:, :], gm[:, R + 1:2 * R + 1], [[-1, R]], 0, 1.0, "gm_ready")
            zero_then_select(ew[:, :], ew[:, :], [[-1, R]], -1, 1.0, "ew_ready")
            pool.wait_ge(s("ew_ready"), 2)
            nc.gpsimd.memset(ew[0:1, R - 1:R], 1.0).then_inc(s("ew_ready"), 1)
            zero_then_select(ew2[:, :, :], ew2[:, :, :], [[0, 2], [-1, R]], -1, 1.0, "ew2_ready")
            nc.gpsimd.memset(sm[:, :, :], 0.0).then_inc(s("sm_zeroed"), 1)
            zero_then_select(half_i[:, :, :], half_i[:, :, :], [[0, B], [-1, R]], 0, 0.5, "half_ready")
            nc.gpsimd.memset(h[:, :, C:C + 1], 1.0).then_inc(s("h_one"), 1)
            nc.gpsimd.memset(otok[:, :, C:C + 1], 1.0).then_inc(s("h_one"), 1)
            nc.gpsimd.memset(qs[:, :, :, :], 0.0).then_inc(s("stacks_zeroed"), 1)
            nc.gpsimd.memset(ks[0:KS, :, :, :], 0.0).then_inc(s("stacks_zeroed"), 1)
            pool.wait_ge(s("stacks_zeroed"), 2)
            nc.gpsimd.memset(ks[KS:128, :, :, :], 1.0).then_inc(s("stacks_zeroed"), 1)
            pool.wait_ge(s("stacks_zeroed"), 3)
            nc.gpsimd.memset(ve[:, :, :, :, :], 0.0).then_inc(s("ve_zeroed"), 1)
            pool.wait_ge(s("ve_zeroed"), 1)
            nc.gpsimd.memset(ve[:, :, :, :, D:D + 1], 1.0).then_inc(s("ve_zeroed"), 1)
            pool.wait_ge(s("ident_ready"), 2)
            nc.gpsimd.tensor_copy(identb[:, :], ident[:, :]).then_inc(s("identb_ready"), 1)

            pool.sem_inc(s("x1_ready"), 1)

            def wide(v):
                return v.unsqueeze(1).to_broadcast([128, LT, C])

            def modulate(n, slot, u, b):
                pool.wait_ge(s("normed"), n + 1)
                pool.wait_ge(s("ms_loaded"), n * 16 + 16)
                if later(n):
                    pool.wait_ge(s("h_ready"), n)
                nc.gpsimd.tensor_tensor(hs[:, :, :], hb[:, :, :], wide(ms[:, slot, C:2 * C]), ALU.mult).then_inc(s("scaled"), 1)
                pool.wait_ge(s("scaled"), n + 1)
                if later(b):
                    u.await_drain(pool, "hT", b - 1)
                nc.gpsimd.tensor_tensor(h[:, :, 0:C], hs[:, :, :], wide(ms[:, slot, 0:C]), ALU.add).then_inc(s("h_ready"), 1)

            def turn_a(t, par):
                if real(t + 2):
                    b = t + 2
                    UA.await_drain(pool, "qk2", b)
                    nc.gpsimd.tensor_tensor(qkr[:, :, :], qk32[:, :, :], parts[:, 0, :, :], ALU.subtract).then_inc(s("rest_ready"), 1)
                    pool.wait_ge(s("mid_ready"), b + 1)
                    if later(b):
                        pool.wait_ge(s("parts_written"), b * 48)
                    nc.gpsimd.tensor_tensor(parts[:, 2, :, :], qkr[:, :, :], parts[:, 1, :, :], ALU.subtract).then_inc(s("low_ready"), 1)
                if real(t + 3):
                    modulate(t + 3, (par + 1) % 2, UA, t + 3)
                if real(t - 1):
                    UA.await_drain(pool, "proj", t - 1)
                    xb = xin[:, bass.ds((t - 1) * LT, LT), :]
                    nc.gpsimd.tensor_tensor(xb, xb, res[:, :, :], ALU.add).then_inc(s("x1_ready"), 1)

            def turn_b(t, par):
                if real(t):
                    UB.await_drain(pool, "fc2", t)
                    if not isinstance(t, int) or t >= 2:
                        pool.wait_ge(s("out_ready"), t - 1)
                    nc.gpsimd.tensor_tensor(x2c[:, par, :, :], xin[:, bass.ds(t * LT, LT), :], res[:, :, :], ALU.add).then_inc(s("x2_ready"), 1)
                if real(t + 2):
                    modulate(t + 2 + B, par, UB, t + 2)

            run(pool, *A_TURNS, turn_a)
            run(pool, *B_TURNS, turn_b)

        @block.scalar
        def _(act):
            act.sem_inc(s("exp_done"), 2)
            act.wait_ge(s("cond_loaded"), 16)
            nc.scalar.activation(cexp[:, :], csb[:, :], ACT.Exp, scale=-1.0).then_inc(s("cexp_ready"), 1)
            act.wait_ge(s("siluT_filled"), 1)
            nc.scalar.copy(siluT_a[:, :], ps[0][:, 0:B]).then_inc(s("siluT_ready"), 1)
            nc.scalar.copy(siluT_b[:, :], ps[0][0:CB + 1, B:2 * B]).then_inc(s("siluT_ready"), 1)
            for i in range(4):
                act.wait_ge(s("wrTa_filled"), i + 1)
                nc.scalar.copy(wrT_a[:, :].rearrange("k (p r) -> k r p", r=VR)[:, 4 * i:4 * i + 4, :],
                               pst[i % 2][:, 0:2, :].rearrange("p a l -> p (a l)")[:, 0:4 * VP]
                               .rearrange("k (r p) -> k r p", p=VP)).then_inc(s("wrTa_ready"), 1)
            for i in range(4):
                act.wait_ge(s("v_filled"), i + 1)
                nc.scalar.copy(vsb[:, 504 * i:504 * i + 504], misc[6 + i % 2][0:B, 0:504]).then_inc(s("v_ready"), 1)
            act.wait_ge(s("lnv_ready"), 1)
            nc.scalar.activation(lns[:, :], lnv[:, :], ACT.Sqrt).then_inc(s("lns_ready"), 1)
            act.wait_ge(s("qn_ready"), 1)
            nc.scalar.activation(qn[:, 1:2], qn[:, 0:1], ACT.Sqrt).then_inc(s("qn_root"), 1)


            def evac_hT(u, b, slot):
                m = u.await_fill(act, "hT", b)
                if u is UA and (not isinstance(b, int) or b >= 2):
                    UA.await_drain(act, "v", b - 2)
                if u is UB and (not isinstance(b, int) or b >= 2):
                    act.wait_ge(s("fc1_filled"), b - 1)
                nc.scalar.copy(hTa[:, slot, :], m[:, 0:L])
                u.drained(nc.scalar.copy(hTb[:, slot, :], m[0:CB + 1, L:2 * L]), "hT")

            def turn_a(t, par):
                if real(t + 2):
                    b = t + 2
                    m = UA.await_fill(act, "qk01", b)
                    if later(b):
                        act.wait_ge(s("rest_ready"), b)
                        act.wait_ge(s("parts_written"), b * 48)
                    both = m[0:QC, :].rearrange("p (c l) -> p c l", c=2)
                    nc.scalar.copy(qk32[:, 0:2, :], both)
                    UA.drained(nc.scalar.copy(parts[:, 0, 0:2, :], both), "qk01")
                    m = UA.await_fill(act, "qk2", b)
                    nc.scalar.copy(qk32[:, 2, :], m[0:QC, 0:L])
                    UA.drained(nc.scalar.copy(parts[:, 0, 2, :], m[0:QC, 0:L]), "qk2")
                if real(t - 1):
                    m = UA.await_fill(act, "oc", t - 1)
                    nc.scalar.copy(oTa[:, :], m[:, 0:L])
                    UA.drained(nc.scalar.copy(oTb[:, :], m[0:CB + 1, L:2 * L]), "oc")

                def exps(g):
                    for mt in range(LT):
                        n = 2 * g + mt
                        act.wait_ge(s("scores_filled"), t * 8 + n + 1)
                        if mt == 0 and g >= 2:
                            UA.await_drain(act, f"oT{g - 2}", t)
                        nc.scalar.activation(pex[:, n % 4, :, :], pst[n % 2][:, :, :], ACT.Exp,
                                             scale=ATT_SCALE).then_inc(s("exp_done"), 1)

                def evac_oT(g):
                    m = UA.await_fill(act, f"oT{g}", t)
                    if g == 0 and later(t):
                        UA.await_drain(act, "tt1", t - 1)
                    UA.drained(nc.scalar.copy(oT[:, g, :], m[:, 0:L]), f"oT{g}")

                if real(t):
                    exps(0)
                    exps(1)
                    evac_oT(0)
                    exps(2)
                if real(t + 3):
                    evac_hT(UA, t + 3, (par + 1) % 2)
                if real(t):
                    evac_oT(1)
                    exps(3)
                    evac_oT(2)
                    evac_oT(3)

            run(act, *A_TURNS, turn_a)
            act.wait_ge(s("lnv_ready"), 2)
            nc.scalar.activation(lns[:, :], lnv[:, :], ACT.Sqrt).then_inc(s("lns_ready"), 1)

            def turn_b(t, par):
                if real(t + 1):
                    b = t + 1
                    act.wait_ge(s("fc1_filled"), b + 1)
                    slot = (par + 1) % 2
                    if not isinstance(b, int) or b >= 2:
                        UB.await_drain(act, "fc2", b - 2)
                    nc.scalar.activation(gT[0:96, slot, 0:4, :], pst[slot][0:96, :, :], ACT.Gelu_apprx_tanh)
                    nc.scalar.activation(gT[0:96, slot, 4:6, :], ps[slot][0:96, :].rearrange("p (c l) -> p c l", c=2),
                                         ACT.Gelu_apprx_tanh).then_inc(s("gelu_done"), 1)
                if real(t - 1):
                    m = UB.await_fill(act, "x2T", t - 1)
                    nc.scalar.copy(x2Ta[:, :], m[:, 0:L])
                    UB.drained(nc.scalar.copy(x2Tb[:, :], m[0:CB, L:2 * L]), "x2T")
                    m = UB.await_fill(act, "z", t - 1)
                    UB.drained(nc.scalar.copy(zT[:, :], m[0:R, 0:L]), "z")
                if real(t + 2):
                    evac_hT(UB, t + 2, par)

            run(act, *B_TURNS, turn_b)

        @block.vector
        def _(dve):
            steps = [0]

            def then(ins, name="dve_step"):
                steps[0] += 1
                ins.then_inc(s("dve_step"), 1)
                dve.wait_ge(s("dve_step"), steps[0])

            dve.sem_inc(s("max_done"), 2)
            dve.wait_ge(s("wqkv_loaded"), 48)
            for src, dst in ((wqkv_a, wqk_a), (wqkv_b, wqk_b)):
                for k in range(2):
                    nc.vector.tensor_copy(dst[:, C * k:C * k + C].rearrange("p (d h) -> p d h", h=H),
                                          src[:, C * k:C * k + C].rearrange("p (h d) -> p d h", d=D)).then_inc(s("wqk_ready"), 1)
            dve.wait_ge(s("cexp_ready"), 1)
            then(nc.vector.tensor_scalar(cden[:, :], cexp[:, :], 1.0, None, ALU.add))
            then(nc.vector.reciprocal(crec[:, :], cden[:, :]))
            nc.vector.tensor_tensor(silu[:, 0:C], csb[:, :], crec[:, :], ALU.mult).then_inc(s("silu_ready"), 1)
            for i in range(2):
                dve.wait_ge(s("ada_filled"), i + 1)
                nc.vector.tensor_copy(ada[:, 432 * i:432 * i + 432], ps[i][0:B, 0:432]).then_inc(s("ada_copied"), 1)
            dve.wait_ge(s("ada_copied"), 2)
            for i in (1, 4):
                nc.vector.tensor_scalar(ada[:, C * i:C * i + C], ada[:, C * i:C * i + C], 1.0, None, ALU.add).then_inc(s("ada_ready"), 1)
            for i in range(4):
                dve.wait_ge(s("wrTb_filled"), i + 1)
                nc.vector.tensor_copy(wrT_b[:, :].rearrange("k (p r) -> k r p", r=VR)[:, 4 * i:4 * i + 4, :],
                                      ps[i % 2][0:CB, 0:4 * VP].rearrange("k (r p) -> k r p", p=VP)).then_inc(s("wrTb_ready"), 1)

            def statistics(n):
                for t in range(NT):
                    nc.vector.bn_stats(bst[:, t, :], xin[:, t, :]).then_inc(s("bn_done"), 1)
                dve.wait_ge(s("bn_done"), NT * (2 * n - 1))
                for t in range(NT):
                    nc.vector.bn_aggr(mv[:, t, :], bst[:, t, :]).then_inc(s("bn_done"), 1)
                dve.wait_ge(s("bn_done"), 2 * NT * n)
                nc.vector.tensor_scalar(lnv[:, :], mv[:, :, 1], ATT_EPS, None, ALU.add).then_inc(s("lnv_ready"), 1)
                dve.wait_ge(s("lns_ready"), n)
                then(nc.vector.reciprocal(lnr[:, :], lns[:, :]))
                then(nc.vector.tensor_tensor(lnt[:, :], lnr[:, :], lnr[:, :], ALU.mult))
                then(nc.vector.tensor_tensor(lnu[:, :], lnt[:, :], lnv[:, :], ALU.mult))
                then(nc.vector.tensor_scalar(lnt[:, :], lnu[:, :], -0.5, 1.5, ALU.mult, ALU.add))
                then(nc.vector.tensor_tensor(rstd[:, :], lnt[:, :], lnr[:, :], ALU.mult))

            dve.wait_ge(s("x_loaded"), 32)
            statistics(1)

            dve.wait_ge(s("gm_ready"), 2)
            dve.wait_ge(s("gram_filled"), 1)
            then(nc.vector.tensor_copy(gm[:, 0:R], pst[0][0:R, 0, 0:R]))
            nc.vector.tensor_copy(pT[:, :], pst[1][0:R, 0, 0:C]).then_inc(s("gm_step"), 1)
            dve.wait_ge(s("ew_ready"), 3)
            with dve.Fori(0, R) as j:
                dve.wait_ge(s("gm_step"), j + 1)
                nc.vector.reciprocal(rp[:, :], gm[0:1, 0:1]).then_inc(s("pivot"), 1)
                dve.wait_ge(s("pivot"), j + 1)
                nc.vector.tensor_scalar(ew[0:1, 0:R - 1], gm[0:1, 1:R], rp[0:1, 0:1], -1.0, ALU.mult, ALU.mult).then_inc(s("ew_set"), 1)
                dve.wait_ge(s("elim_filled"), j + 1)
                nc.vector.tensor_copy(gm[:, 0:R], pst[0][0:R, 0, 1:R + 1])
                nc.vector.tensor_copy(gm[:, R + 1:2 * R + 1], pst[0][0:R, 0, R + 1:2 * R + 1]).then_inc(s("gm_step"), 1)
            dve.wait_ge(s("linvT_filled"), 1)
            nc.vector.tensor_copy(linvT[:, :], pst[1][0:R, 0, 0:R]).then_inc(s("linvT_ready"), 1)
            dve.wait_ge(s("qtu_filled"), 1)
            then(nc.vector.tensor_copy(qtu[:, :], pst[0][0:R, 0, 0:C]))
            then(nc.vector.tensor_tensor(qsq[:, :], qtu[:, :], qtu[:, :], ALU.mult))
            nc.vector.tensor_reduce(qn[:, 0:1], qsq[:, :], AX.X, ALU.add).then_inc(s("qn_ready"), 1)
            dve.wait_ge(s("qn_root"), 1)
            then(nc.vector.reciprocal(qn[:, 2:3], qn[:, 1:2]))
            then(nc.vector.tensor_tensor(qn[:, 3:4], qn[:, 2:3], qn[:, 2:3], ALU.mult))
            then(nc.vector.tensor_tensor(qn[:, 4:5], qn[:, 3:4], qn[:, 0:1], ALU.mult))
            then(nc.vector.tensor_scalar(qn[:, 5:6], qn[:, 4:5], -0.5, 1.5, ALU.mult, ALU.add))
            then(nc.vector.tensor_tensor(qn[:, 6:7], qn[:, 5:6], qn[:, 2:3], ALU.mult))
            nc.vector.tensor_scalar(qt[:, :], qtu[:, :], qn[:, 6:7], None, ALU.mult).then_inc(s("qt_ready"), 1)
            dve.wait_ge(s("q_filled"), 1)
            then(nc.vector.tensor_copy(qa[:, :], pst[1][:, 0, 0:R]))
            nc.vector.tensor_copy(qb[:, :], pst[1][0:CB, 0, R:2 * R]).then_inc(s("q_ready"), 1)
            dve.wait_ge(s("sm_zeroed"), 1)
            dve.wait_ge(s("ew2_ready"), 2)
            nc.vector.tensor_copy(sm[:, 0, 0:R], qa[0:R, :]).then_inc(s("sm_step"), 1)
            nc.vector.tensor_copy(sm[:, 1, 0:R], qt[:, 0:R]).then_inc(s("sm_step"), 1)
            with dve.Fori(0, R) as j:
                dve.wait_ge(s("sm_step"), j * 2 + 2)
                nc.vector.tensor_scalar(st1[0:1, 0:1], sm[0:1, 0, 0:1], 0.0, 2.0, ALU.is_ge, ALU.mult).then_inc(s("sign_step"), 1)
                dve.wait_ge(s("sign_step"), j * 3 + 1)
                nc.vector.tensor_scalar(sg[0:1, bass.ds(j, 1)], st1[0:1, 0:1], 1.0, None, ALU.subtract)
                nc.vector.scalar_tensor_tensor(out=st1[0:1, 1:2], in0=sm[0:1, 0, 0:1], scalar=-1.0, in1=st1[0:1, 0:1],
                                               op0=ALU.add, op1=ALU.add).then_inc(s("sign_step"), 1)
                dve.wait_ge(s("sign_step"), j * 3 + 2)
                nc.vector.reciprocal(st1[0:1, 2:3], st1[0:1, 1:2]).then_inc(s("sign_step"), 1)
                dve.wait_ge(s("sign_step"), j * 3 + 3)
                nc.vector.tensor_scalar(ew2[0:1, :, 0:R - 1], sm[0:1, :, 1:R], st1[0:1, 2:3], -1.0, ALU.mult, ALU.mult).then_inc(s("ew2_set"), 1)
                dve.wait_ge(s("sign_filled"), j + 1)
                nc.vector.tensor_copy(sm[:, :, 0:R], pst[0][0:R, 0:2, 1:R + 1]).then_inc(s("sm_step"), 2)
            dve.sem_inc(s("signs_done"), 1)
            dve.wait_ge(s("ss_filled"), 1)
            then(nc.vector.tensor_copy(ss[:, :], pst[1][0:R, 0, 0:R]))

            dve.wait_ge(s("upT_filled"), 1)
            upT = pst[0][0:R, 0:2, :].rearrange("p a (b n) -> p (a b) n", n=R)
            then(nc.vector.tensor_tensor(q0[:, :, :], up[:, :, :], upT, ALU.subtract))
            for i in range(2):
                nc.vector.tensor_scalar(aa[:, :, i, :], q0[:, :, :], (-1.0) ** i * 2.0 ** -SQUARINGS, None, ALU.mult).then_inc(s("aa_ready"), 1)
            dve.wait_ge(s("a2_filled"), 1)
            a2p = pst[1][0:R, 0:2, :].rearrange("p a (b n) -> p (a b) n", n=R)
            dve.wait_ge(s("aa_ready"), 2)
            dve.wait_ge(s("half_ready"), 2)
            then(nc.vector.tensor_copy(a2[:, :, :], a2p))
            then(nc.vector.scalar_tensor_tensor(out=q0[:, :, :], in0=a2[:, :, :], scalar=1.0 / 24, in1=half_i[:, :, :], op0=ALU.mult, op1=ALU.add))
            for i in range(2):
                nc.vector.scalar_tensor_tensor(out=qq[:, :, i, :], in0=aa[:, :, i, :], scalar=1.0 / 6, in1=q0[:, :, :],
                                               op0=ALU.mult, op1=ALU.add).then_inc(s("qq_ready"), 1)

            def ef_psum(i):
                return pst[i][0:R, :, :].rearrange("p a (e n) -> p a e n", n=R)

            hB = B // 2
            dve.wait_ge(s("e0_filled"), 1)
            for i in range(2):
                nc.vector.tensor_tensor(ef[:, hB * i:hB * i + hB, :, :],
                                        pst[i][0:R, 0:2, :].rearrange("p a (b e n) -> p (a b) e n", e=2, n=R),
                                        aa[:, hB * i:hB * i + hB, :, :], ALU.add).then_inc(s("ef_step"), 1)
            with dve.Fori(0, SQUARINGS) as j:
                for i in range(2):
                    dve.wait_ge(s("sq_filled"), j * 2 + i + 1)
                    e = ef[:, hB * i:hB * i + hB, :, :].rearrange("p b e n -> p (b e n)")
                    nc.vector.scalar_tensor_tensor(out=e, in0=e, scalar=2.0, in1=pst[i][0:R, 0:2, :].rearrange("p a n -> p (a n)"),
                                                   op0=ALU.mult, op1=ALU.add).then_inc(s("ef_step"), 1)
            dve.wait_ge(s("ef_step"), 2 * SQUARINGS + 2)
            nc.vector.tensor_tensor(efs[:, :, :], ef[:, :, 1, :], ss[:, :].unsqueeze(1).to_broadcast([R, B, R]), ALU.mult).then_inc(s("efs_ready"), 1)
            for i in range(3):
                n = min(3, B - 3 * i)
                dve.wait_ge(s("fq_filled"), i + 1)
                nc.vector.tensor_copy(fq[:, 3 * i:3 * i + n, :], pst[i % 2][0:R, 0:2, :].rearrange("p a l -> p (a l)")[:, 0:n * C]
                                      .rearrange("p (b n) -> p b n", n=C)).then_inc(s("fq_ready"), 1)


            def normalise(b, n):
                if later(n):
                    dve.wait_ge(s("scaled"), n)
                for t in range(LT):
                    i = b * LT + t
                    ins = nc.vector.tensor_scalar(hb[:, t, :], xin[:, bass.ds(i, 1), :].rearrange("p a c -> p (a c)"),
                                                  mv[:, bass.ds(i, 1), 0], rstd[:, bass.ds(i, 1)],
                                                  ALU.subtract, ALU.mult)
                ins.then_inc(s("normed"), 1)

            def gated(m, b, which):
                return nc.vector.tensor_tensor(res[:, :, :], m[:, 0:LT * C].rearrange("p (t c) -> p t c", t=LT),
                                               gates[:, which, bass.ds(b, 1), :].to_broadcast([128, LT, C]), ALU.mult)

            def turn_a(t, par):
                if real(t - 1):
                    for lt in range(LT):
                        m = UA.await_fill(dve, f"tt{lt}", t - 1)
                        mh = m[:, :].rearrange("p (h e) -> p h e", e=32)
                        nc.vector.reciprocal(rden[:, lt, :], mh[:, :, D]).then_inc(s("rden_ready"), 1)
                        dve.wait_ge(s("rden_ready"), (t - 1) * LT + lt + 1)
                        UA.drained(nc.vector.tensor_tensor(otok[:, lt, 0:C].rearrange("p (h d) -> p h d", d=D), mh[:, :, 0:D],
                                                           rden[:, lt, :].unsqueeze(2).to_broadcast([128, H, D]), ALU.mult), f"tt{lt}")

                def maxima(us):
                    for u in us:
                        k, lt = u // 2, u % 2
                        dve.wait_ge(s("max_filled"), (t + 1) * 16 + u + 1)
                        nc.vector.tensor_reduce(nm[:, lt, 2 * k:2 * k + 2], ps[u % 2][:, :].rearrange("p (h l) -> p h l", h=2),
                                                AX.X, ALU.max, negate=True).then_inc(s("max_done"), 1)

                if real(t + 1):
                    maxima(range(4))
                    m = UA.await_fill(dve, "v", t + 1)
                    if real(t - 1):
                        UA.await_drain(dve, "oT3", t - 1)
                    slot = (par + 1) % 2
                    UA.drained(nc.vector.tensor_copy(ve[:, slot, :, :, 0:D], m[:, 0:LT * C].rearrange("p (t h d) -> p t h d", t=LT, d=D)), "v")
                    maxima(range(4, 6))
                if real(t - 1):
                    m = UA.await_fill(dve, "proj", t - 1)
                    dve.wait_ge(s("x1_ready"), t)
                    UA.drained(gated(m, t - 1, 0), "proj")
                if real(t + 2):
                    dve.wait_ge(s("rest_ready"), t + 3)
                    if later(t + 2):
                        dve.wait_ge(s("parts_written"), (t + 2) * 48)
                    nc.vector.tensor_copy(parts[:, 1, :, :], qkr[:, :, :]).then_inc(s("mid_ready"), 1)
                if real(t + 3):
                    normalise(t + 3, t + 3)
                if real(t + 1):
                    b = t + 1
                    maxima(range(6, 16))
                    dve.wait_ge(s("max_done"), b * 16 + 18)
                    nc.vector.tensor_copy(nmb[:, :, 0, :], nm[:, :, :]).then_inc(s("shift_high"), 1)
                    dve.wait_ge(s("shift_high"), b + 1)
                    nc.vector.tensor_tensor(nmb[:, :, 1, :], nm[:, :, :], nmb[:, :, 0, :], ALU.subtract).then_inc(s("shift_ready"), 1)
                    m = UA.await_fill(dve, "nmT", b)
                    if later(b):
                        dve.wait_ge(s("shift_loaded"), b * 16)
                    UA.drained(nc.vector.tensor_copy(nmT[:, :], m[0:2 * H, 0:L // 2].bitcast(BF16)), "nmT")

            dve.wait_ge(s("gates_loaded"), 32)
            dve.wait_ge(s("ve_zeroed"), 2)
            run(dve, *A_TURNS, turn_a)

            dve.wait_ge(s("x1_ready"), B + 1)
            statistics(2)
            nc.vector.memset(gT[96:97, :, :, :], 1.0).then_inc(s("gT_one"), 1)

            def turn_b(t, par):
                if real(t + 2):
                    normalise(t + 2, t + 2 + B)
                if real(t):
                    m = UB.await_fill(dve, "fc2", t)
                    if later(t):
                        dve.wait_ge(s("x2_ready"), t)
                    UB.drained(gated(m, t, 1), "fc2")
                if real(t - 1):
                    b = t - 1
                    m = UB.await_fill(dve, "w", b)
                    if not isinstance(t, int) or b >= 2:
                        dve.wait_ge(s("out_written"), b * 16)
                    dve.wait_ge(s("x2_ready"), b + 1)
                    slot = (par + 1) % 2
                    nc.vector.tensor_tensor(osb[:, slot, :, :], m[:, 0:LT * C].rearrange("p (t c) -> p t c", t=LT),
                                            x2c[:, slot, :, :], ALU.add).then_inc(s("out_ready"), 1)
                    dve.wait_ge(s("out_ready"), b + 1)
                    dve.sem_inc(s("bank6_drained"), 1)

            run(dve, *B_TURNS, turn_b)

        @block.tensor
        def _(pe):
            mm = nc.tensor.matmul
            tr = nc.tensor.transpose
            pe.wait_ge(s("ident_ready"), 2)
            pe.wait_ge(s("ones_ready"), 2)
            pe.wait_ge(s("silu_ready"), 1)
            tr(ps[0][:, 0:B], silu[:, 0:128], ident[0:B, 0:B])
            tr(ps[0][0:CB + 1, B:2 * B], silu[:, 128:C + 1], ident[0:B, 0:B]).then_inc(s("siluT_filled"), 1)
            pe.wait_ge(s("siluT_ready"), 2)
            pe.wait_ge(s("wada_loaded"), 48)
            for i in range(2):
                mm(ps[i][0:B, 0:432], siluT_a[:, :], wada_a[:, 432 * i:432 * i + 432], start=True, stop=False)
                mm(ps[i][0:B, 0:432], siluT_b[:, :], wada_b[:, 432 * i:432 * i + 432], start=False, stop=True).then_inc(s("ada_filled"), 1)
            pe.wait_ge(s("wr_loaded"), 32)
            pe.wait_ge(s("ada_copied"), 2)
            for i in range(4):
                if i >= 2:
                    pe.wait_ge(s("wrTa_ready"), i - 1)
                    pe.wait_ge(s("wrTb_ready"), i - 1)
                ta = pst[i % 2][:, 0:2, :].rearrange("p a l -> p (a l)")
                for r in range(4):
                    last = tr(ta[:, VP * r:VP * r + VP], wr[:, 4 * i + r, 0:128], ident[0:VP, 0:VP])
                last.then_inc(s("wrTa_filled"), 1)
                for r in range(4):
                    last = tr(ps[i % 2][0:CB, VP * r:VP * r + VP], wr[:, 4 * i + r, 128:C], ident[0:VP, 0:VP])
                last.then_inc(s("wrTb_filled"), 1)
            pe.wait_ge(s("wrTa_ready"), 4)
            pe.wait_ge(s("wrTb_ready"), 4)
            for i in range(4):
                if i >= 2:
                    pe.wait_ge(s("v_ready"), i - 1)
                cols = slice(504 * i, 504 * i + 504)
                o = misc[6 + i % 2][0:B, 0:504]
                mm(o, siluT_a[:, :], wrT_a[:, cols], start=True, stop=False)
                mm(o, siluT_b[0:CB, :], wrT_b[:, cols], start=False, stop=False)
                mm(o, ones_row[0:1, 0:B], br[0:1, cols], start=False, stop=True).then_inc(s("v_filled"), 1)
            pe.wait_ge(s("p_loaded"), 32)
            tr(pst[1][0:R, 0, 0:128], pa[:, :], ident[:, :])
            tr(pst[1][0:R, 0, 128:C], pbm[:, :], ident[0:CB, 0:CB])
            mm(pst[0][0:R, 0, 0:R], pa[:, :], pa[:, :], start=True, stop=False)
            mm(pst[0][0:R, 0, 0:R], pbm[:, :], pbm[:, :], start=False, stop=True).then_inc(s("gram_filled"), 1)
            with pe.Fori(0, R) as j:
                pe.wait_ge(s("ew_set"), j + 1)
                settled(pe, "pe")
                mm(pst[0][0:R, 0, 0:2 * R + 1], ew[:, :], gm[:, :], start=True, stop=True).then_inc(s("elim_filled"), 1)
            pe.wait_ge(s("gm_step"), R + 1)
            tr(pst[1][0:R, 0, 0:R], gm[:, R + 1:2 * R + 1], ident[0:R, 0:R]).then_inc(s("linvT_filled"), 1)
            pe.wait_ge(s("linvT_ready"), 1)
            mm(pst[0][0:R, 0, 0:C], linvT[:, :], pT[:, :], start=True, stop=True).then_inc(s("qtu_filled"), 1)
            pe.wait_ge(s("qt_ready"), 1)
            tr(pst[1][:, 0, 0:R], qt[:, 0:128], ident[0:R, 0:R])
            tr(pst[1][0:CB, 0, R:2 * R], qt[:, 128:C], ident[0:R, 0:R]).then_inc(s("q_filled"), 1)
            with pe.Fori(0, R) as j:
                pe.wait_ge(s("ew2_set"), j + 1)
                settled(pe, "pe")
                mm(pst[0][0:R, 0, 0:R + 1], ew2[:, 1, :], sm[:, 0, :], start=True, stop=True)
                mm(pst[0][0:R, 1, 0:R + 1], ew2[:, 0, :], sm[:, 1, :], start=True, stop=True).then_inc(s("sign_filled"), 1)
            pe.wait_ge(s("signs_done"), 1)
            pe.wait_ge(s("sm_step"), 2 * R + 2)
            mm(pst[1][0:R, 0, 0:R], sg[:, :], sg[:, :], start=True, stop=True).then_inc(s("ss_filled"), 1)
            pe.wait_ge(s("up_loaded"), 16 * (R - 1))
            for b in range(B):
                last = tr(pst[0][0:R, b // 4, R * (b % 4):R * (b % 4) + R], up[:, b, :], ident[0:R, 0:R])
            last.then_inc(s("upT_filled"), 1)
            pe.wait_ge(s("aa_ready"), 2)
            for b in range(B):
                last = mm(pst[1][0:R, b // 4, R * (b % 4):R * (b % 4) + R], aa[:, b, 1, :], aa[:, b, 0, :], start=True, stop=True)
            last.then_inc(s("a2_filled"), 1)
            pe.wait_ge(s("qq_ready"), 2)

            def ef_out(b, e):
                b4 = b % 4
                return pst[b // 4][0:R, b4 // 2, (b4 % 2) * 128 + e * R:(b4 % 2) * 128 + e * R + R]

            for b in range(B):
                for e in range(2):
                    last = mm(ef_out(b, e), a2[:, b, :], qq[:, b, e, :], start=True, stop=True)
            last.then_inc(s("e0_filled"), 1)
            with pe.Fori(0, SQUARINGS) as j:
                for i in range(2):
                    pe.wait_ge(s("ef_step"), j * 2 + i + 1)
                    settled(pe, "pe")
                    for b in range(4 * i, 4 * i + 4):
                        mm(ef_out(b, 0), ef[:, b, 1, :], ef[:, b, 0, :], start=True, stop=True)
                        last = mm(ef_out(b, 1), ef[:, b, 0, :], ef[:, b, 1, :], start=True, stop=True)
                    last.then_inc(s("sq_filled"), 1)
            pe.wait_ge(s("efs_ready"), 1)
            for i in range(3):
                if i == 2:
                    pe.wait_ge(s("fq_ready"), 1)
                for b in range(3 * i, min(3 * i + 3, B)):
                    o = pst[i % 2][0:R, 0:2, :].rearrange("p a l -> p (a l)")
                    last = mm(o[:, C * (b - 3 * i):C * (b - 3 * i) + C], efs[:, b, :], qt[:, :], start=True, stop=True)
                last.then_inc(s("fq_filled"), 1)
            pe.wait_ge(s("fq_ready"), 3)

            def two_chunks(m, src):
                for lt in range(LT):
                    tr(m[:, 128 * lt:128 * lt + 128], src[:, lt, 0:128], ident[:, :])
                    k = src.shape[2] - 128
                    last = tr(m[0:k, L + 128 * lt:L + 128 * lt + 128], src[:, lt, 128:128 + k], ident[:, :])
                return last

            def project(o, a, b, wa, wb):
                mm(o, a, wa, start=True, stop=False)
                return mm(o, b, wb, start=False, stop=True)

            def transpose_h(u, b, n):
                pe.wait_ge(s("h_ready"), n + 1)
                m = u.claim(pe, "hT", b)
                u.filled(two_chunks(m, h), "hT")

            pe.wait_ge(s("h_one"), 2)
            pe.wait_ge(s("wqk_ready"), 4)
            pe.wait_ge(s("stacks_zeroed"), 3)
            pe.wait_ge(s("identb_ready"), 1)
            pe.wait_ge(s("wp_loaded"), 48)

            def turn_a(t, par):
                def use(name, b, make):
                    if real(b):
                        make(b)
                    else:
                        UA.skip(pe, name, b)

                def qk(name, chunks):
                    def make(b):
                        UA.await_drain(pe, "hT", b)
                        m = UA.claim(pe, name, b)
                        for c in chunks:
                            cols = slice(QC * c, QC * c + QC)
                            last = project(m[0:QC, (c % 2) * L:(c % 2) * L + L], wqk_a[:, cols], wqk_b[:, cols],
                                           hTa[:, par, :], hTb[:, par, :])
                        UA.filled(last, name)
                    use(name, t + 2, make)

                def by_token(lt):
                    def make(b):
                        UA.await_drain(pe, "oT3", b)
                        m = UA.claim(pe, f"tt{lt}", b)
                        for g in range(G):
                            last = tr(m[:, 128 * g:128 * g + 128], oT[:, g, 128 * lt:128 * lt + 128], ident[:, :])
                        UA.filled(last, f"tt{lt}")
                    use(f"tt{lt}", t - 1, make)

                def max_scores(us):
                    if not real(t + 1):
                        return
                    slot = (par + 1) % 2
                    if us[0] == 0:
                        pe.wait_ge(s("stacks_loaded"), (t + 1) * 96 + 96)
                    for u in us:
                        k, lt = u // 2, u % 2
                        pe.wait_ge(s("max_done"), (t + 1) * 16 + u + 1)
                        for i in range(2):
                            hd = 2 * k + i
                            last = mm(ps[u % 2][:, L * i:L * i + L], qs[0:KS, slot, hd, 128 * lt:128 * lt + 128],
                                      ks[0:KS, slot, hd, :], start=True, stop=True)
                        last.then_inc(s("max_filled"), 1)

                def values(b):
                    slot = (par + 1) % 2
                    m = UA.claim(pe, "v", b)
                    for lt in range(LT):
                        rows = slice(128 * lt, 128 * lt + 128)
                        last = project(m[:, C * lt:C * lt + C], hTa[:, slot, rows], hTb[:, slot, rows],
                                       wqkv_a[:, 2 * C:3 * C], wqkv_b[:, 2 * C:3 * C])
                    UA.filled(last, "v")

                def channels(b):
                    UA.await_drain(pe, "tt1", b)
                    m = UA.claim(pe, "oc", b)
                    UA.filled(two_chunks(m, otok), "oc")

                def projection(b):
                    UA.await_drain(pe, "oc", b)
                    m = UA.claim(pe, "proj", b)
                    for lt in range(LT):
                        rows = slice(128 * lt, 128 * lt + 128)
                        last = project(m[:, C * lt:C * lt + C], oTa[:, rows], oTb[:, rows], wp_a[:, :], wp_b[:, :])
                    UA.filled(last, "proj")

                def scores(g):
                    if not real(t):
                        return
                    if g == 0:
                        pe.wait_ge(s("shift_loaded"), t * 16 + 16)
                    for mt in range(LT):
                        n = 2 * g + mt
                        pe.wait_ge(s("exp_done"), t * 8 + n + 1)
                        for j in range(4):
                            last = mm(pst[n % 2][:, j, :], ks[0:KS + 2, par, 4 * g + j, 128 * mt:128 * mt + 128],
                                      qs[0:KS + 2, par, 4 * g + j, :], start=True, stop=True)
                        last.then_inc(s("scores_filled"), 1)

                def weighted(g):
                    def make(b):
                        m = UA.claim(pe, f"oT{g}", b)
                        for mt in range(LT):
                            pe.wait_ge(s("exp_done"), b * 8 + 2 * g + mt + 3)
                            for j in range(4):
                                last = mm(m[32 * j:32 * j + 32, 0:L], ve[:, par, mt, 4 * g + j, :], pex[:, (2 * g + mt) % 4, j, :],
                                          start=(mt == 0), stop=(mt == LT - 1))
                        UA.filled(last, f"oT{g}")
                    use(f"oT{g}", t, make)

                def shift(b):
                    pe.wait_ge(s("shift_ready"), b + 1)
                    m = UA.claim(pe, "nmT", b)
                    for lt in range(LT):
                        last = tr(m[0:2 * H, 64 * lt:64 * lt + 64].bitcast(BF16), nmb[:, lt, :, :].rearrange("p a h -> p (a h)"), identb[:, :])
                    UA.filled(last, "nmT")

                def next_hT(b):
                    transpose_h(UA, b, b)

                qk("qk01", (0, 1))
                by_token(0)
                by_token(1)
                qk("qk2", (2,))
                max_scores(range(0, 4))
                use("v", t + 1, values)
                use("oc", t - 1, channels)
                max_scores(range(4, 6))
                use("proj", t - 1, projection)
                scores(0)
                max_scores(range(6, 8))
                scores(1)
                max_scores(range(8, 10))
                weighted(0)
                max_scores(range(10, 12))
                scores(2)
                use("hT", t + 3, next_hT)
                max_scores(range(12, 14))
                weighted(1)
                max_scores(range(14, 16))
                scores(3)
                weighted(2)
                use("nmT", t + 1, shift)
                weighted(3)

            run(pe, *A_TURNS, turn_a)

            pe.wait_ge(s("mlp_loaded"), 80)
            pe.wait_ge(s("gT_one"), 1)
            pe.wait_ge(s("exp_done"), 8 * B + 2)

            def turn_b(t, par):
                def use(name, b, make):
                    if real(b):
                        make(b)
                    else:
                        UB.skip(pe, name, b)

                def up_projection():
                    b, slot = t + 1, (par + 1) % 2
                    if not real(b):
                        return
                    UB.await_drain(pe, "hT", b)
                    if not isinstance(b, int) or b >= 2:
                        pe.wait_ge(s("gelu_done"), b - 1)
                    for c in range(FC):
                        o = pst[slot][0:96, c, :] if c < 4 else ps[slot][0:96, L * (c - 4):L * (c - 4) + L]
                        cols = slice(96 * c, 96 * c + 96)
                        last = project(o, wfc1_a[:, cols], wfc1_b[:, cols], hTa[:, slot, :], hTb[:, slot, :])
                    last.then_inc(s("fc1_filled"), 1)

                def x2_channels(b):
                    pe.wait_ge(s("x2_ready"), b + 1)
                    m = UB.claim(pe, "x2T", b)
                    UB.filled(two_chunks(m, x2c[:, (par + 1) % 2, :, :]), "x2T")

                def down_projection(b):
                    pe.wait_ge(s("gelu_done"), b + 1)
                    m = UB.claim(pe, "fc2", b)
                    for lt in range(LT):
                        for c in range(FC):
                            k = 97 if c == FC - 1 else 96
                            last = mm(m[:, C * lt:C * lt + C], gT[0:k, par, c, 128 * lt:128 * lt + 128], wfc2[0:k, c, :],
                                      start=(c == 0), stop=(c == FC - 1))
                    UB.filled(last, "fc2")

                def coordinates(b):
                    UB.await_drain(pe, "x2T", b)
                    m = UB.claim(pe, "z", b)
                    UB.filled(project(m[0:R, 0:L], qa[:, :], qb[:, :], x2Ta[:, :], x2Tb[:, :]), "z")

                def rotation(b):
                    UB.await_drain(pe, "z", b)
                    m = UB.claim(pe, "w", b)
                    for lt in range(LT):
                        last = mm(m[:, C * lt:C * lt + C], zT[:, 128 * lt:128 * lt + 128],
                                  fq[:, bass.ds(b, 1), :].rearrange("p a n -> p (a n)"), start=True, stop=True)
                    UB.filled(last, "w")

                up_projection()
                use("x2T", t - 1, x2_channels)
                use("fc2", t, down_projection)
                use("z", t - 1, coordinates)
                use("hT", t + 2, lambda b: transpose_h(UB, b, b + B))
                use("w", t - 1, rotation)

            run(pe, *B_TURNS, turn_b)


_INS = ['x', 'cond_1152', 'L0_cond_W_qkv', 'L0_cond_b_qkv', 'L0_cond_W_proj', 'L0_cond_b_proj', 'L0_cond_W_fc1',
        'L0_cond_b_fc1', 'L0_cond_W_fc2', 'L0_cond_b_fc2', 'L0_cond_W_ada', 'L0_cond_b_ada', 'L1_cond_P',
        'L1_cond_W', 'L1_cond_b']
_OUTS = [((8, 256, 144), 'float32')]


def kernel(**inputs):
    import numpy as _np
    import concourse.bacc as _bacc
    from concourse import mybir as _mybir
    from concourse.bass_utils import run_bass_kernel_spmd as _run

    nc = _bacc.Bacc("TRN2", target_bir_lowering=False, num_devices=1)
    arrays, args = {}, []
    for name in _INS:
        a = _np.ascontiguousarray(inputs[name])
        arrays[f"in_{name}_dram"] = a
        args.append(nc.dram_tensor(f"in_{name}_dram", a.shape, _mybir.dt.from_np(a.dtype), kind="ExternalInput").ap())
    for i, (shape, dtype) in enumerate(_OUTS):
        dt = _mybir.dt.from_np(_np.dtype(dtype))
        args.append(nc.dram_tensor(f"out_{i}_dram", shape, dt, kind="ExternalOutput").ap())
    cond_seq_program(nc, *args)
    r = _run(nc, [arrays], core_ids=[0])
    return r.results[0]["out_0_dram"]
```

```python
from contextlib import ExitStack

import concourse.bass as bass
from concourse import mybir

F32 = mybir.dt.float32
BF16 = mybir.dt.bfloat16
ACT = mybir.ActivationFunctionType
ALU = mybir.AluOpType
AX = mybir.AxisListType


def cond_seq_program(nc, x, cond, w_qkv, b_qkv, w_proj, b_proj, w_fc1, b_fc1, w_fc2, b_fc2,
                     w_ada, b_ada, p_mat, w_rot, b_rot, out):
    B, L, C = x.shape
    H = 16
    D = C // H
    FF = w_fc1.shape[1]
    R = p_mat.shape[1]
    NV = w_rot.shape[0]
    LT = L // 128
    NT = B * LT
    CB = C - 128
    QC = 96
    NQ = 2 * C // QC
    FC = FF // 96
    G = H // 4
    SR = 6 * CB + 3
    KS = 96
    ATT_SCALE = float(D) ** -0.5
    ATT_EPS = 1e-6
    SQUARINGS = 14
    VR = 16
    VP = NV // VR

    Q_RUNS = [(0, 1, 3), (1, 1, 2), (2, 1, 1)]
    K_RUNS = [(0, 3, 1), (0, 2, 1), (0, 1, 1)]

    ctx = ExitStack()
    with ctx:
        def sb(name, shape, dt=F32):
            return ctx.enter_context(nc.sbuf_tensor(name, shape, dt))

        def pb(name, shape, dt=F32):
            return ctx.enter_context(nc.psum_tensor(name, shape, dt))

        def sem(name):
            return ctx.enter_context(nc.semaphore(name))

        scr_ada = nc.dram_tensor("scr_ada", [B, 6 * C], F32, kind="Internal").ap()
        scr_qk = nc.dram_tensor("scr_qk", [3, 2 * C, L], BF16, kind="Internal").ap()

        ident = sb("ident", [128, 128])
        identb = sb("identb", [128, 128], BF16)
        half_i = sb("half_i", [R, B, R])
        ones_row = sb("ones_row", [1, 128])
        wqkv_a = sb("wqkv_a", [128, 3 * C])
        wqkv_b = sb("wqkv_b", [CB + 1, 3 * C])
        wqk_a = sb("wqk_a", [128, 2 * C])
        wqkv_r = sb("wqkv_r", [SR, 3 * C], BF16)
        wfc1_r = sb("wfc1_r", [SR, FF], BF16)
        wqk_r = sb("wqk_r", [SR, 2 * C], BF16)
        wpart = sb("wpart", [CB + 1, 3, 3 * C + FF], BF16)
        wp_a = sb("wp_a", [128, C])
        wp_b = sb("wp_b", [CB + 1, C])
        wfc1_a = sb("wfc1_a", [128, FF])
        wfc1_b = sb("wfc1_b", [CB + 1, FF])
        wfc2 = sb("wfc2", [97, FC, C])
        wada_a = sb("wada_a", [128, 6 * C])
        wada_b = sb("wada_b", [CB + 1, 6 * C])
        pa = sb("pa", [128, R])
        pbm = sb("pbm", [CB, R])
        wr = sb("wr", [VP, VR, C])
        br = sb("br", [1, NV])
        wrT_a = sb("wrT_a", [128, NV])
        late = sb("late", [128, NV])
        wrT_b = late[0:CB, :]
        csb = sb("csb", [B, C])
        cexp = sb("cexp", [B, C])
        cden = sb("cden", [B, C])
        crec = sb("crec", [B, C])
        silu = sb("silu", [B, C + 1])
        siluT_a = sb("siluT_a", [128, B])
        siluT_b = sb("siluT_b", [CB + 1, B])
        ada = sb("ada", [B, 6 * C])
        gates = sb("gates", [128, 2, B, C])
        ms = sb("ms", [128, 2, 2 * C])
        vsb = wr[0:B, :, :].rearrange("b r k -> b (r k)")[:, 0:NV]
        up = sb("up", [R, B, R])
        aa = sb("aa", [R, B, 2, R])
        a2 = sb("a2", [R, B, R])
        q0 = sb("q0", [R, B, R])
        qq = sb("qq", [R, B, 2, R])
        wrest = qq[0:CB + 1, :, :, :].rearrange("p b t r -> p (b t r)")[:, 0:3 * C + FF]
        ef = sb("ef", [R, B, 2, R])
        efs = sb("efs", [R, B, R])
        fq = sb("fq", [R, B, C])
        gm = sb("gm", [R, 2 * R + 1])
        ew = sb("ew", [R, R])
        rp = sb("rp", [1, 1])
        linv = sb("linv", [R, R])
        linvT = sb("linvT", [R, R])
        pT = sb("pT", [R, C])
        qtu = sb("qtu", [R, C])
        qsq = sb("qsq", [R, C])
        qn = sb("qn", [R, 8])
        qt = sb("qt", [R, C])
        qa = sb("qa", [128, R])
        qb = sb("qb", [CB, R])
        q1 = sb("q1", [R, R])
        q1m = sb("q1m", [R, R])
        q1r = sb("q1r", [R, R])
        q1u = sb("q1u", [R, R])
        pm = sb("pm", [R, R])
        sgn = sb("sgn", [R, 8])
        srow = sb("srow", [R, R])
        sdia = sb("sdia", [R, R])
        scol = sb("scol", [R, 1])
        ss = sb("ss", [R, R])
        xin = sb("xin", [128, NT, C])
        bst = sb("bst", [128, NT, 6])
        mv = sb("mv", [128, NT, 2])
        lnv = sb("lnv", [128, NT])
        lns = sb("lns", [128, NT])
        lnr = sb("lnr", [128, NT])
        lnt = sb("lnt", [128, NT])
        lnu = sb("lnu", [128, NT])
        rstd = sb("rstd", [128, NT])
        hb = sb("hb", [128, LT, C])
        hs = sb("hs", [128, LT, C])
        h = sb("h", [128, LT, C])
        hr = sb("hr", [128, LT, SR], BF16)
        hrest = sb("hrest", [128, LT, 2, CB])
        hTa = sb("hTa", [128, 2, L])
        hTr = sb("hTr", [SR, 2, L], BF16)
        qk32 = sb("qk32", [QC, NQ, L])
        qkr = sb("qkr", [QC, NQ, L])
        parts = sb("parts", [QC, 3, NQ, L], BF16)
        qs = sb("qs", [128, 2, H, L], BF16)
        ks = sb("ks", [128, 2, H, L], BF16)
        ve = sb("ve", [128, 2, LT, H, 32])
        nm = sb("nm", [128, LT, H])
        nmb = sb("nmb", [128, LT, 2, H], BF16)
        nmT = sb("nmT", [2 * H, L], BF16)
        pex = sb("pex", [128, 4, 4, L])
        oT = sb("oT", [128, G, L])
        rden = sb("rden", [128, LT, H])
        otok = sb("otok", [128, LT, C + 1])
        oTa = sb("oTa", [128, L])
        oTb = sb("oTb", [CB + 1, L])
        res = sb("res", [128, LT, C])
        gT = pex[0:97, :, :, :].rearrange("p a b l -> p (a b) l")[:, 0:12, :].rearrange("p (s c) l -> p s c l", s=2)
        x2Ta = late[:, 0:L]
        x2Tb = late[0:CB, L:2 * L]
        zT = late[0:R, 2 * L:3 * L]
        x2c, osb = (late[:, at:at + 2 * LT * C].rearrange("p (s t c) -> p s t c", s=2, t=LT)
                    for at in (3 * L, 3 * L + 2 * LT * C))

        ps = [pb(f"ps{i}", [128, 512]) for i in range(2)]
        pst = [pb(f"pst{i}", [128, 4, L]) for i in range(2)]
        m6 = pb("m6", [128, 512])
        m7 = pb("m7", [128, 512])
        misc = {6: m6, 7: m7}

        S = {}

        def s(name):
            if name not in S:
                S[name] = sem(name)
            return S[name]

        A_STAGES = {"P": -1, "X": 0, "M": 1, "F": 2, "N": 3}
        A_USES = {6: [("qk01", "F"), ("tt0", "P"), ("qk2", "F"), ("oc", "P"), ("hT", "N"), ("nmT", "M")],
                  7: [("tt1", "P"), ("v", "M"), ("proj", "P"), ("oT0", "X"), ("oT1", "X"), ("oT2", "X"), ("oT3", "X")]}
        A_FIRST, A_LAST = -3, B
        B_STAGES = {"R": -1, "D": 0, "U": 1, "N": 2}
        B_USES = {6: [("x2T", "R"), ("hT", "N"), ("w", "R")], 7: [("fc2", "D"), ("z", "R")]}
        B_FIRST, B_LAST = -2, B

        class Shared:

            def __init__(self, stages, uses, first, base):
                self.where = {n: (bank, i, stages[st]) for bank, names in uses.items() for i, (n, st) in enumerate(names)}
                self.n = {bank: len(names) for bank, names in uses.items()}
                self.first, self.base = first, base

            def at(self, name, b):
                bank, i, offset = self.where[name]
                return bank, (b - offset - self.first) * self.n[bank] + self.base[bank] + i

            def claim(self, pe, name, b):
                bank, k = self.at(name, b)
                if not (isinstance(k, int) and k == 0):
                    pe.wait_ge(s(f"bank{bank}_drained"), k)
                return misc[bank]

            def filled(self, ins, name):
                ins.then_inc(s(f"bank{self.where[name][0]}_filled"), 1)

            def skip(self, pe, name, b):
                self.claim(pe, name, b)
                pe.sem_inc(s(f"bank{self.where[name][0]}_filled"), 1)
                pe.sem_inc(s(f"bank{self.where[name][0]}_drained"), 1)

            def await_fill(self, eng, name, b):
                bank, k = self.at(name, b)
                eng.wait_ge(s(f"bank{bank}_filled"), k + 1)
                return misc[bank]

            def drained(self, ins, name):
                ins.then_inc(s(f"bank{self.where[name][0]}_drained"), 1)

            def await_drain(self, eng, name, b):
                bank, k = self.at(name, b)
                eng.wait_ge(s(f"bank{bank}_drained"), k + 1)

        def settled(eng, name):
            eng.sem_inc(s(f"{name}_passed"), 1)

        UA = Shared(A_STAGES, A_USES, A_FIRST, {6: 0, 7: 0})
        UB = Shared(B_STAGES, B_USES, B_FIRST, {bank: (A_LAST - A_FIRST + 1) * len(names) for bank, names in A_USES.items()})

        def real(b):
            return not isinstance(b, int) or 0 <= b < B

        def later(b):
            return not isinstance(b, int) or b > 0

        def run(eng, first, last, lo, hi, turn):
            for t in range(first, lo):
                turn(t, t % 2)
            with eng.Fori(0, (hi - lo) // 2) as i:
                for u in range(2):
                    turn(i * 2 + (lo + u), (lo + u) % 2)
            for t in range(hi, last + 1):
                turn(t, t % 2)

        A_TURNS = (A_FIRST, A_LAST, 1, 5)
        B_TURNS = (B_FIRST, B_LAST, 1, 5)

        block = ctx.enter_context(nc.Block())

        @block.sync
        def _(sp):
            sp.sem_inc(s("out_written"), 16)
            sp.dma_start(csb[:, :], cond).then_inc(s("cond_loaded"), 16)
            sp.dma_start(pa[:, :], p_mat[0:128, :]).then_inc(s("p_loaded"), 16)
            sp.dma_start(pbm[:, :], p_mat[128:C, :]).then_inc(s("p_loaded"), 16)
            sp.dma_start(wada_a[:, :], w_ada[0:128, :]).then_inc(s("wada_loaded"), 16)
            sp.dma_start(wada_b[0:CB, :], w_ada[128:C, :]).then_inc(s("wada_loaded"), 16)
            sp.dma_start(wada_b[CB:CB + 1, :], b_ada.rearrange("(a n) -> a n", a=1)).then_inc(s("wada_loaded"), 16)
            sp.dma_start(wr[:, :, :], w_rot.rearrange("(p r) k -> p r k", r=VR)).then_inc(s("wr_loaded"), 16)
            sp.dma_start(br[:, :], b_rot.rearrange("(a n) -> a n", a=1)).then_inc(s("wr_loaded"), 16)
            xv = x.rearrange("b (t p) c -> p (b t) c", p=128)
            for q in range(2):
                sp.dma_start(xin[:, 8 * q:8 * q + 8, :], xv[:, 8 * q:8 * q + 8, :]).then_inc(s("x_loaded"), 16)
            sp.dma_start(wqkv_a[:, :], w_qkv[0:128, :]).then_inc(s("wqkv_loaded"), 16)
            sp.dma_start(wqkv_b[0:CB, :], w_qkv[128:C, :]).then_inc(s("wqkv_loaded"), 16)
            sp.dma_start(wqkv_b[CB:CB + 1, :], b_qkv.rearrange("(a n) -> a n", a=1)).then_inc(s("wqkv_loaded"), 16)
            sp.dma_start(wp_a[:, :], w_proj[0:128, :]).then_inc(s("wp_loaded"), 16)
            sp.dma_start(wp_b[0:CB, :], w_proj[128:C, :]).then_inc(s("wp_loaded"), 16)
            sp.dma_start(wp_b[CB:CB + 1, :], b_proj.rearrange("(a n) -> a n", a=1)).then_inc(s("wp_loaded"), 16)
            sp.dma_start(wfc1_a[:, :], w_fc1[0:128, :]).then_inc(s("mlp_loaded"), 16)
            sp.dma_start(wfc1_b[0:CB, :], w_fc1[128:C, :]).then_inc(s("mlp_loaded"), 16)
            sp.dma_start(wfc1_b[CB:CB + 1, :], b_fc1.rearrange("(a n) -> a n", a=1)).then_inc(s("mlp_loaded"), 16)
            sp.dma_start(wfc2[0:96, :, :], w_fc2.rearrange("(c p) n -> p c n", p=96)).then_inc(s("mlp_loaded"), 16)
            sp.dma_start(wfc2[96:97, FC - 1, :], b_fc2.rearrange("(a n) -> a n", a=1)).then_inc(s("mlp_loaded"), 16)
            sp.wait_ge(s("wpart_ready"), 3)
            for dst, at, n in ((wqkv_r, 0, 3 * C), (wfc1_r, 3 * C, FF)):
                for i, part in enumerate((0, 1, 2, 0, 1, 0)):
                    sp.dma_start(dst[CB * i:CB * i + CB, :], wpart[0:CB, part, at:at + n]).then_inc(s("wstack_loaded"), 16)
                sp.dma_start(dst[6 * CB:SR, :], wpart[CB:CB + 1, :, at:at + n]).then_inc(s("wstack_loaded"), 16)
            sp.wait_ge(s("ada_ready"), 2)
            sp.dma_start(scr_ada, ada[:, :]).then_inc(s("ada_written"), 16)
            sp.wait_ge(s("ada_written"), 16)
            for i, at in enumerate((2, 5)):
                sp.dma_start(gates[:, i, :, :], scr_ada[:, at * C:at * C + C].partition_broadcast(128)).then_inc(s("gates_loaded"), 16)
            sp.wait_ge(s("v_ready"), 4)
            sp.wait_ge(s("up_zeroed"), 1)
            at = 0
            for i in range(R - 1):
                n = R - 1 - i
                sp.dma_start(up[i:i + 1, :, i + 1:R], vsb[:, at:at + n], allow_slow_non_contiguous=(n == 1)).then_inc(s("up_loaded"), 16)
                at += n

            def modulation(b, slot, at, n):
                if later(n):
                    sp.wait_ge(s("ms_loaded"), n * 16)
                    settled(sp, "sp")
                if not isinstance(n, int) or n >= 2:
                    sp.wait_ge(s("h_step"), n * 5 - 5)
                settled(sp, "sp")
                sp.dma_start(ms[:, slot, :], scr_ada[bass.ds(b, 1), at:at + 2 * C].rearrange("a n -> (a n)").partition_broadcast(128)
                             ).then_inc(s("ms_loaded"), 16)

            def turn_a(t, par):
                if real(t + 3):
                    modulation(t + 3, (par + 1) % 2, 0, t + 3)
                if real(t + 2):
                    b = t + 2
                    UA.await_drain(sp, "qk2", b)
                    settled(sp, "sp")
                    if later(b):
                        sp.wait_ge(s("stacks_loaded"), b * 96)
                        settled(sp, "sp")
                    sp.dma_start(scr_qk[0].rearrange("(c p) n -> p c n", p=QC), parts[:, 0, :, :]).then_inc(s("parts_written"), 16)
                    for i, name in enumerate(("mid_ready", "low_ready")):
                        sp.wait_ge(s(name), b + 1)
                        settled(sp, "sp")
                        sp.dma_start(scr_qk[i + 1].rearrange("(c p) n -> p c n", p=QC), parts[:, i + 1, :, :]).then_inc(s("parts_written"), 16)
                    sp.wait_ge(s("parts_written"), b * 48 + 48)
                    settled(sp, "sp")
                    if real(t):
                        sp.wait_ge(s("exp_done"), t * 8 + 10)
                        settled(sp, "sp")
                    qkv = scr_qk.rearrange("t (k d h) n -> t k d (h n)", k=2, d=D)
                    for stack, which, runs in ((qs, 0, Q_RUNS), (ks, 1, K_RUNS)):
                        row = 0
                        for part, n, repeat in runs:
                            src = qkv[part:part + n, which]
                            if repeat > 1:
                                src = src.to_broadcast([repeat, D, H * L])
                            rows = D * n * repeat
                            sp.dma_start(stack[row:row + rows, par, :, :].rearrange("p h l -> p (h l)"), src).then_inc(s("stacks_loaded"), 16)
                            row += rows
                if real(t + 1):
                    b = t + 1
                    UA.await_drain(sp, "nmT", b)
                    settled(sp, "sp")
                    sp.dma_start(qs[KS:KS + 2, (par + 1) % 2, :, :].rearrange("t h l -> t (h l)"), nmT[:, :]).then_inc(s("shift_loaded"), 16)

            def turn_b(t, par):
                if real(t + 2):
                    modulation(t + 2, par, 3 * C, t + 2 + B)
                if real(t - 1):
                    sp.wait_ge(s("out_ready"), t)
                    settled(sp, "sp")
                    if not isinstance(t, int) or t >= 2:
                        sp.wait_ge(s("out_written"), t * 16)
                    sp.dma_start(out[bass.ds(t - 1, 1)].rearrange("a (t p) c -> p (a t) c", p=128), osb[:, (par + 1) % 2, :, :]).then_inc(s("out_written"), 16)

            run(sp, *A_TURNS, turn_a)
            run(sp, *B_TURNS, turn_b)
            sp.wait_ge(s("out_written"), 16 * B + 16)

        @block.gpsimd
        def _(pool):
            def zero_then_select(t, view, pattern, base, fill, name):
                nc.gpsimd.memset(t, 0.0).then_inc(s(name), 1)
                pool.wait_ge(s(name), 1)
                nc.gpsimd.affine_select(out=view, in_=view, compare_op=ALU.not_equal, fill=fill, base=base,
                                        pattern=pattern, channel_multiplier=1).then_inc(s(name), 1)

            zero_then_select(ident[:, :], ident[:, :], [[-1, 128]], 0, 1.0, "ident_ready")
            nc.gpsimd.memset(silu[:, C:C + 1], 1.0).then_inc(s("ones_ready"), 1)
            nc.gpsimd.memset(ones_row[:, :], 1.0).then_inc(s("ones_ready"), 1)
            nc.gpsimd.memset(up[:, :, :], 0.0).then_inc(s("up_zeroed"), 1)
            zero_then_select(gm[:, :], gm[:, R + 1:2 * R + 1], [[-1, R]], 0, 1.0, "gm_ready")
            zero_then_select(ew[:, :], ew[:, :], [[-1, R]], -1, 1.0, "ew_ready")
            pool.wait_ge(s("ew_ready"), 2)
            nc.gpsimd.memset(ew[0:1, R - 1:R], 1.0).then_inc(s("ew_ready"), 1)
            nc.gpsimd.memset(sgn[:, :], -1.0).then_inc(s("exponent_set"), 1)
            zero_then_select(half_i[:, :, :], half_i[:, :, :], [[0, B], [-1, R]], 0, 0.5, "half_ready")
            nc.gpsimd.memset(hr[:, :, 6 * CB:SR], 1.0).then_inc(s("h_one"), 1)
            nc.gpsimd.memset(otok[:, :, C:C + 1], 1.0).then_inc(s("h_one"), 1)
            nc.gpsimd.memset(qs[:, :, :, :], 0.0).then_inc(s("stacks_zeroed"), 1)
            nc.gpsimd.memset(ks[0:KS, :, :, :], 0.0).then_inc(s("stacks_zeroed"), 1)
            pool.wait_ge(s("stacks_zeroed"), 2)
            nc.gpsimd.memset(ks[KS:128, :, :, :], 1.0).then_inc(s("stacks_zeroed"), 1)
            pool.wait_ge(s("stacks_zeroed"), 3)
            nc.gpsimd.memset(ve[:, :, :, :, :], 0.0).then_inc(s("ve_zeroed"), 1)
            pool.wait_ge(s("ve_zeroed"), 1)
            nc.gpsimd.memset(ve[:, :, :, :, D:D + 1], 1.0).then_inc(s("ve_zeroed"), 1)
            pool.wait_ge(s("ident_ready"), 2)
            nc.gpsimd.tensor_copy(identb[:, :], ident[:, :]).then_inc(s("identb_ready"), 1)

            pool.wait_ge(s("exponent_set"), 1)
            pool.wait_ge(s("q_ready"), 2)
            with pool.Fori(0, R) as j:
                def step(ins, k):
                    ins.then_inc(s("sign_step"), 1)
                    pool.wait_ge(s("sign_step"), j * 11 + k)
                    if k in (1, 3):
                        settled(pool, "sign_step")

                col = bass.ds(j, 1)
                step(nc.gpsimd.tensor_tensor(q1m[:, :], q1[:, :], ident[0:R, col].to_broadcast([R, R]), ALU.mult), 1)
                step(nc.gpsimd.partition_all_reduce(q1r[:, :], q1m[:, :], R, bass.bass_isa.ReduceOp.add), 2)
                step(nc.gpsimd.tensor_copy(sgn[:, 1:2], q1r[:, col]), 3)
                step(nc.gpsimd.tensor_scalar(sgn[:, 2:3], sgn[:, 1:2], 0.0, 0.5, ALU.is_ge, ALU.subtract), 4)
                nc.gpsimd.tensor_tensor(pm[:, col], q1r[:, col], sgn[:, 2:3], ALU.add).then_inc(s("pivot_kept"), 1)
                step(nc.gpsimd.tensor_tensor(sgn[:, 3:4], sgn[:, 1:2], sgn[:, 2:3], ALU.add), 5)
                step(nc.gpsimd.tensor_tensor(sgn[:, 4:5], sgn[:, 3:4], sgn[:, 3:4], ALU.mult), 6)
                step(nc.gpsimd.tensor_tensor(sgn[:, 5:6], sgn[:, 4:5], sgn[:, 0:1], ALU.pow), 7)
                step(nc.gpsimd.tensor_tensor(sgn[:, 6:7], sgn[:, 5:6], sgn[:, 3:4], ALU.mult), 8)
                step(nc.gpsimd.tensor_tensor(sgn[:, 7:8], q1[:, col], sgn[:, 6:7], ALU.mult), 9)
                step(nc.gpsimd.tensor_tensor(q1u[:, :], q1r[:, :], sgn[:, 7:8].to_broadcast([R, R]), ALU.mult), 10)
                step(nc.gpsimd.tensor_tensor(q1[:, :], q1[:, :], q1u[:, :], ALU.subtract), 11)

            def wide(v):
                return v.unsqueeze(1).to_broadcast([128, LT, C])

            def turn_b(t, par):
                if real(t):
                    UB.await_drain(pool, "fc2", t)
                    if not isinstance(t, int) or t >= 2:
                        pool.wait_ge(s("out_ready"), t - 1)
                    nc.gpsimd.tensor_tensor(x2c[:, par, :, :], xin[:, bass.ds(t * LT, LT), :], res[:, :, :], ALU.add).then_inc(s("x2_ready"), 1)
            run(pool, *B_TURNS, turn_b)

        @block.scalar
        def _(act):
            act.sem_inc(s("exp_done"), 2)
            act.wait_ge(s("cond_loaded"), 16)
            nc.scalar.activation(cexp[:, :], csb[:, :], ACT.Exp, scale=-1.0).then_inc(s("cexp_ready"), 1)
            act.wait_ge(s("siluT_filled"), 1)
            nc.scalar.copy(siluT_a[:, :], ps[0][:, 0:B]).then_inc(s("siluT_ready"), 1)
            nc.scalar.copy(siluT_b[:, :], ps[0][0:CB + 1, B:2 * B]).then_inc(s("siluT_ready"), 1)
            for i in range(4):
                act.wait_ge(s("wrTa_filled"), i + 1)
                nc.scalar.copy(wrT_a[:, :].rearrange("k (p r) -> k r p", r=VR)[:, 4 * i:4 * i + 4, :],
                               pst[i % 2][:, 0:2, :].rearrange("p a l -> p (a l)")[:, 0:4 * VP]
                               .rearrange("k (r p) -> k r p", p=VP)).then_inc(s("wrTa_ready"), 1)
            for i in range(4):
                act.wait_ge(s("v_filled"), i + 1)
                nc.scalar.copy(vsb[:, 504 * i:504 * i + 504], misc[6 + i % 2][0:B, 0:504]).then_inc(s("v_ready"), 1)
            act.wait_ge(s("lnv_ready"), 1)
            nc.scalar.activation(lns[:, :], lnv[:, :], ACT.Sqrt).then_inc(s("lns_ready"), 1)


            act.wait_ge(s("gm_ready"), 2)
            act.sem_inc(s("inv_step"), 1)
            with act.Fori(0, R // 8) as i:
                for u in range(8):
                    act.wait_ge(s("elim_filled"), i * 16 + 2 * u + 2)
                    nc.scalar.copy(gm[:, R + 1:2 * R + 1], pst[1][0:R, 0, 0:R]).then_inc(s("inv_step"), 1)
            act.wait_ge(s("qn_ready"), 1)
            nc.scalar.activation(qn[:, 1:2], qn[:, 0:1], ACT.Sqrt).then_inc(s("qn_root"), 1)

            def evac_hT(u, b, slot):
                m = u.await_fill(act, "hT", b)
                if u is UA and (not isinstance(b, int) or b >= 2):
                    UA.await_drain(act, "v", b - 2)
                if u is UB and (not isinstance(b, int) or b >= 2):
                    act.wait_ge(s("fc1_filled"), b - 1)
                nc.scalar.copy(hTa[:, slot, :], m[:, 0:L])
                u.drained(nc.scalar.copy(hTr[:, slot, :], m[0:SR, L:L + L // 2].bitcast(BF16)), "hT")

            def turn_a(t, par):
                if real(t + 2):
                    b = t + 2
                    m = UA.await_fill(act, "qk01", b)
                    if later(b):
                        act.wait_ge(s("rest_ready"), b)
                        act.wait_ge(s("parts_written"), b * 48)
                    both = m[0:QC, :].rearrange("p (c l) -> p c l", c=2)
                    nc.scalar.copy(qk32[:, 0:2, :], both)
                    UA.drained(nc.scalar.copy(parts[:, 0, 0:2, :], both), "qk01")
                    m = UA.await_fill(act, "qk2", b)
                    nc.scalar.copy(qk32[:, 2, :], m[0:QC, 0:L])
                    UA.drained(nc.scalar.copy(parts[:, 0, 2, :], m[0:QC, 0:L]), "qk2")
                if real(t - 1):
                    m = UA.await_fill(act, "oc", t - 1)
                    nc.scalar.copy(oTa[:, :], m[:, 0:L])
                    UA.drained(nc.scalar.copy(oTb[:, :], m[0:CB + 1, L:2 * L]), "oc")

                def exps(g):
                    for mt in range(LT):
                        n = 2 * g + mt
                        act.wait_ge(s("scores_filled"), t * 8 + n + 1)
                        if mt == 0 and g >= 2:
                            UA.await_drain(act, f"oT{g - 2}", t)
                        nc.scalar.activation(pex[:, n % 4, :, :], pst[n % 2][:, :, :], ACT.Exp,
                                             scale=ATT_SCALE).then_inc(s("exp_done"), 1)

                def evac_oT(g):
                    m = UA.await_fill(act, f"oT{g}", t)
                    if g == 0 and later(t):
                        UA.await_drain(act, "tt1", t - 1)
                    UA.drained(nc.scalar.copy(oT[:, g, :], m[:, 0:L]), f"oT{g}")

                if real(t):
                    exps(0)
                    exps(1)
                    evac_oT(0)
                    exps(2)
                if real(t + 3):
                    evac_hT(UA, t + 3, (par + 1) % 2)
                if real(t):
                    evac_oT(1)
                    exps(3)
                    evac_oT(2)
                    evac_oT(3)

            run(act, *A_TURNS, turn_a)
            act.wait_ge(s("lnv_ready"), 2)
            nc.scalar.activation(lns[:, :], lnv[:, :], ACT.Sqrt).then_inc(s("lns_ready"), 1)

            def turn_b(t, par):
                if real(t + 1):
                    b = t + 1
                    act.wait_ge(s("fc1_filled"), b + 1)
                    slot = (par + 1) % 2
                    if not isinstance(b, int) or b >= 2:
                        UB.await_drain(act, "fc2", b - 2)
                    nc.scalar.activation(gT[0:96, slot, 0:4, :], pst[slot][0:96, :, :], ACT.Gelu_apprx_tanh)
                    nc.scalar.activation(gT[0:96, slot, 4:6, :], ps[slot][0:96, :].rearrange("p (c l) -> p c l", c=2),
                                         ACT.Gelu_apprx_tanh).then_inc(s("gelu_done"), 1)
                if real(t - 1):
                    m = UB.await_fill(act, "x2T", t - 1)
                    nc.scalar.copy(x2Ta[:, :], m[:, 0:L])
                    UB.drained(nc.scalar.copy(x2Tb[:, :], m[0:CB, L:2 * L]), "x2T")
                    m = UB.await_fill(act, "z", t - 1)
                    UB.drained(nc.scalar.copy(zT[:, :], m[0:R, 0:L]), "z")
                if real(t + 2):
                    evac_hT(UB, t + 2, par)

            run(act, *B_TURNS, turn_b)

        @block.vector
        def _(dve):
            steps = [0]

            def then(ins, name="dve_step"):
                steps[0] += 1
                ins.then_inc(s("dve_step"), 1)
                dve.wait_ge(s("dve_step"), steps[0])

            dve.sem_inc(s("max_done"), 2)
            dve.wait_ge(s("wqkv_loaded"), 48)
            def by_channel(src, dst):
                for k in range(2):
                    nc.vector.tensor_copy(dst[:, C * k:C * k + C].rearrange("p (d h) -> p d h", h=H),
                                          src[:, C * k:C * k + C].rearrange("p (h d) -> p d h", d=D)).then_inc(s("wqk_ready"), 1)

            by_channel(wqkv_a, wqk_a)
            dve.wait_ge(s("cexp_ready"), 1)
            then(nc.vector.tensor_scalar(cden[:, :], cexp[:, :], 1.0, None, ALU.add))
            then(nc.vector.reciprocal(crec[:, :], cden[:, :]))
            nc.vector.tensor_tensor(silu[:, 0:C], csb[:, :], crec[:, :], ALU.mult).then_inc(s("silu_ready"), 1)
            for i in range(2):
                dve.wait_ge(s("ada_filled"), i + 1)
                nc.vector.tensor_copy(ada[:, 432 * i:432 * i + 432], ps[i][0:B, 0:432]).then_inc(s("ada_copied"), 1)
            dve.wait_ge(s("ada_copied"), 2)
            for i in (1, 4):
                nc.vector.tensor_scalar(ada[:, C * i:C * i + C], ada[:, C * i:C * i + C], 1.0, None, ALU.add).then_inc(s("ada_ready"), 1)
            for i in range(4):
                dve.wait_ge(s("wrTb_filled"), i + 1)
                nc.vector.tensor_copy(wrT_b[:, :].rearrange("k (p r) -> k r p", r=VR)[:, 4 * i:4 * i + 4, :],
                                      ps[i % 2][0:CB, 0:4 * VP].rearrange("k (r p) -> k r p", p=VP)).then_inc(s("wrTb_ready"), 1)

            def statistics(n):
                for t in range(NT):
                    nc.vector.bn_stats(bst[:, t, :], xin[:, t, :]).then_inc(s("bn_done"), 1)
                dve.wait_ge(s("bn_done"), NT * (2 * n - 1))
                for t in range(NT):
                    nc.vector.bn_aggr(mv[:, t, :], bst[:, t, :]).then_inc(s("bn_done"), 1)
                dve.wait_ge(s("bn_done"), 2 * NT * n)
                nc.vector.tensor_scalar(lnv[:, :], mv[:, :, 1], ATT_EPS, None, ALU.add).then_inc(s("lnv_ready"), 1)
                dve.wait_ge(s("lns_ready"), n)
                then(nc.vector.reciprocal(lnr[:, :], lns[:, :]))
                then(nc.vector.tensor_tensor(lnt[:, :], lnr[:, :], lnr[:, :], ALU.mult))
                then(nc.vector.tensor_tensor(lnu[:, :], lnt[:, :], lnv[:, :], ALU.mult))
                then(nc.vector.tensor_scalar(lnt[:, :], lnu[:, :], -0.5, 1.5, ALU.mult, ALU.add))
                then(nc.vector.tensor_tensor(rstd[:, :], lnt[:, :], lnr[:, :], ALU.mult))

            dve.wait_ge(s("x_loaded"), 32)
            statistics(1)

            dve.wait_ge(s("wqkv_loaded"), 48)
            dve.wait_ge(s("mlp_loaded"), 80)
            for w, at, n in ((wqkv_b, 0, 3 * C), (wfc1_b, 3 * C, FF)):
                cols = slice(at, at + n)
                then(nc.vector.tensor_copy(wpart[:, 0, cols], w[:, :]))
                then(nc.vector.tensor_tensor(wrest[:, cols], w[:, :], wpart[:, 0, cols], ALU.subtract))
            then(nc.vector.tensor_copy(wpart[:, 1, :], wrest[:, :]))
            nc.vector.tensor_tensor(wpart[:, 2, :], wrest[:, :], wpart[:, 1, :], ALU.subtract).then_inc(s("wpart_ready"), 3)

            dve.wait_ge(s("gm_ready"), 2)
            dve.wait_ge(s("gram_filled"), 1)
            then(nc.vector.tensor_copy(gm[:, 0:R], pst[0][0:R, 0, 0:R]))
            nc.vector.tensor_copy(pT[:, :], pst[1][0:R, 0, 0:C]).then_inc(s("pT_ready"), 1)
            dve.wait_ge(s("ew_ready"), 3)
            then(nc.vector.reciprocal(rp[:, :], gm[0:1, 0:1]))
            nc.vector.tensor_scalar(ew[0:1, 0:R - 1], gm[0:1, 1:R], rp[0:1, 0:1], -1.0, ALU.mult, ALU.mult).then_inc(s("ew_set"), 1)
            state = pst[0][0:R, 0, 1:R + 1]

            def eliminated(i, u):
                dve.wait_ge(s("elim_filled"), i * 16 + 2 * u + 1)
                nc.vector.reciprocal(rp[:, :], state[0:1, 0:1]).then_inc(s("pivot"), 1)
                dve.wait_ge(s("elim_filled"), i * 16 + 2 * u + 2)
                nc.vector.tensor_copy(gm[:, 0:R], state)
                dve.wait_ge(s("pivot"), i * 8 + u + 1)
                nc.vector.tensor_scalar(ew[0:1, 0:R - 1], state[0:1, 1:R], rp[0:1, 0:1], -1.0, ALU.mult, ALU.mult).then_inc(s("ew_set"), 1)

            with dve.Fori(0, R // 8 - 1) as i:
                for u in range(8):
                    eliminated(i, u)
            for u in range(7):
                eliminated(R // 8 - 1, u)
            dve.wait_ge(s("linvT_filled"), 1)
            nc.vector.tensor_copy(linvT[:, :], pst[1][0:R, 0, 0:R]).then_inc(s("linvT_ready"), 1)
            dve.wait_ge(s("qtu_filled"), 1)
            then(nc.vector.tensor_copy(qtu[:, :], pst[0][0:R, 0, 0:C]))
            then(nc.vector.tensor_tensor(qsq[:, :], qtu[:, :], qtu[:, :], ALU.mult))
            nc.vector.tensor_reduce(qn[:, 0:1], qsq[:, :], AX.X, ALU.add).then_inc(s("qn_ready"), 1)
            dve.wait_ge(s("qn_root"), 1)
            then(nc.vector.reciprocal(qn[:, 2:3], qn[:, 1:2]))
            then(nc.vector.tensor_tensor(qn[:, 3:4], qn[:, 2:3], qn[:, 2:3], ALU.mult))
            then(nc.vector.tensor_tensor(qn[:, 4:5], qn[:, 3:4], qn[:, 0:1], ALU.mult))
            then(nc.vector.tensor_scalar(qn[:, 5:6], qn[:, 4:5], -0.5, 1.5, ALU.mult, ALU.add))
            then(nc.vector.tensor_tensor(qn[:, 6:7], qn[:, 5:6], qn[:, 2:3], ALU.mult))
            nc.vector.tensor_scalar(qt[:, :], qtu[:, :], qn[:, 6:7], None, ALU.mult).then_inc(s("qt_ready"), 1)
            dve.wait_ge(s("q_filled"), 1)
            then(nc.vector.tensor_copy(qa[:, :], pst[1][:, 0, 0:R]))
            nc.vector.tensor_copy(qb[:, :], pst[1][0:CB, 0, R:2 * R]).then_inc(s("q_ready"), 1)
            nc.vector.tensor_scalar(q1[:, :], qa[0:R, :], 0.5, None, ALU.mult).then_inc(s("q_ready"), 1)
            dve.wait_ge(s("upT_filled"), 1)
            upT = pst[0][0:R, 0:2, :].rearrange("p a (b n) -> p (a b) n", n=R)
            then(nc.vector.tensor_tensor(q0[:, :, :], up[:, :, :], upT, ALU.subtract))
            for i in range(2):
                nc.vector.tensor_scalar(aa[:, :, i, :], q0[:, :, :], (-1.0) ** i * 2.0 ** -SQUARINGS, None, ALU.mult).then_inc(s("aa_ready"), 1)
            dve.wait_ge(s("a2_filled"), 1)
            a2p = pst[1][0:R, 0:2, :].rearrange("p a (b n) -> p (a b) n", n=R)
            dve.wait_ge(s("aa_ready"), 2)
            dve.wait_ge(s("half_ready"), 2)
            then(nc.vector.tensor_copy(a2[:, :, :], a2p))
            then(nc.vector.scalar_tensor_tensor(out=q0[:, :, :], in0=a2[:, :, :], scalar=1.0 / 24, in1=half_i[:, :, :], op0=ALU.mult, op1=ALU.add))
            for i in range(2):
                nc.vector.scalar_tensor_tensor(out=qq[:, :, i, :], in0=aa[:, :, i, :], scalar=1.0 / 6, in1=q0[:, :, :],
                                               op0=ALU.mult, op1=ALU.add).then_inc(s("qq_ready"), 1)

            def ef_psum(i):
                return pst[i][0:R, :, :].rearrange("p a (e n) -> p a e n", n=R)

            hB = B // 2
            dve.wait_ge(s("e0_filled"), 1)
            for i in range(2):
                nc.vector.tensor_tensor(ef[:, hB * i:hB * i + hB, :, :],
                                        pst[i][0:R, 0:2, :].rearrange("p a (b e n) -> p (a b) e n", e=2, n=R),
                                        aa[:, hB * i:hB * i + hB, :, :], ALU.add).then_inc(s("ef_step"), 1)
            with dve.Fori(0, SQUARINGS) as j:
                for i in range(2):
                    dve.wait_ge(s("sq_filled"), j * 2 + i + 1)
                    e = ef[:, hB * i:hB * i + hB, :, :].rearrange("p b e n -> p (b e n)")
                    nc.vector.scalar_tensor_tensor(out=e, in0=e, scalar=2.0, in1=pst[i][0:R, 0:2, :].rearrange("p a n -> p (a n)"),
                                                   op0=ALU.mult, op1=ALU.add).then_inc(s("ef_step"), 1)
            dve.wait_ge(s("ef_step"), 2 * SQUARINGS + 2)

            def rotated_basis():
                dve.wait_ge(s("pivot_kept"), R)
                then(nc.vector.tensor_scalar(sdia[:, :], pm[:, :], 0.0, 2.0, ALU.is_ge, ALU.mult))
                then(nc.vector.tensor_scalar(srow[:, :], sdia[:, :], 1.0, None, ALU.subtract))
                then(nc.vector.tensor_tensor(sdia[:, :], srow[:, :], ident[0:R, 0:R], ALU.mult))
                then(nc.vector.tensor_reduce(scol[:, :], sdia[:, :], AX.X, ALU.add))
                then(nc.vector.tensor_scalar(ss[:, :], srow[:, :], scol[:, 0:1], None, ALU.mult))
                nc.vector.tensor_tensor(efs[:, :, :], ef[:, :, 1, :], ss[:, :].unsqueeze(1).to_broadcast([R, B, R]), ALU.mult).then_inc(s("efs_ready"), 1)
                for i in range(3):
                    n = min(3, B - 3 * i)
                    dve.wait_ge(s("fq_filled"), i + 1)
                    nc.vector.tensor_copy(fq[:, 3 * i:3 * i + n, :], pst[i % 2][0:R, 0:2, :].rearrange("p a l -> p (a l)")[:, 0:n * C]
                                          .rearrange("p (b n) -> p b n", n=C)).then_inc(s("fq_ready"), 1)

            dve.wait_ge(s("wstack_loaded"), 14 * 16)
            by_channel(wqkv_r, wqk_r)

            def wide(v):
                return v.unsqueeze(1).to_broadcast([128, LT, C])

            def modulate(n, slot, u, b):
                dve.wait_ge(s("normed"), n + 1)
                dve.wait_ge(s("ms_loaded"), n * 16 + 16)
                nc.vector.tensor_tensor(hs[:, :, :], hb[:, :, :], wide(ms[:, slot, C:2 * C]), ALU.mult).then_inc(s("scaled"), 1)
                dve.wait_ge(s("scaled"), n + 1)
                if later(b):
                    u.await_drain(dve, "hT", b - 1)
                nc.vector.tensor_tensor(h[:, :, :], hs[:, :, :], wide(ms[:, slot, 0:C]), ALU.add).then_inc(s("h_step"), 1)
                rem = h[:, :, 128:C]

                def stacked(first, count):
                    return hr[:, :, CB * first:CB * (first + count)].rearrange("p t (i c) -> p t i c", c=CB)

                def repeated(v, count):
                    return v.unsqueeze(2).to_broadcast([128, LT, count, CB])

                dve.wait_ge(s("h_step"), n * 5 + 1)
                nc.vector.tensor_copy(stacked(0, 3), repeated(rem, 3)).then_inc(s("h_step"), 1)
                dve.wait_ge(s("h_step"), n * 5 + 2)
                nc.vector.tensor_tensor(hrest[:, :, 0, :], rem, hr[:, :, 0:CB], ALU.subtract).then_inc(s("h_step"), 1)
                dve.wait_ge(s("h_step"), n * 5 + 3)
                nc.vector.tensor_copy(stacked(3, 2), repeated(hrest[:, :, 0, :], 2)).then_inc(s("h_step"), 1)
                dve.wait_ge(s("h_step"), n * 5 + 4)
                nc.vector.tensor_tensor(hr[:, :, 5 * CB:6 * CB], hrest[:, :, 0, :], hr[:, :, 3 * CB:4 * CB], ALU.subtract).then_inc(s("h_step"), 1)

            def normalise(b, n):
                if later(n):
                    dve.wait_ge(s("scaled"), n)
                for t in range(LT):
                    i = b * LT + t
                    ins = nc.vector.tensor_scalar(hb[:, t, :], xin[:, bass.ds(i, 1), :].rearrange("p a c -> p (a c)"),
                                                  mv[:, bass.ds(i, 1), 0], rstd[:, bass.ds(i, 1)],
                                                  ALU.subtract, ALU.mult)
                ins.then_inc(s("normed"), 1)

            def gated(m, b, which):
                return nc.vector.tensor_tensor(res[:, :, :], m[:, 0:LT * C].rearrange("p (t c) -> p t c", t=LT),
                                               gates[:, which, bass.ds(b, 1), :].to_broadcast([128, LT, C]), ALU.mult)

            def turn_a(t, par):
                if real(t - 1):
                    for lt in range(LT):
                        m = UA.await_fill(dve, f"tt{lt}", t - 1)
                        mh = m[:, :].rearrange("p (h e) -> p h e", e=32)
                        nc.vector.reciprocal(rden[:, lt, :], mh[:, :, D]).then_inc(s("rden_ready"), 1)
                        dve.wait_ge(s("rden_ready"), (t - 1) * LT + lt + 1)
                        UA.drained(nc.vector.tensor_tensor(otok[:, lt, 0:C].rearrange("p (h d) -> p h d", d=D), mh[:, :, 0:D],
                                                           rden[:, lt, :].unsqueeze(2).to_broadcast([128, H, D]), ALU.mult), f"tt{lt}")

                def maxima(us):
                    for u in us:
                        k, lt = u // 2, u % 2
                        dve.wait_ge(s("max_filled"), (t + 1) * 16 + u + 1)
                        nc.vector.tensor_reduce(nm[:, lt, 2 * k:2 * k + 2], ps[u % 2][:, :].rearrange("p (h l) -> p h l", h=2),
                                                AX.X, ALU.max, negate=True).then_inc(s("max_done"), 1)

                if real(t + 2):
                    b = t + 2
                    UA.await_drain(dve, "qk2", b)
                    nc.vector.tensor_tensor(qkr[:, :, :], qk32[:, :, :], parts[:, 0, :, :], ALU.subtract).then_inc(s("rest_ready"), 1)
                    dve.wait_ge(s("rest_ready"), b + 1)
                    if later(b):
                        dve.wait_ge(s("parts_written"), b * 48)
                    nc.vector.tensor_copy(parts[:, 1, :, :], qkr[:, :, :]).then_inc(s("mid_ready"), 1)
                    dve.wait_ge(s("mid_ready"), b + 1)
                    nc.vector.tensor_tensor(parts[:, 2, :, :], qkr[:, :, :], parts[:, 1, :, :], ALU.subtract).then_inc(s("low_ready"), 1)
                if real(t + 1):
                    maxima(range(4))
                    m = UA.await_fill(dve, "v", t + 1)
                    if real(t - 1):
                        UA.await_drain(dve, "oT3", t - 1)
                    slot = (par + 1) % 2
                    UA.drained(nc.vector.tensor_copy(ve[:, slot, :, :, 0:D], m[:, 0:LT * C].rearrange("p (t h d) -> p t h d", t=LT, d=D)), "v")
                    maxima(range(4, 6))
                if real(t - 1):
                    m = UA.await_fill(dve, "proj", t - 1)
                    dve.wait_ge(s("x1_ready"), t)
                    UA.drained(gated(m, t - 1, 0), "proj")
                    UA.await_drain(dve, "proj", t - 1)
                    xb = xin[:, bass.ds((t - 1) * LT, LT), :]
                    nc.vector.tensor_tensor(xb, xb, res[:, :, :], ALU.add).then_inc(s("x1_ready"), 1)
                if real(t + 3):
                    normalise(t + 3, t + 3)
                    modulate(t + 3, (par + 1) % 2, UA, t + 3)
                if real(t + 1):
                    b = t + 1
                    maxima(range(6, 16))
                    dve.wait_ge(s("max_done"), b * 16 + 18)
                    nc.vector.tensor_copy(nmb[:, :, 0, :], nm[:, :, :]).then_inc(s("shift_high"), 1)
                    dve.wait_ge(s("shift_high"), b + 1)
                    nc.vector.tensor_tensor(nmb[:, :, 1, :], nm[:, :, :], nmb[:, :, 0, :], ALU.subtract).then_inc(s("shift_ready"), 1)
                    m = UA.await_fill(dve, "nmT", b)
                    if later(b):
                        dve.wait_ge(s("shift_loaded"), b * 16)
                    UA.drained(nc.vector.tensor_copy(nmT[:, :], m[0:2 * H, 0:L // 2].bitcast(BF16)), "nmT")

            dve.sem_inc(s("x1_ready"), 1)
            dve.wait_ge(s("gates_loaded"), 32)
            dve.wait_ge(s("ve_zeroed"), 2)
            dve.wait_ge(s("h_one"), 2)
            run(dve, *A_TURNS, turn_a)

            dve.wait_ge(s("x1_ready"), B + 1)
            statistics(2)
            nc.vector.memset(gT[96:97, :, :, :], 1.0).then_inc(s("gT_one"), 1)
            rotated_basis()

            def turn_b(t, par):
                if real(t + 2):
                    normalise(t + 2, t + 2 + B)
                    modulate(t + 2 + B, par, UB, t + 2)
                if real(t):
                    m = UB.await_fill(dve, "fc2", t)
                    if later(t):
                        dve.wait_ge(s("x2_ready"), t)
                    UB.drained(gated(m, t, 1), "fc2")
                if real(t - 1):
                    b = t - 1
                    m = UB.await_fill(dve, "w", b)
                    if not isinstance(t, int) or b >= 2:
                        dve.wait_ge(s("out_written"), b * 16)
                    dve.wait_ge(s("x2_ready"), b + 1)
                    slot = (par + 1) % 2
                    nc.vector.tensor_tensor(osb[:, slot, :, :], m[:, 0:LT * C].rearrange("p (t c) -> p t c", t=LT),
                                            x2c[:, slot, :, :], ALU.add).then_inc(s("out_ready"), 1)
                    dve.wait_ge(s("out_ready"), b + 1)
                    dve.sem_inc(s("bank6_drained"), 1)

            run(dve, *B_TURNS, turn_b)

        @block.tensor
        def _(pe):
            mm = nc.tensor.matmul
            tr = nc.tensor.transpose
            pe.wait_ge(s("ident_ready"), 2)
            pe.wait_ge(s("ones_ready"), 2)
            pe.wait_ge(s("silu_ready"), 1)
            tr(ps[0][:, 0:B], silu[:, 0:128], ident[0:B, 0:B])
            tr(ps[0][0:CB + 1, B:2 * B], silu[:, 128:C + 1], ident[0:B, 0:B]).then_inc(s("siluT_filled"), 1)
            pe.wait_ge(s("siluT_ready"), 2)
            pe.wait_ge(s("wada_loaded"), 48)
            for i in range(2):
                mm(ps[i][0:B, 0:432], siluT_a[:, :], wada_a[:, 432 * i:432 * i + 432], start=True, stop=False)
                mm(ps[i][0:B, 0:432], siluT_b[:, :], wada_b[:, 432 * i:432 * i + 432], start=False, stop=True).then_inc(s("ada_filled"), 1)
            pe.wait_ge(s("wr_loaded"), 32)
            pe.wait_ge(s("ada_copied"), 2)
            for i in range(4):
                if i >= 2:
                    pe.wait_ge(s("wrTa_ready"), i - 1)
                    pe.wait_ge(s("wrTb_ready"), i - 1)
                ta = pst[i % 2][:, 0:2, :].rearrange("p a l -> p (a l)")
                for r in range(4):
                    last = tr(ta[:, VP * r:VP * r + VP], wr[:, 4 * i + r, 0:128], ident[0:VP, 0:VP])
                last.then_inc(s("wrTa_filled"), 1)
                for r in range(4):
                    last = tr(ps[i % 2][0:CB, VP * r:VP * r + VP], wr[:, 4 * i + r, 128:C], ident[0:VP, 0:VP])
                last.then_inc(s("wrTb_filled"), 1)
            pe.wait_ge(s("wrTa_ready"), 4)
            pe.wait_ge(s("wrTb_ready"), 4)
            for i in range(4):
                if i >= 2:
                    pe.wait_ge(s("v_ready"), i - 1)
                cols = slice(504 * i, 504 * i + 504)
                o = misc[6 + i % 2][0:B, 0:504]
                mm(o, siluT_a[:, :], wrT_a[:, cols], start=True, stop=False)
                mm(o, siluT_b[0:CB, :], wrT_b[:, cols], start=False, stop=False)
                mm(o, ones_row[0:1, 0:B], br[0:1, cols], start=False, stop=True).then_inc(s("v_filled"), 1)
            pe.wait_ge(s("p_loaded"), 32)
            tr(pst[1][0:R, 0, 0:128], pa[:, :], ident[:, :])
            tr(pst[1][0:R, 0, 128:C], pbm[:, :], ident[0:CB, 0:CB])
            mm(pst[0][0:R, 0, 0:R], pa[:, :], pa[:, :], start=True, stop=False)
            mm(pst[0][0:R, 0, 0:R], pbm[:, :], pbm[:, :], start=False, stop=True).then_inc(s("gram_filled"), 1)
            pe.wait_ge(s("pT_ready"), 1)
            with pe.Fori(0, R // 8) as i:
                for u in range(8):
                    pe.wait_ge(s("ew_set"), i * 8 + u + 1)
                    settled(pe, "pe")
                    mm(pst[0][0:R, 0, 0:R + 1], ew[:, :], gm[:, 0:R + 1], start=True, stop=True).then_inc(s("elim_filled"), 1)
                    pe.wait_ge(s("inv_step"), i * 8 + u + 1)
                    settled(pe, "pe")
                    mm(pst[1][0:R, 0, 0:R], ew[:, :], gm[:, R + 1:2 * R + 1], start=True, stop=True).then_inc(s("elim_filled"), 1)
            pe.wait_ge(s("inv_step"), R + 1)
            tr(pst[1][0:R, 0, 0:R], gm[:, R + 1:2 * R + 1], ident[0:R, 0:R]).then_inc(s("linvT_filled"), 1)
            pe.wait_ge(s("linvT_ready"), 1)
            mm(pst[0][0:R, 0, 0:C], linvT[:, :], pT[:, :], start=True, stop=True).then_inc(s("qtu_filled"), 1)
            pe.wait_ge(s("qt_ready"), 1)
            tr(pst[1][:, 0, 0:R], qt[:, 0:128], ident[0:R, 0:R])
            tr(pst[1][0:CB, 0, R:2 * R], qt[:, 128:C], ident[0:R, 0:R]).then_inc(s("q_filled"), 1)
            pe.wait_ge(s("up_loaded"), 16 * (R - 1))
            for b in range(B):
                last = tr(pst[0][0:R, b // 4, R * (b % 4):R * (b % 4) + R], up[:, b, :], ident[0:R, 0:R])
            last.then_inc(s("upT_filled"), 1)
            pe.wait_ge(s("aa_ready"), 2)
            for b in range(B):
                last = mm(pst[1][0:R, b // 4, R * (b % 4):R * (b % 4) + R], aa[:, b, 1, :], aa[:, b, 0, :], start=True, stop=True)
            last.then_inc(s("a2_filled"), 1)
            pe.wait_ge(s("qq_ready"), 2)

            def ef_out(b, e):
                b4 = b % 4
                return pst[b // 4][0:R, b4 // 2, (b4 % 2) * 128 + e * R:(b4 % 2) * 128 + e * R + R]

            for b in range(B):
                for e in range(2):
                    last = mm(ef_out(b, e), a2[:, b, :], qq[:, b, e, :], start=True, stop=True)
            last.then_inc(s("e0_filled"), 1)
            with pe.Fori(0, SQUARINGS) as j:
                for i in range(2):
                    pe.wait_ge(s("ef_step"), j * 2 + i + 1)
                    settled(pe, "pe")
                    for b in range(4 * i, 4 * i + 4):
                        mm(ef_out(b, 0), ef[:, b, 1, :], ef[:, b, 0, :], start=True, stop=True)
                        last = mm(ef_out(b, 1), ef[:, b, 0, :], ef[:, b, 1, :], start=True, stop=True)
                    last.then_inc(s("sq_filled"), 1)
            def rotate_basis():
                pe.wait_ge(s("efs_ready"), 1)
                for i in range(3):
                    if i == 2:
                        pe.wait_ge(s("fq_ready"), 1)
                    for b in range(3 * i, min(3 * i + 3, B)):
                        o = pst[i % 2][0:R, 0:2, :].rearrange("p a l -> p (a l)")
                        last = mm(o[:, C * (b - 3 * i):C * (b - 3 * i) + C], efs[:, b, :], qt[:, :], start=True, stop=True)
                    last.then_inc(s("fq_filled"), 1)
                pe.wait_ge(s("fq_ready"), 3)

            def two_chunks(m, src):
                for lt in range(LT):
                    tr(m[:, 128 * lt:128 * lt + 128], src[:, lt, 0:128], ident[:, :])
                    k = src.shape[2] - 128
                    last = tr(m[0:k, L + 128 * lt:L + 128 * lt + 128], src[:, lt, 128:128 + k], ident[:, :])
                return last

            def project(o, a, b, wa, wb):
                mm(o, a, wa, start=True, stop=False)
                return mm(o, b, wb, start=False, stop=True)

            def transpose_h(u, b, n):
                pe.wait_ge(s("h_step"), n * 5 + 5)
                m = u.claim(pe, "hT", b)
                for lt in range(LT):
                    tr(m[:, 128 * lt:128 * lt + 128], h[:, lt, 0:128], ident[:, :])
                    last = tr(m[0:SR, L + 64 * lt:L + 64 * lt + 64].bitcast(BF16), hr[:, lt, :], identb[:, :])
                u.filled(last, "hT")

            pe.wait_ge(s("h_one"), 2)
            pe.wait_ge(s("wqk_ready"), 4)
            pe.wait_ge(s("stacks_zeroed"), 3)
            pe.wait_ge(s("identb_ready"), 1)
            pe.wait_ge(s("wp_loaded"), 48)

            def turn_a(t, par):
                def use(name, b, make):
                    if real(b):
                        make(b)
                    else:
                        UA.skip(pe, name, b)

                def qk(name, chunks):
                    def make(b):
                        UA.await_drain(pe, "hT", b)
                        m = UA.claim(pe, name, b)
                        for c in chunks:
                            cols = slice(QC * c, QC * c + QC)
                            last = project(m[0:QC, (c % 2) * L:(c % 2) * L + L], wqk_a[:, cols], wqk_r[:, cols],
                                           hTa[:, par, :], hTr[:, par, :])
                        UA.filled(last, name)
                    use(name, t + 2, make)

                def by_token(lt):
                    def make(b):
                        UA.await_drain(pe, "oT3", b)
                        m = UA.claim(pe, f"tt{lt}", b)
                        for g in range(G):
                            last = tr(m[:, 128 * g:128 * g + 128], oT[:, g, 128 * lt:128 * lt + 128], ident[:, :])
                        UA.filled(last, f"tt{lt}")
                    use(f"tt{lt}", t - 1, make)

                def max_scores(us):
                    if not real(t + 1):
                        return
                    slot = (par + 1) % 2
                    if us[0] == 0:
                        pe.wait_ge(s("stacks_loaded"), (t + 1) * 96 + 96)
                    for u in us:
                        k, lt = u // 2, u % 2
                        pe.wait_ge(s("max_done"), (t + 1) * 16 + u + 1)
                        for i in range(2):
                            hd = 2 * k + i
                            last = mm(ps[u % 2][:, L * i:L * i + L], qs[0:KS, slot, hd, 128 * lt:128 * lt + 128],
                                      ks[0:KS, slot, hd, :], start=True, stop=True)
                        last.then_inc(s("max_filled"), 1)

                def values(b):
                    slot = (par + 1) % 2
                    m = UA.claim(pe, "v", b)
                    for lt in range(LT):
                        rows = slice(128 * lt, 128 * lt + 128)
                        last = project(m[:, C * lt:C * lt + C], hTa[:, slot, rows], hTr[:, slot, rows],
                                       wqkv_a[:, 2 * C:3 * C], wqkv_r[:, 2 * C:3 * C])
                    UA.filled(last, "v")

                def channels(b):
                    UA.await_drain(pe, "tt1", b)
                    m = UA.claim(pe, "oc", b)
                    UA.filled(two_chunks(m, otok), "oc")

                def projection(b):
                    UA.await_drain(pe, "oc", b)
                    m = UA.claim(pe, "proj", b)
                    for lt in range(LT):
                        rows = slice(128 * lt, 128 * lt + 128)
                        last = project(m[:, C * lt:C * lt + C], oTa[:, rows], oTb[:, rows], wp_a[:, :], wp_b[:, :])
                    UA.filled(last, "proj")

                def scores(g):
                    if not real(t):
                        return
                    if g == 0:
                        pe.wait_ge(s("shift_loaded"), t * 16 + 16)
                    for mt in range(LT):
                        n = 2 * g + mt
                        pe.wait_ge(s("exp_done"), t * 8 + n + 1)
                        for j in range(4):
                            last = mm(pst[n % 2][:, j, :], ks[0:KS + 2, par, 4 * g + j, 128 * mt:128 * mt + 128],
                                      qs[0:KS + 2, par, 4 * g + j, :], start=True, stop=True)
                        last.then_inc(s("scores_filled"), 1)

                def weighted(g):
                    def make(b):
                        m = UA.claim(pe, f"oT{g}", b)
                        for mt in range(LT):
                            pe.wait_ge(s("exp_done"), b * 8 + 2 * g + mt + 3)
                            for j in range(4):
                                last = mm(m[32 * j:32 * j + 32, 0:L], ve[:, par, mt, 4 * g + j, :], pex[:, (2 * g + mt) % 4, j, :],
                                          start=(mt == 0), stop=(mt == LT - 1))
                        UA.filled(last, f"oT{g}")
                    use(f"oT{g}", t, make)

                def shift(b):
                    pe.wait_ge(s("shift_ready"), b + 1)
                    m = UA.claim(pe, "nmT", b)
                    for lt in range(LT):
                        last = tr(m[0:2 * H, 64 * lt:64 * lt + 64].bitcast(BF16), nmb[:, lt, :, :].rearrange("p a h -> p (a h)"), identb[:, :])
                    UA.filled(last, "nmT")

                def next_hT(b):
                    transpose_h(UA, b, b)

                qk("qk01", (0, 1))
                by_token(0)
                by_token(1)
                qk("qk2", (2,))
                max_scores(range(0, 4))
                use("v", t + 1, values)
                use("oc", t - 1, channels)
                max_scores(range(4, 6))
                use("proj", t - 1, projection)
                scores(0)
                max_scores(range(6, 8))
                scores(1)
                max_scores(range(8, 10))
                weighted(0)
                max_scores(range(10, 12))
                scores(2)
                use("hT", t + 3, next_hT)
                max_scores(range(12, 14))
                weighted(1)
                max_scores(range(14, 16))
                scores(3)
                weighted(2)
                use("nmT", t + 1, shift)
                weighted(3)

            run(pe, *A_TURNS, turn_a)

            pe.wait_ge(s("mlp_loaded"), 80)
            pe.wait_ge(s("gT_one"), 1)
            pe.wait_ge(s("exp_done"), 8 * B + 2)
            rotate_basis()

            def turn_b(t, par):
                def use(name, b, make):
                    if real(b):
                        make(b)
                    else:
                        UB.skip(pe, name, b)

                def up_projection():
                    b, slot = t + 1, (par + 1) % 2
                    if not real(b):
                        return
                    UB.await_drain(pe, "hT", b)
                    if not isinstance(b, int) or b >= 2:
                        pe.wait_ge(s("gelu_done"), b - 1)
                    for c in range(FC):
                        o = pst[slot][0:96, c, :] if c < 4 else ps[slot][0:96, L * (c - 4):L * (c - 4) + L]
                        cols = slice(96 * c, 96 * c + 96)
                        last = project(o, wfc1_a[:, cols], wfc1_r[:, cols], hTa[:, slot, :], hTr[:, slot, :])
                    last.then_inc(s("fc1_filled"), 1)

                def x2_channels(b):
                    pe.wait_ge(s("x2_ready"), b + 1)
                    m = UB.claim(pe, "x2T", b)
                    UB.filled(two_chunks(m, x2c[:, (par + 1) % 2, :, :]), "x2T")

                def down_projection(b):
                    pe.wait_ge(s("gelu_done"), b + 1)
                    m = UB.claim(pe, "fc2", b)
                    for lt in range(LT):
                        for c in range(FC):
                            k = 97 if c == FC - 1 else 96
                            last = mm(m[:, C * lt:C * lt + C], gT[0:k, par, c, 128 * lt:128 * lt + 128], wfc2[0:k, c, :],
                                      start=(c == 0), stop=(c == FC - 1))
                    UB.filled(last, "fc2")

                def coordinates(b):
                    UB.await_drain(pe, "x2T", b)
                    m = UB.claim(pe, "z", b)
                    UB.filled(project(m[0:R, 0:L], qa[:, :], qb[:, :], x2Ta[:, :], x2Tb[:, :]), "z")

                def rotation(b):
                    UB.await_drain(pe, "z", b)
                    m = UB.claim(pe, "w", b)
                    for lt in range(LT):
                        last = mm(m[:, C * lt:C * lt + C], zT[:, 128 * lt:128 * lt + 128],
                                  fq[:, bass.ds(b, 1), :].rearrange("p a n -> p (a n)"), start=True, stop=True)
                    UB.filled(last, "w")

                up_projection()
                use("x2T", t - 1, x2_channels)
                use("fc2", t, down_projection)
                use("z", t - 1, coordinates)
                use("hT", t + 2, lambda b: transpose_h(UB, b, b + B))
                use("w", t - 1, rotation)

            run(pe, *B_TURNS, turn_b)


_INS = ['x', 'cond_1152', 'L0_cond_W_qkv', 'L0_cond_b_qkv', 'L0_cond_W_proj', 'L0_cond_b_proj', 'L0_cond_W_fc1',
        'L0_cond_b_fc1', 'L0_cond_W_fc2', 'L0_cond_b_fc2', 'L0_cond_W_ada', 'L0_cond_b_ada', 'L1_cond_P',
        'L1_cond_W', 'L1_cond_b']
_OUTS = [((8, 256, 144), 'float32')]


def kernel(**inputs):
    import numpy as _np
    import concourse.bacc as _bacc
    from concourse import mybir as _mybir
    from concourse.bass_utils import run_bass_kernel_spmd as _run

    nc = _bacc.Bacc("TRN2", target_bir_lowering=False, num_devices=1)
    arrays, args = {}, []
    for name in _INS:
        a = _np.ascontiguousarray(inputs[name])
        arrays[f"in_{name}_dram"] = a
        args.append(nc.dram_tensor(f"in_{name}_dram", a.shape, _mybir.dt.from_np(a.dtype), kind="ExternalInput").ap())
    for i, (shape, dtype) in enumerate(_OUTS):
        dt = _mybir.dt.from_np(_np.dtype(dtype))
        args.append(nc.dram_tensor(f"out_{i}_dram", shape, dt, kind="ExternalOutput").ap())
    cond_seq_program(nc, *args)
    r = _run(nc, [arrays], core_ids=[0])
    return r.results[0]["out_0_dram"]
```

```python
from contextlib import ExitStack

import concourse.bass as bass
from concourse import mybir

F32 = mybir.dt.float32
BF16 = mybir.dt.bfloat16
ACT = mybir.ActivationFunctionType
ALU = mybir.AluOpType
AX = mybir.AxisListType


def cond_seq_program(nc, x, cond, w_qkv, b_qkv, w_proj, b_proj, w_fc1, b_fc1, w_fc2, b_fc2,
                     w_ada, b_ada, p_mat, w_rot, b_rot, out):
    B, L, C = x.shape
    H = 16
    D = C // H
    FF = w_fc1.shape[1]
    R = p_mat.shape[1]
    NV = w_rot.shape[0]
    LT = L // 128
    NT = B * LT
    CB = C - 128
    QC = 96
    NQ = 2 * C // QC
    FC = FF // 128
    FL = FF - 128 * FC
    G = H // 4
    SR = 6 * CB + 3
    KS = 96
    ATT_SCALE = float(D) ** -0.5
    ATT_EPS = 1e-6
    SQUARINGS = 14
    BP = B // 2
    VR = 16
    VP = NV // VR

    Q_RUNS = [(0, 0, 1, 3), (3, 1, 1, 2), (5, 2, 1, 1)]
    K_RUNS = [(5, 0, 1, 1), (3, 0, 2, 1), (0, 0, 3, 1)]

    ctx = ExitStack()
    with ctx:
        def sb(name, shape, dt=F32):
            return ctx.enter_context(nc.sbuf_tensor(name, shape, dt))

        def pb(name, shape, dt=F32):
            return ctx.enter_context(nc.psum_tensor(name, shape, dt))

        def sem(name):
            return ctx.enter_context(nc.semaphore(name))

        scr_ada = nc.dram_tensor("scr_ada", [B, 6 * C], F32, kind="Internal").ap()
        scr_v = nc.dram_tensor("scr_v", [B, NV], F32, kind="Internal").ap()
        scr_qk = nc.dram_tensor("scr_qk", [3, 2 * C, L], BF16, kind="Internal").ap()

        ident = sb("ident", [128, 128])
        identb = sb("identb", [128, 128], BF16)
        half_i = sb("half_i", [2 * R, BP, 2 * R])
        wqkv_a = sb("wqkv_a", [128, 3 * C])
        wqkv_b = sb("wqkv_b", [CB + 1, 3 * C])
        wqk_a = sb("wqk_a", [128, 2 * C])
        wqkv_r = sb("wqkv_r", [SR, 3 * C], BF16)
        wfc1_r = sb("wfc1_r", [SR, FF], BF16)
        wqk_r = sb("wqk_r", [SR, 2 * C], BF16)
        wpart = sb("wpart", [CB + 1, 3, 3 * C + FF], BF16)
        wp_a = sb("wp_a", [128, C])
        wp_b = sb("wp_b", [CB + 1, C])
        wfc1_a = sb("wfc1_a", [128, FF])
        wfc1_b = sb("wfc1_b", [CB + 1, FF])
        wfc2 = sb("wfc2", [128, FC + 1, C])
        wada_a = sb("wada_a", [128, 6 * C])
        wada_b = sb("wada_b", [CB + 1, 6 * C])
        pa = sb("pa", [128, R])
        pbm = sb("pbm", [CB, R])
        wr = sb("wr", [VP, VR, C])
        wrT_a = sb("wrT_a", [128, NV])
        late = sb("late", [128, NV])
        wrT_b = late[0:CB + 1, :]
        csb = sb("csb", [B, C])
        cexp = sb("cexp", [B, C])
        cden = sb("cden", [B, C])
        crec = sb("crec", [B, C])
        silu = sb("silu", [B, C + 1])
        siluT_a = sb("siluT_a", [128, B])
        siluT_b = sb("siluT_b", [CB + 1, B])
        ada = sb("ada", [B, 6 * C])
        gates = sb("gates", [128, 2, B, C])
        ms = sb("ms", [128, 2, 2 * C])
        vsb = wr[0:B, :, :].rearrange("b r k -> b (r k)")[:, 0:NV]
        up = sb("up", [2 * R, BP, R])
        ub = sb("ub", [2 * R, BP, 2 * R])
        aa = sb("aa", [2 * R, BP, 2, 2 * R])
        a2 = sb("a2", [2 * R, BP, 2 * R])
        q0 = sb("q0", [2 * R, BP, 2 * R])
        qq = sb("qq", [2 * R, BP, 2, 2 * R])
        wrest = qq[0:CB + 1, :, :, :].rearrange("p b t r -> p (b t r)")[:, 0:3 * C + FF]
        ef = sb("ef", [2 * R, BP, 2, 2 * R])
        efs = sb("efs", [R, B, R])
        fq = sb("fq", [R, B, C])
        gm = sb("gm", [R, 2 * R + 1])
        ew = sb("ew", [R, 2, R])
        rp = sb("rp", [1, 1])
        linv = sb("linv", [R, R])
        linvT = sb("linvT", [R, R])
        pT = sb("pT", [R, C])
        qtu = sb("qtu", [R, C])
        qsq = sb("qsq", [R, C])
        qn = sb("qn", [R, 8])
        qt = sb("qt", [R, C])
        qa = sb("qa", [128, R])
        qb = sb("qb", [CB, R])
        q1 = sb("q1", [R, 2, R + 1])
        q1m = sb("q1m", [R, R + 1])
        q1r = sb("q1r", [R, R + 1])
        q1u = sb("q1u", [R, R])
        pm = sb("pm", [R, R])
        sgn = sb("sgn", [R, 8])
        srow = sb("srow", [R, R])
        sdia = sb("sdia", [R, R])
        scol = sb("scol", [R, 1])
        ss = sb("ss", [2 * R, R])
        xin = sb("xin", [128, NT, C])
        bst = sb("bst", [128, NT, 6])
        mv = sb("mv", [128, NT, 2])
        lnv = sb("lnv", [128, NT])
        lns = sb("lns", [128, NT])
        lnr = sb("lnr", [128, NT])
        lnt = sb("lnt", [128, NT])
        lnu = sb("lnu", [128, NT])
        rstd = sb("rstd", [128, NT])
        hb = sb("hb", [128, LT, C])
        hs = sb("hs", [128, LT, C])
        h = sb("h", [128, LT, C])
        hr = sb("hr", [128, LT, SR], BF16)
        hrest = sb("hrest", [128, LT, 2, CB])
        hTa = sb("hTa", [128, 2, L])
        hTr = sb("hTr", [SR, 2, L], BF16)
        qk32 = sb("qk32", [QC, NQ, L])
        qkr = sb("qkr", [QC, NQ, L])
        parts = sb("parts", [QC, 3, NQ, L], BF16)
        qs = sb("qs", [128, 2, H, L], BF16)
        ks = sb("ks", [128, 2, H, L], BF16)
        ve = sb("ve", [128, 2, LT, H, 32])
        nm = sb("nm", [128, LT, H])
        nmb = sb("nmb", [128, LT, 2, H], BF16)
        nmT = sb("nmT", [2 * H, L], BF16)
        pex = sb("pex", [128, 4, 4, L])
        oT = sb("oT", [128, G, L])
        rden = sb("rden", [128, LT, H])
        otok = sb("otok", [128, LT, C + 1])
        oTa = sb("oTa", [128, L])
        oTb = sb("oTb", [CB + 1, L])
        res = sb("res", [128, LT, C])
        gT = pex[:, :, :, :].rearrange("p a b l -> p (a b) l")[:, 0:2 * FC + 2, :].rearrange("p (s c) l -> p s c l", s=2)
        x2Ta = late[:, 0:L]
        x2Tb = late[0:CB, L:2 * L]
        zT = late[0:R, 2 * L:3 * L]
        x2c, osb = (late[:, at:at + 2 * LT * C].rearrange("p (s t c) -> p s t c", s=2, t=LT)
                    for at in (3 * L, 3 * L + 2 * LT * C))

        ps = [pb(f"ps{i}", [128, 512]) for i in range(2)]
        pst = [pb(f"pst{i}", [128, 4, L]) for i in range(2)]
        m6 = pb("m6", [128, 512])
        m7 = pb("m7", [128, 512])
        misc = {6: m6, 7: m7}

        S = {}

        def s(name):
            if name not in S:
                S[name] = sem(name)
            return S[name]

        A_STAGES = {"X": 0, "P": 0, "S": 0, "M": 1, "F": 2, "N": 2}
        A_USES = {6: [("sq00", "S"), ("hT", "N"), ("sq01", "S"), ("qk01", "F"), ("nmT", "M"), ("tt0", "P"), ("oc", "P")],
                  7: [("oT0", "X"), ("oT1", "X"), ("oT2", "X"), ("oT3", "X"), ("qk2", "F"), ("tt1", "P"), ("proj", "P")]}
        A_FIRST, A_LAST = -2, B - 1
        B_STAGES = {"R": -2, "D": 0, "U": 1, "N": 2}
        B_USES = {6: [("x2T", "R"), ("w", "R"), ("hT", "N")], 7: [("z", "R"), ("fc2", "D")]}
        B_FIRST, B_LAST = -2, B + 1

        class Shared:

            def __init__(self, stages, uses, first, base):
                self.where = {n: (bank, i, stages[st]) for bank, names in uses.items() for i, (n, st) in enumerate(names)}
                self.n = {bank: len(names) for bank, names in uses.items()}
                self.first, self.base = first, base

            def at(self, name, b):
                bank, i, offset = self.where[name]
                return bank, (b - offset - self.first) * self.n[bank] + self.base[bank] + i

            def claim(self, pe, name, b):
                bank, k = self.at(name, b)
                if not (isinstance(k, int) and k == 0):
                    pe.wait_ge(s(f"bank{bank}_drained"), k)
                return misc[bank]

            def filled(self, ins, name):
                ins.then_inc(s(f"bank{self.where[name][0]}_filled"), 1)

            def skip(self, pe, name, b):
                self.claim(pe, name, b)
                pe.sem_inc(s(f"bank{self.where[name][0]}_filled"), 1)
                pe.sem_inc(s(f"bank{self.where[name][0]}_drained"), 1)

            def await_fill(self, eng, name, b):
                bank, k = self.at(name, b)
                eng.wait_ge(s(f"bank{bank}_filled"), k + 1)
                return misc[bank]

            def drained(self, ins, name):
                ins.then_inc(s(f"bank{self.where[name][0]}_drained"), 1)

            def await_drain(self, eng, name, b):
                bank, k = self.at(name, b)
                eng.wait_ge(s(f"bank{bank}_drained"), k + 1)

        def settled(eng, name):
            eng.sem_inc(s(f"{name}_passed"), 1)

        UA = Shared(A_STAGES, A_USES, A_FIRST, {6: 0, 7: 0})
        UB = Shared(B_STAGES, B_USES, B_FIRST, {bank: (A_LAST - A_FIRST + 1) * len(names) for bank, names in A_USES.items()})

        def real(b):
            return not isinstance(b, int) or 0 <= b < B

        def squares(t):
            return not isinstance(t, int) or 0 <= t < SQUARINGS // 2

        def later(b):
            return not isinstance(b, int) or b > 0

        def run(eng, first, last, lo, hi, turn):
            for t in range(first, lo):
                turn(t, t % 2)
            with eng.Fori(0, (hi - lo) // 2) as i:
                for u in range(2):
                    turn(i * 2 + (lo + u), (lo + u) % 2)
            for t in range(hi, last + 1):
                turn(t, t % 2)

        UP_FIRST = 16
        UNROLLED = 4

        def left(i):
            return min(R, R - 8 * (i if isinstance(i, int) else UNROLLED) + 1)

        def eliminations(eng, step, between, last=8):
            for k in range(8 * UNROLLED):
                step(k // 8, k % 8)
                for work in between.get(k, ()):
                    work()
            with eng.Fori(0, R // 8 - 1 - UNROLLED) as i:
                for u in range(8):
                    step(i + UNROLLED, u)
            for u in range(last):
                step(R // 8 - 1, u)
                for work in between.get(R - 8 + u, ()):
                    work()

        A_TURNS = (A_FIRST + 1, A_LAST, 1, 5)
        B_TURNS = (B_FIRST, B_LAST, 2, 6)

        block = ctx.enter_context(nc.Block())

        values_psum = pst[0][:, 0:2, :].rearrange("p a l -> p (a l)")[:, 0:LT * C]

        def blocks(bank):
            return bank[:, 0:2, :].rearrange("p a (b n) -> p (a b) n", n=2 * R)

        ROTATED = [(0, 3, pst[1][0:R, 0:2, :].rearrange("p a l -> p (a l)")),
                   (3, 3, pst[1][0:R, 2:4, :].rearrange("p a l -> p (a l)")),
                   (6, B - 6, ps[1][0:R, :])]

        @block.sync
        def _(sp):
            sp.sem_inc(s("out_written"), 32)
            sp.dma_start(pa[:, :], p_mat[0:128, :]).then_inc(s("p_loaded"), 16)
            sp.dma_start(pbm[:, :], p_mat[128:C, :]).then_inc(s("p_loaded"), 16)
            sp.dma_start(csb[:, :], cond).then_inc(s("cond_loaded"), 16)
            sp.dma_start(wada_a[:, :], w_ada[0:128, :]).then_inc(s("wada_loaded"), 16)
            sp.dma_start(wada_b[0:CB, :], w_ada[128:C, :]).then_inc(s("wada_loaded"), 16)
            sp.dma_start(wada_b[CB:CB + 1, :], b_ada.rearrange("(a n) -> a n", a=1)).then_inc(s("wada_loaded"), 16)
            sp.dma_start(wr[:, :, :], w_rot.rearrange("(p r) k -> p r k", r=VR)).then_inc(s("wr_loaded"), 16)
            sp.dma_start(wrT_b[CB:CB + 1, :], b_rot.rearrange("(a n) -> a n", a=1)).then_inc(s("wr_loaded"), 16)
            xv = x.rearrange("b (t p) c -> p (b t) c", p=128)
            for q in range(2):
                sp.dma_start(xin[:, 8 * q:8 * q + 8, :], xv[:, 8 * q:8 * q + 8, :]).then_inc(s("x_loaded"), 16)
            sp.dma_start(wqkv_a[:, :], w_qkv[0:128, :]).then_inc(s("wqkv_loaded"), 16)
            sp.dma_start(wqkv_b[0:CB, :], w_qkv[128:C, :]).then_inc(s("wqkv_loaded"), 16)
            sp.dma_start(wqkv_b[CB:CB + 1, :], b_qkv.rearrange("(a n) -> a n", a=1)).then_inc(s("wqkv_loaded"), 16)
            sp.dma_start(wp_a[:, :], w_proj[0:128, :]).then_inc(s("wp_loaded"), 16)
            sp.dma_start(wp_b[0:CB, :], w_proj[128:C, :]).then_inc(s("wp_loaded"), 16)
            sp.dma_start(wp_b[CB:CB + 1, :], b_proj.rearrange("(a n) -> a n", a=1)).then_inc(s("wp_loaded"), 16)
            sp.dma_start(wfc1_a[:, :], w_fc1[0:128, :]).then_inc(s("mlp_loaded"), 16)
            sp.dma_start(wfc1_b[0:CB, :], w_fc1[128:C, :]).then_inc(s("mlp_loaded"), 16)
            sp.dma_start(wfc1_b[CB:CB + 1, :], b_fc1.rearrange("(a n) -> a n", a=1)).then_inc(s("mlp_loaded"), 16)
            sp.dma_start(wfc2[:, 0:FC, :], w_fc2[0:128 * FC, :].rearrange("(c p) n -> p c n", p=128)).then_inc(s("mlp_loaded"), 16)
            sp.dma_start(wfc2[0:FL, FC, :], w_fc2[128 * FC:FF, :]).then_inc(s("mlp_loaded"), 16)
            sp.dma_start(wfc2[FL:FL + 1, FC, :], b_fc2.rearrange("(a n) -> a n", a=1)).then_inc(s("mlp_loaded"), 16)
            sp.wait_ge(s("ada_ready"), 2)
            sp.dma_start(scr_ada, ada[:, :]).then_inc(s("ada_written"), 16)
            sp.wait_ge(s("ada_written"), 16)
            for i, at in enumerate((2, 5)):
                sp.dma_start(gates[:, i, :, :], scr_ada[:, at * C:at * C + C].partition_broadcast(128)).then_inc(s("gates_loaded"), 16)

            def modulation(b, slot, at, n):
                if later(n):
                    sp.wait_ge(s("ms_loaded"), n * 16)
                    settled(sp, "sp")
                if not isinstance(n, int) or n >= 2:
                    sp.wait_ge(s("h_step"), n * 5 - 5)
                settled(sp, "sp")
                sp.dma_start(ms[:, slot, :], scr_ada[bass.ds(b, 1), at:at + 2 * C].rearrange("a n -> (a n)").partition_broadcast(128)
                             ).then_inc(s("ms_loaded"), 16)

            def stack_weights():
                sp.wait_ge(s("wpart_ready"), 6)
                for dst, at, n in ((wqkv_r, 0, 3 * C), (wfc1_r, 3 * C, FF)):
                    for i, part in enumerate((0, 1, 2, 0, 1, 0)):
                        sp.dma_start(dst[CB * i:CB * i + CB, :], wpart[0:CB, part, at:at + n]).then_inc(s("wstack_loaded"), 16)
                    sp.dma_start(dst[6 * CB:SR, :], wpart[CB:CB + 1, :, at:at + n]).then_inc(s("wstack_loaded"), 16)

            sp.wait_ge(s("v_ready"), 4)
            sp.wait_ge(s("up_zeroed"), 1)
            sp.dma_start(scr_v, vsb).then_inc(s("v_written"), 16)
            modulation(0, 0, 0, 0)
            sp.wait_ge(s("v_written"), 16)
            at = 0
            for i in range(R - 1):
                if i == UP_FIRST:
                    stack_weights()
                n = R - 1 - i
                sp.dma_start(up[i:i + R + 1:R, :, i + 1:R], scr_v[:, at:at + n].rearrange("(e p) n -> e p n", e=2),
                             allow_slow_non_contiguous=(n == 1)).then_inc(s("up_loaded"), 16)
                at += n

            def turn_a(t, par):
                if real(t + 3):
                    modulation(t + 3, (par + 1) % 2, 0, t + 3)
                if real(t + 1):
                    b = t + 1
                    UA.await_drain(sp, "nmT", b)
                    settled(sp, "sp")
                    sp.dma_start(qs[KS:KS + 2, (par + 1) % 2, :, :].rearrange("t h l -> t (h l)"), nmT[:, :]).then_inc(s("shift_loaded"), 16)
                if real(t + 2):
                    b = t + 2
                    UA.await_drain(sp, "qk2", b)
                    settled(sp, "sp")
                    if later(b):
                        sp.wait_ge(s("stacks_loaded"), b * 96)
                        settled(sp, "sp")
                    sp.dma_start(scr_qk[0].rearrange("(c p) n -> p c n", p=QC), parts[:, 0, :, :]).then_inc(s("part0_written"), 16)
                    if real(t):
                        sp.wait_ge(s("exp_done"), t * 8 + 10)
                        settled(sp, "sp")
                    qkv = scr_qk.rearrange("t (k d h) n -> t k d (h n)", k=2, d=D)

                    def stack(to, which, row, part, n, repeat):
                        src = qkv[part:part + n, which]
                        if repeat > 1:
                            src = src.to_broadcast([repeat, D, H * L])
                        sp.dma_start(to[D * row:D * (row + n * repeat), par, :, :].rearrange("p h l -> p (h l)"), src).then_inc(s("stacks_loaded"), 16)

                    for i, name in enumerate(("mid_ready", "low_ready", None)):
                        if name:
                            sp.wait_ge(s(name), b + 1)
                            settled(sp, "sp")
                            sp.dma_start(scr_qk[i + 1].rearrange("(c p) n -> p c n", p=QC), parts[:, i + 1, :, :]).then_inc(s(f"part{i + 1}_written"), 16)
                        sp.wait_ge(s(f"part{i}_written"), b * 16 + 16)
                        settled(sp, "sp")
                        stack(qs, 0, *Q_RUNS[i])
                        stack(ks, 1, *K_RUNS[i])

            def turn_b(t, par):
                if real(t + 2):
                    modulation(t + 2, par, 3 * C, t + 2 + B)
                if real(t - 2):
                    b = t - 2
                    sp.wait_ge(s("out_ready"), b + 1)
                    settled(sp, "sp")
                    sp.wait_ge(s("out_written"), b * 16 + 32)
                    settled(sp, "sp")
                    sp.dma_start(out[bass.ds(b, 1)].rearrange("a (t p) c -> p (a t) c", p=128), osb[:, par, :, :]).then_inc(s("out_written"), 16)

            turn_a(A_FIRST, 0)
            run(sp, *A_TURNS, turn_a)
            run(sp, *B_TURNS, turn_b)
            sp.wait_ge(s("out_written"), 16 * B + 32)

        @block.gpsimd
        def _(pool):
            def zero_then_select(t, view, pattern, base, fill, name):
                nc.gpsimd.memset(t, 0.0).then_inc(s(name), 1)
                pool.wait_ge(s(name), 1)
                nc.gpsimd.affine_select(out=view, in_=view, compare_op=ALU.not_equal, fill=fill, base=base,
                                        pattern=pattern, channel_multiplier=1).then_inc(s(name), 1)

            zero_then_select(ident[:, :], ident[:, :], [[-1, 128]], 0, 1.0, "ident_ready")
            nc.gpsimd.memset(silu[:, C:C + 1], 1.0).then_inc(s("ones_ready"), 1)
            nc.gpsimd.memset(up[:, :, :], 0.0).then_inc(s("up_zeroed"), 1)
            nc.gpsimd.memset(ub[:, :, :], 0.0).then_inc(s("ub_zeroed"), 1)
            zero_then_select(gm[:, :], gm[:, R + 1:2 * R + 1], [[-1, R]], 0, 1.0, "gm_ready")
            for i in range(2):
                zero_then_select(ew[:, i, :], ew[:, i, :], [[-1, R]], -1, 1.0, f"ew{i}_ready")
                pool.wait_ge(s(f"ew{i}_ready"), 2)
                nc.gpsimd.memset(ew[0:1, i, R - 1:R], 1.0).then_inc(s(f"ew{i}_ready"), 1)
            nc.gpsimd.memset(sgn[:, :], -1.0).then_inc(s("signs_set_up"), 1)
            nc.gpsimd.memset(q1[:, :, R:R + 1], 0.0).then_inc(s("signs_set_up"), 1)
            zero_then_select(half_i[:, :, :], half_i[:, :, :], [[0, BP], [-1, 2 * R]], 0, 0.5, "half_ready")
            nc.gpsimd.memset(hr[:, :, 6 * CB:SR], 1.0).then_inc(s("h_one"), 1)
            nc.gpsimd.memset(otok[:, :, C:C + 1], 1.0).then_inc(s("h_one"), 1)
            nc.gpsimd.memset(qs[:, :, :, :], 0.0).then_inc(s("stacks_zeroed"), 1)

            pool.wait_ge(s("wqkv_loaded"), 48)
            pool.wait_ge(s("mlp_loaded"), 96)
            for n, (w, at, width) in enumerate(((wqkv_b, 0, 3 * C), (wfc1_b, 3 * C, FF))):
                cols = slice(at, at + width)
                nc.gpsimd.tensor_copy(wpart[:, 0, cols], w[:, :]).then_inc(s("wpart_ready"), 1)
                pool.wait_ge(s("wpart_ready"), 2 * n + 1)
                nc.gpsimd.tensor_tensor(wrest[:, cols], w[:, :], wpart[:, 0, cols], ALU.subtract).then_inc(s("wpart_ready"), 1)
            pool.wait_ge(s("wpart_ready"), 4)
            nc.gpsimd.tensor_copy(wpart[:, 1, :], wrest[:, :]).then_inc(s("wpart_ready"), 1)
            pool.wait_ge(s("wpart_ready"), 5)
            nc.gpsimd.tensor_tensor(wpart[:, 2, :], wrest[:, :], wpart[:, 1, :], ALU.subtract).then_inc(s("wpart_ready"), 1)

            nc.gpsimd.memset(ks[0:KS, :, :, :], 0.0).then_inc(s("stacks_zeroed"), 1)
            pool.wait_ge(s("stacks_zeroed"), 2)
            nc.gpsimd.memset(ks[KS:128, :, :, :], 1.0).then_inc(s("stacks_zeroed"), 1)
            pool.wait_ge(s("stacks_zeroed"), 3)
            nc.gpsimd.memset(ve[:, :, :, :, :], 0.0).then_inc(s("ve_zeroed"), 1)
            pool.wait_ge(s("ve_zeroed"), 1)
            nc.gpsimd.memset(ve[:, :, :, :, D:D + 1], 1.0).then_inc(s("ve_zeroed"), 1)
            pool.wait_ge(s("ident_ready"), 2)
            nc.gpsimd.tensor_copy(identb[:, :], ident[:, :]).then_inc(s("identb_ready"), 1)

            def by_channel(src, dst):
                for k in range(2):
                    nc.gpsimd.tensor_copy(dst[:, C * k:C * k + C].rearrange("p (d h) -> p d h", h=H),
                                          src[:, C * k:C * k + C].rearrange("p (h d) -> p d h", d=D)).then_inc(s("wqk_ready"), 1)

            by_channel(wqkv_a, wqk_a)

            pool.wait_ge(s("signs_set_up"), 2)
            pool.wait_ge(s("q_ready"), 2)

            def sign(k, u, W):
                done = k * 9

                def finished(ins):
                    ins.then_inc(s("sign_step"), 1)

                def then(ins, k, fixed=False):
                    finished(ins)
                    pool.wait_ge(s("sign_step"), done + k)
                    if fixed:
                        settled(pool, "sign_step")

                old, new = q1[:, u % 2, 0:W + 1], q1[:, 1 - u % 2, 0:W]
                col = bass.ds(k, 1)
                then(nc.gpsimd.tensor_tensor(q1m[:, 0:W + 1], old, ident[0:R, col].to_broadcast([R, W + 1]), ALU.mult), 1, True)
                then(nc.gpsimd.partition_all_reduce(q1r[:, 0:W + 1], q1m[:, 0:W + 1], R, bass.bass_isa.ReduceOp.add), 2, True)
                then(nc.gpsimd.tensor_scalar(sgn[:, 1:2], q1r[:, 0:1], 0.0, 0.5, ALU.is_lt, ALU.subtract), 3)
                then(nc.gpsimd.tensor_tensor(sgn[:, 2:3], sgn[:, 1:2], q1r[:, 0:1], ALU.subtract), 4)
                finished(nc.gpsimd.tensor_tensor(sgn[:, 3:4], sgn[:, 2:3], sgn[:, 2:3], ALU.mult))
                nc.gpsimd.tensor_tensor(sgn[:, 4:5], old[:, 0:1], sgn[:, 2:3], ALU.mult).then_inc(s("sign_column"), 1)
                pool.wait_ge(s("sign_step"), done + 5)
                finished(nc.gpsimd.tensor_tensor(sgn[:, 5:6], sgn[:, 3:4], sgn[:, 0:1], ALU.pow))
                nc.gpsimd.tensor_tensor(pm[:, col], sgn[:, 1:2], q1r[:, 0:1], ALU.subtract).then_inc(s("pivot_kept"), 1)
                pool.wait_ge(s("sign_step"), done + 6)
                pool.wait_ge(s("sign_column"), k + 1)
                then(nc.gpsimd.tensor_tensor(sgn[:, 6:7], sgn[:, 4:5], sgn[:, 5:6], ALU.mult), 7)
                then(nc.gpsimd.tensor_tensor(q1u[:, 0:W], q1r[:, 1:W + 1], sgn[:, 6:7].to_broadcast([R, W]), ALU.mult), 8)
                then(nc.gpsimd.tensor_tensor(new, old[:, 1:W + 1], q1u[:, 0:W], ALU.add), 9)

            for quarter in range(4):
                with pool.Fori(0, R // 32) as i:
                    for u in range(8):
                        sign(i * 8 + (R // 4 * quarter + u), u, R - R // 4 * quarter)

        @block.scalar
        def _(act):
            act.sem_inc(s("exp_done"), 2)
            act.wait_ge(s("cond_loaded"), 16)
            nc.scalar.activation(cexp[:, :], csb[:, :], ACT.Exp, scale=-1.0).then_inc(s("cexp_ready"), 1)

            def siluT():
                act.wait_ge(s("siluT_filled"), 1)
                nc.scalar.copy(siluT_a[:, :], ps[0][:, 0:B]).then_inc(s("siluT_ready"), 1)
                nc.scalar.copy(siluT_b[:, :], ps[0][0:CB + 1, B:2 * B]).then_inc(s("siluT_ready"), 1)

            def conditioning():
                act.wait_ge(s("ada_filled"), 1)
                for i in range(4):
                    n = 6 * C // 4
                    nc.scalar.copy(ada[:, n * i:n * i + n], ps[1][32 * i:32 * i + B, 0:n]).then_inc(s("ada_copied"), 1)

            def wrT(i, a):
                def copy():
                    name, dst, bank, k = ("wrTa", wrT_a, misc[6 + i % 2], 128) if a else ("wrTb", wrT_b, ps[i % 2], CB)
                    act.wait_ge(s(f"{name}_filled"), i + 1)
                    nc.scalar.copy(dst[0:k, :].rearrange("k (p r) -> k r p", r=VR)[:, 4 * i:4 * i + 4, :],
                                   bank[0:k, 0:4 * VP].rearrange("k (r p) -> k r p", p=VP)).then_inc(s(f"{name}_ready"), 1)
                return copy

            def v_quarter(i):
                def copy():
                    act.wait_ge(s("v_filled"), 1)
                    nc.scalar.copy(vsb[:, 504 * i:504 * i + 504], m6[32 * i:32 * i + B, 0:504]).then_inc(s("v_ready"), 1)
                return copy

            def ln_root():
                act.wait_ge(s("lnv_ready"), 1)
                nc.scalar.activation(lns[:, :], lnv[:, :], ACT.Sqrt).then_inc(s("lns_ready"), 1)

            def eliminated(i, u):
                act.wait_ge(s("inv_filled"), i * 8 + u + 1)
                nc.scalar.copy(gm[:, R + 1:2 * R + 1], pst[1][0:R, 0, 0:R]).then_inc(s("inv_step"), 1)

            act.wait_ge(s("gm_ready"), 2)
            act.sem_inc(s("inv_step"), 1)
            def evac_hT(u, b, slot):
                m = u.await_fill(act, "hT", b)
                if u is UA and (not isinstance(b, int) or b >= 2):
                    act.wait_ge(s("values_filled"), b - 1)
                if u is UB and (not isinstance(b, int) or b >= 2):
                    act.wait_ge(s("fc1_filled"), b - 1)
                nc.scalar.copy(hTa[:, slot, :], m[:, 0:L])
                u.drained(nc.scalar.copy(hTr[:, slot, :], m[0:SR, L:L + L // 2].bitcast(BF16)), "hT")

            def turn_a(t, par, parts_of_turn="ABC"):
                def exps(g):
                    for mt in range(LT):
                        n = 2 * g + mt
                        act.wait_ge(s("scores_filled"), t * 8 + n + 1)
                        if mt == 0 and g >= 2:
                            UA.await_drain(act, f"oT{g - 2}", t)
                        nc.scalar.activation(pex[:, n % 4, :, :], pst[n % 2][:, :, :], ACT.Exp,
                                             scale=ATT_SCALE).then_inc(s("exp_done"), 1)

                def evac_oT(g):
                    m = UA.await_fill(act, f"oT{g}", t)
                    if g == 0 and later(t):
                        UA.await_drain(act, "tt1", t - 1)
                    UA.drained(nc.scalar.copy(oT[:, g, :], m[:, 0:L]), f"oT{g}")

                if "A" in parts_of_turn:
                    if real(t):
                        exps(0)
                        exps(1)
                        evac_oT(0)
                        exps(2)
                        evac_oT(1)
                    if real(t + 2):
                        evac_hT(UA, t + 2, par)
                if "B" in parts_of_turn:
                    if real(t):
                        exps(3)
                        evac_oT(2)
                        evac_oT(3)
                    if real(t + 2):
                        b = t + 2
                        m = UA.await_fill(act, "qk01", b)
                        if later(b):
                            act.wait_ge(s("rest_ready"), b)
                            act.wait_ge(s("part0_written"), b * 16)
                        both = m[0:QC, :].rearrange("p (c l) -> p c l", c=2)
                        nc.scalar.copy(qk32[:, 0:2, :], both)
                        UA.drained(nc.scalar.copy(parts[:, 0, 0:2, :], both), "qk01")
                        m = UA.await_fill(act, "qk2", b)
                        nc.scalar.copy(qk32[:, 2, :], m[0:QC, 0:L])
                        UA.drained(nc.scalar.copy(parts[:, 0, 2, :], m[0:QC, 0:L]), "qk2")
                if "C" in parts_of_turn:
                    if real(t + 1):
                        b = t + 1
                        m = UA.await_fill(act, "nmT", b)
                        if later(b):
                            act.wait_ge(s("shift_loaded"), b * 16)
                        UA.drained(nc.scalar.copy(nmT[:, :], m[0:2 * H, 0:L // 2].bitcast(BF16)), "nmT")
                    if real(t):
                        m = UA.await_fill(act, "oc", t)
                        nc.scalar.copy(oTa[:, :], m[:, 0:L])
                        UA.drained(nc.scalar.copy(oTb[:, :], m[0:CB + 1, L:2 * L]), "oc")
                    if real(t + 2):
                        act.wait_ge(s("values_filled"), t + 3)
                        if real(t):
                            UA.await_drain(act, "oT3", t)
                        nc.scalar.copy(ve[:, par, :, :, 0:D], values_psum.rearrange("p (t h d) -> p t h d", t=LT, d=D)).then_inc(s("values_used"), 1)

            def by_channel():
                act.wait_ge(s("wstack_loaded"), 14 * 16)
                for k in range(2):
                    nc.scalar.copy(wqk_r[:, C * k:C * k + C].rearrange("p (d h) -> p d h", h=H),
                                   wqkv_r[:, C * k:C * k + C].rearrange("p (h d) -> p d h", d=D)).then_inc(s("wqk_ready"), 1)

            between = {1: [siluT], 5: [conditioning], 26: [ln_root]}
            between |= {7 + 2 * i + (1 - a): [wrT(i, a)] for i in range(4) for a in range(2)}
            between |= {18 + i: [v_quarter(i)] for i in range(4)}
            between |= {56: [by_channel], 58: [lambda: turn_a(A_FIRST, 0, "A")], 60: [lambda: turn_a(A_FIRST, 0, "B")]}
            eliminations(act, eliminated, between)
            act.wait_ge(s("qn_ready"), 1)
            nc.scalar.activation(qn[:, 1:2], qn[:, 0:1], ACT.Sqrt).then_inc(s("qn_root"), 1)

            act.wait_ge(s("ve_zeroed"), 2)
            turn_a(A_FIRST, 0, "C")
            run(act, *A_TURNS, turn_a)
            act.wait_ge(s("lnv_ready"), 2)
            nc.scalar.activation(lns[:, :], lnv[:, :], ACT.Sqrt).then_inc(s("lns_ready"), 1)

            def turn_b(t, par):
                if real(t - 2):
                    m = UB.await_fill(act, "x2T", t - 2)
                    nc.scalar.copy(x2Ta[:, :], m[:, 0:L])
                    UB.drained(nc.scalar.copy(x2Tb[:, :], m[0:CB, L:2 * L]), "x2T")
                    m = UB.await_fill(act, "z", t - 2)
                    UB.drained(nc.scalar.copy(zT[:, :], m[0:R, 0:L]), "z")
                if real(t + 1):
                    b = t + 1
                    act.wait_ge(s("fc1_filled"), b + 1)
                    slot = (par + 1) % 2
                    if not isinstance(b, int) or b >= 2:
                        UB.await_drain(act, "fc2", b - 2)
                    nc.scalar.activation(gT[:, slot, 0:FC, :], pst[slot][:, :, :], ACT.Gelu_apprx_tanh)
                    nc.scalar.activation(gT[0:FL, slot, FC, :], ps[slot][0:FL, 0:L], ACT.Gelu_apprx_tanh).then_inc(s("gelu_done"), 1)
                if real(t + 2):
                    evac_hT(UB, t + 2, par)

            run(act, *B_TURNS, turn_b)

        @block.vector
        def _(dve):
            steps = [0]

            def then(ins, name="dve_step"):
                steps[0] += 1
                ins.then_inc(s("dve_step"), 1)
                dve.wait_ge(s("dve_step"), steps[0])

            dve.sem_inc(s("max_done"), 2)

            def silu_of_cond():
                dve.wait_ge(s("cexp_ready"), 1)
                then(nc.vector.tensor_scalar(cden[:, :], cexp[:, :], 1.0, None, ALU.add))
                then(nc.vector.reciprocal(crec[:, :], cden[:, :]))
                nc.vector.tensor_tensor(silu[:, 0:C], csb[:, :], crec[:, :], ALU.mult).then_inc(s("silu_ready"), 1)

            def conditioning():
                dve.wait_ge(s("ada_copied"), 4)
                for i in (1, 4):
                    nc.vector.tensor_scalar(ada[:, C * i:C * i + C], ada[:, C * i:C * i + C], 1.0, None, ALU.add).then_inc(s("ada_ready"), 1)

            def tile_statistics(tiles):
                for t in tiles:
                    nc.vector.bn_stats(bst[:, t, :], xin[:, t, :]).then_inc(s("bn_done"), 1)

            def tile_aggregates(tiles, done):
                dve.wait_ge(s("bn_done"), done)
                for t in tiles:
                    nc.vector.bn_aggr(mv[:, t, :], bst[:, t, :]).then_inc(s("bn_done"), 1)

            def variance(n):
                dve.wait_ge(s("bn_done"), 2 * NT * n)
                nc.vector.tensor_scalar(lnv[:, :], mv[:, :, 1], ATT_EPS, None, ALU.add).then_inc(s("lnv_ready"), 1)

            def deviation(n, steps=range(5)):
                for i in steps:
                    if i == 0:
                        dve.wait_ge(s("lns_ready"), n)
                        ins = nc.vector.reciprocal(lnr[:, :], lns[:, :])
                    elif i == 1:
                        ins = nc.vector.tensor_tensor(lnt[:, :], lnr[:, :], lnr[:, :], ALU.mult)
                    elif i == 2:
                        ins = nc.vector.tensor_tensor(lnu[:, :], lnt[:, :], lnv[:, :], ALU.mult)
                    elif i == 3:
                        ins = nc.vector.tensor_scalar(lnt[:, :], lnu[:, :], -0.5, 1.5, ALU.mult, ALU.add)
                    else:
                        ins = nc.vector.tensor_tensor(rstd[:, :], lnt[:, :], lnr[:, :], ALU.mult)
                    then(ins)

            dve.wait_ge(s("gm_ready"), 2)
            dve.wait_ge(s("gram_filled"), 1)
            then(nc.vector.tensor_copy(gm[:, 0:R], pst[0][0:R, 0, 0:R]))
            nc.vector.tensor_copy(pT[:, :], pst[1][0:R, 0, 0:C]).then_inc(s("pT_ready"), 1)
            for i in range(2):
                dve.wait_ge(s(f"ew{i}_ready"), 3)
            then(nc.vector.reciprocal(rp[:, :], gm[0:1, 0:1]))
            nc.vector.tensor_scalar(ew[0:1, 0, 0:R - 1], gm[0:1, 1:R], rp[0:1, 0:1], -1.0, ALU.mult, ALU.mult).then_inc(s("ew_set"), 1)
            state = pst[0][0:R, 0, 1:R + 1]

            def eliminated(i, u):
                dve.wait_ge(s("elim_filled"), i * 8 + u + 1)
                nc.vector.reciprocal(rp[:, :], state[0:1, 0:1]).then_inc(s("pivot"), 1)
                nc.vector.tensor_copy(gm[:, 0:left(i)], state[:, 0:left(i)])
                dve.wait_ge(s("pivot"), i * 8 + u + 1)
                nc.vector.tensor_scalar(ew[0:1, (u + 1) % 2, 0:left(i) - 1], state[0:1, 1:left(i)], rp[0:1, 0:1], -1.0,
                                        ALU.mult, ALU.mult).then_inc(s("ew_set"), 1)

            def loaded_statistics(i):
                def work():
                    if i == 0:
                        dve.wait_ge(s("x_loaded"), 32)
                    tile_statistics(range(2 * i, 2 * i + 2))
                return work

            def scaled_matrix():
                dve.wait_ge(s("up_loaded"), 16 * (R - 1))
                dve.wait_ge(s("ub_zeroed"), 1)
                for e in range(2):
                    half = slice(R * e, R * e + R)
                    nc.vector.tensor_copy(ub[half, :, half], up[half, :, :]).then_inc(s("ub_ready"), 1)
                dve.wait_ge(s("upT_filled"), 1)
                then(nc.vector.tensor_tensor(q0[:, :, :], ub[:, :, :], blocks(pst[0]), ALU.subtract))
                for i in range(2):
                    nc.vector.tensor_scalar(aa[:, :, i, :], q0[:, :, :], (-1.0) ** i * 2.0 ** -SQUARINGS, None, ALU.mult).then_inc(s("aa_ready"), 1)

            def polynomial():
                dve.wait_ge(s("a2_filled"), 1)
                dve.wait_ge(s("aa_ready"), 2)
                dve.wait_ge(s("half_ready"), 2)
                then(nc.vector.tensor_copy(a2[:, :, :], blocks(pst[1])))
                then(nc.vector.scalar_tensor_tensor(out=q0[:, :, :], in0=a2[:, :, :], scalar=1.0 / 24, in1=half_i[:, :, :], op0=ALU.mult, op1=ALU.add))
                for i in range(2):
                    nc.vector.scalar_tensor_tensor(out=qq[:, :, i, :], in0=aa[:, :, i, :], scalar=1.0 / 6, in1=q0[:, :, :],
                                                   op0=ALU.mult, op1=ALU.add).then_inc(s("qq_ready"), 1)

            def exponential_of_scaled():
                dve.wait_ge(s("e0_filled"), 1)
                nc.vector.tensor_tensor(ef[:, :, :, :].rearrange("p b e n -> p (b e n)"), pst[0][:, :, :].rearrange("p a l -> p (a l)"),
                                        aa[:, :, :, :].rearrange("p b e n -> p (b e n)"), ALU.add).then_inc(s("ef_ready"), 1)

            def squared(level, i, t):
                if not squares(t):
                    return
                if level == 0:
                    m = UA.await_fill(dve, f"sq0{i}", t)
                else:
                    m = ps[i]
                    dve.wait_ge(s(f"sq1{i}_filled"), t + 1)
                e = ef[:, 2 * i:2 * i + 2, :, :].rearrange("p b e n -> p (b e n)")
                ins = nc.vector.scalar_tensor_tensor(out=e, in0=e, scalar=2.0, in1=m[:, :], op0=ALU.mult, op1=ALU.add)
                if level == 0:
                    UA.drained(ins, f"sq0{i}")
                else:
                    ins.then_inc(s(f"sq1{i}_drained"), 1)

            def rotated_basis():
                dve.wait_ge(s("pivot_kept"), R)
                for i in range(2):
                    dve.wait_ge(s(f"sq1{i}_drained"), SQUARINGS // 2)
                then(nc.vector.tensor_scalar(sdia[:, :], pm[:, :], 0.0, 2.0, ALU.is_lt, ALU.mult))
                then(nc.vector.tensor_scalar(srow[:, :], sdia[:, :], 1.0, None, ALU.subtract))
                then(nc.vector.tensor_tensor(sdia[:, :], srow[:, :], ident[0:R, 0:R], ALU.mult))
                then(nc.vector.tensor_reduce(scol[:, :], sdia[:, :], AX.X, ALU.add))
                then(nc.vector.tensor_scalar(ss[0:R, :], srow[:, :], scol[:, 0:1], None, ALU.mult))
                then(nc.vector.tensor_copy(ss[R:2 * R, :], ss[0:R, :]))
                for e in range(2):
                    half = slice(R * e, R * e + R)
                    nc.vector.tensor_tensor(efs[:, BP * e:BP * e + BP, :], ef[half, :, 1, half], ss[half, :].unsqueeze(1).to_broadcast([R, BP, R]),
                                            ALU.mult).then_inc(s("efs_ready"), 1)
                for b0, n, bank in ROTATED:
                    dve.wait_ge(s("fq_filled"), b0 // 3 + 1)
                    nc.vector.tensor_copy(fq[:, b0:b0 + n, :], bank[:, 0:n * C].rearrange("p (b n) -> p b n", n=C)).then_inc(s("fq_ready"), 1)

            def wide(v):
                return v.unsqueeze(1).to_broadcast([128, LT, C])

            def modulate(n, slot, u, b, parts_of_it="hr"):
                if "h" in parts_of_it:
                    modulated(n, slot, u, b)
                if "r" in parts_of_it:
                    stacked_parts(n)

            def modulated(n, slot, u, b):
                dve.wait_ge(s("normed"), n + 1)
                dve.wait_ge(s("ms_loaded"), n * 16 + 16)
                nc.vector.tensor_tensor(hs[:, :, :], hb[:, :, :], wide(ms[:, slot, C:2 * C]), ALU.mult).then_inc(s("scaled"), 1)
                dve.wait_ge(s("scaled"), n + 1)
                if later(b):
                    u.await_drain(dve, "hT", b - 1)
                nc.vector.tensor_tensor(h[:, :, :], hs[:, :, :], wide(ms[:, slot, 0:C]), ALU.add).then_inc(s("h_step"), 1)

            def stacked_parts(n):
                rem = h[:, :, 128:C]

                def stacked(first, count):
                    return hr[:, :, CB * first:CB * (first + count)].rearrange("p t (i c) -> p t i c", c=CB)

                def repeated(v, count):
                    return v.unsqueeze(2).to_broadcast([128, LT, count, CB])

                dve.wait_ge(s("h_step"), n * 5 + 1)
                nc.vector.tensor_copy(stacked(0, 3), repeated(rem, 3)).then_inc(s("h_step"), 1)
                dve.wait_ge(s("h_step"), n * 5 + 2)
                nc.vector.tensor_tensor(hrest[:, :, 0, :], rem, hr[:, :, 0:CB], ALU.subtract).then_inc(s("h_step"), 1)
                dve.wait_ge(s("h_step"), n * 5 + 3)
                nc.vector.tensor_copy(stacked(3, 2), repeated(hrest[:, :, 0, :], 2)).then_inc(s("h_step"), 1)
                dve.wait_ge(s("h_step"), n * 5 + 4)
                nc.vector.tensor_tensor(hr[:, :, 5 * CB:6 * CB], hrest[:, :, 0, :], hr[:, :, 3 * CB:4 * CB], ALU.subtract).then_inc(s("h_step"), 1)

            def normalise(b, n):
                if later(n):
                    dve.wait_ge(s("scaled"), n)
                for t in range(LT):
                    i = b * LT + t
                    ins = nc.vector.tensor_scalar(hb[:, t, :], xin[:, bass.ds(i, 1), :].rearrange("p a c -> p (a c)"),
                                                  mv[:, bass.ds(i, 1), 0], rstd[:, bass.ds(i, 1)],
                                                  ALU.subtract, ALU.mult)
                ins.then_inc(s("normed"), 1)

            def gated(m, b, which):
                return nc.vector.tensor_tensor(res[:, :, :], m[:, 0:LT * C].rearrange("p (t c) -> p t c", t=LT),
                                               gates[:, which, bass.ds(b, 1), :].to_broadcast([128, LT, C]), ALU.mult)

            def turn_a(t, par, parts_of_turn="AaBCDE"):
                def maxima(us):
                    for u in us:
                        if real(t + 1):
                            k, lt = u // 2, u % 2
                            dve.wait_ge(s("max_filled"), (t + 1) * 16 + u + 1)
                            nc.vector.tensor_reduce(nm[:, lt, 2 * k:2 * k + 2], ps[u % 2][:, :].rearrange("p (h l) -> p h l", h=2),
                                                    AX.X, ALU.max, negate=True).then_inc(s("max_done"), 1)

                if "A" in parts_of_turn:
                    if isinstance(t, int) and t == A_LAST:
                        dve.wait_ge(s("x1_ready"), B)
                        tile_statistics(range(NT - LT))
                        tile_aggregates(range(NT - LT), 2 * NT + NT - LT)
                    squared(0, 0, t)
                    if real(t + 2):
                        normalise(t + 2, t + 2)
                        modulate(t + 2, par, UA, t + 2, "h")
                if "a" in parts_of_turn:
                    if real(t + 2):
                        modulate(t + 2, par, UA, t + 2, "r")
                    if isinstance(t, int) and t == -1:
                        polynomial()
                if "B" in parts_of_turn:
                    maxima(range(0, 4))
                    if isinstance(t, int) and t == -1:
                        exponential_of_scaled()
                    maxima(range(4, 8))
                    squared(0, 1, t)
                    maxima(range(8, 16))
                    if real(t + 1):
                        b = t + 1
                        dve.wait_ge(s("max_done"), b * 16 + 18)
                        nc.vector.tensor_copy(nmb[:, :, 0, :], nm[:, :, :]).then_inc(s("shift_high"), 1)
                        dve.wait_ge(s("shift_high"), b + 1)
                        nc.vector.tensor_tensor(nmb[:, :, 1, :], nm[:, :, :], nmb[:, :, 0, :], ALU.subtract).then_inc(s("shift_ready"), 1)
                    squared(1, 0, t)
                    if real(t):
                        for lt in range(LT):
                            m = UA.await_fill(dve, f"tt{lt}", t)
                            mh = m[:, :].rearrange("p (h e) -> p h e", e=32)
                            nc.vector.reciprocal(rden[:, lt, :], mh[:, :, D]).then_inc(s("rden_ready"), 1)
                            dve.wait_ge(s("rden_ready"), t * LT + lt + 1)
                            UA.drained(nc.vector.tensor_tensor(otok[:, lt, 0:C].rearrange("p (h d) -> p h d", d=D), mh[:, :, 0:D],
                                                               rden[:, lt, :].unsqueeze(2).to_broadcast([128, H, D]), ALU.mult), f"tt{lt}")
                    if real(t + 2):
                        b = t + 2
                        UA.await_drain(dve, "qk2", b)
                        nc.vector.tensor_tensor(qkr[:, :, :], qk32[:, :, :], parts[:, 0, :, :], ALU.subtract).then_inc(s("rest_ready"), 1)
                if "C" in parts_of_turn and real(t + 2):
                    b = t + 2
                    dve.wait_ge(s("rest_ready"), b + 1)
                    if later(b):
                        dve.wait_ge(s("part1_written"), b * 16)
                    nc.vector.tensor_copy(parts[:, 1, :, :], qkr[:, :, :]).then_inc(s("mid_ready"), 1)
                if "D" in parts_of_turn and real(t + 2):
                    b = t + 2
                    dve.wait_ge(s("mid_ready"), b + 1)
                    if later(b):
                        dve.wait_ge(s("part2_written"), b * 16)
                    nc.vector.tensor_tensor(parts[:, 2, :, :], qkr[:, :, :], parts[:, 1, :, :], ALU.subtract).then_inc(s("low_ready"), 1)
                if "E" in parts_of_turn:
                    squared(1, 1, t)
                    if real(t):
                        m = UA.await_fill(dve, "proj", t)
                        dve.wait_ge(s("x1_ready"), t + 1)
                        UA.drained(gated(m, t, 0), "proj")
                        UA.await_drain(dve, "proj", t)
                        xb = xin[:, bass.ds(t * LT, LT), :]
                        nc.vector.tensor_tensor(xb, xb, res[:, :, :], ALU.add).then_inc(s("x1_ready"), 1)
                    if isinstance(t, int) and t == -2:
                        scaled_matrix()

            between = {0: [silu_of_cond], 6: [conditioning], 25: [lambda: variance(1)]}
            between |= {27 + i: [lambda i=i: deviation(1, [i])] for i in range(5)}
            between |= {15 + i: [loaded_statistics(i)] for i in range(8)}
            between |= {23 + i: [lambda i=i: tile_aggregates(range(8 * i, 8 * i + 8), NT)] for i in range(2)}
            between |= {56: [lambda: turn_a(A_FIRST, 0, "A")], 57: [lambda: turn_a(A_FIRST, 0, "a")], 61: [lambda: turn_a(A_FIRST, 0, "B")], 62: [lambda: turn_a(A_FIRST, 0, "C")]}
            dve.wait_ge(s("h_one"), 2)
            eliminations(dve, eliminated, between, last=7)
            dve.wait_ge(s("linvT_filled"), 1)
            nc.vector.tensor_copy(linvT[:, :], pst[1][0:R, 0, 0:R]).then_inc(s("linvT_ready"), 1)
            turn_a(A_FIRST, 0, "D")
            dve.wait_ge(s("qtu_filled"), 1)
            then(nc.vector.tensor_copy(qtu[:, :], pst[0][0:R, 0, 0:C]))
            then(nc.vector.tensor_tensor(qsq[:, :], qtu[:, :], qtu[:, :], ALU.mult))
            nc.vector.tensor_reduce(qn[:, 0:1], qsq[:, :], AX.X, ALU.add).then_inc(s("qn_ready"), 1)
            dve.wait_ge(s("qn_root"), 1)
            then(nc.vector.reciprocal(qn[:, 2:3], qn[:, 1:2]))
            then(nc.vector.tensor_tensor(qn[:, 3:4], qn[:, 2:3], qn[:, 2:3], ALU.mult))
            then(nc.vector.tensor_tensor(qn[:, 4:5], qn[:, 3:4], qn[:, 0:1], ALU.mult))
            then(nc.vector.tensor_scalar(qn[:, 5:6], qn[:, 4:5], -0.5, 1.5, ALU.mult, ALU.add))
            then(nc.vector.tensor_tensor(qn[:, 6:7], qn[:, 5:6], qn[:, 2:3], ALU.mult))
            nc.vector.tensor_scalar(qt[:, :], qtu[:, :], qn[:, 6:7], None, ALU.mult).then_inc(s("qt_ready"), 1)
            dve.wait_ge(s("q_filled"), 1)
            then(nc.vector.tensor_copy(qa[:, :], pst[1][:, 0, 0:R]))
            nc.vector.tensor_copy(qb[:, :], pst[1][0:CB, 0, R:2 * R]).then_inc(s("q_ready"), 1)
            nc.vector.tensor_scalar(q1[:, 0, 0:R], qa[0:R, :], 0.5, None, ALU.mult).then_inc(s("q_ready"), 1)

            dve.sem_inc(s("x1_ready"), 1)
            dve.wait_ge(s("gates_loaded"), 32)
            dve.wait_ge(s("ve_zeroed"), 2)
            turn_a(A_FIRST, 0, "E")
            run(dve, *A_TURNS, turn_a)

            dve.wait_ge(s("x1_ready"), B + 1)
            tile_statistics(range(NT - LT, NT))
            tile_aggregates(range(NT - LT, NT), 4 * NT - LT)
            variance(2)
            deviation(2)
            nc.vector.memset(gT[FL:FL + 1, :, FC, :], 1.0).then_inc(s("gT_one"), 1)

            def turn_b(t, par):
                if real(t + 2):
                    normalise(t + 2, t + 2 + B)
                    modulate(t + 2 + B, par, UB, t + 2)
                if real(t - 2):
                    b = t - 2
                    m = UB.await_fill(dve, "w", b)
                    dve.wait_ge(s("out_written"), b * 16 + 16)
                    nc.vector.tensor_tensor(osb[:, par, :, :], m[:, 0:LT * C].rearrange("p (t c) -> p t c", t=LT),
                                            x2c[:, par, :, :], ALU.add).then_inc(s("out_ready"), 1)
                    dve.wait_ge(s("out_ready"), b + 1)
                    dve.sem_inc(s("bank6_drained"), 1)
                if real(t):
                    m = UB.await_fill(dve, "fc2", t)
                    UB.drained(gated(m, t, 1), "fc2")
                    UB.await_drain(dve, "fc2", t)
                    nc.vector.tensor_tensor(x2c[:, par, :, :], xin[:, bass.ds(t * LT, LT), :], res[:, :, :], ALU.add).then_inc(s("x2_ready"), 1)
                if isinstance(t, int) and t == 1:
                    rotated_basis()

            run(dve, *B_TURNS, turn_b)

        @block.tensor
        def _(pe):
            mm = nc.tensor.matmul
            tr = nc.tensor.transpose
            pe.wait_ge(s("ident_ready"), 2)
            pe.wait_ge(s("p_loaded"), 32)
            tr(pst[1][0:R, 0, 0:128], pa[:, :], ident[:, :])
            tr(pst[1][0:R, 0, 128:C], pbm[:, :], ident[0:CB, 0:CB])
            mm(pst[0][0:R, 0, 0:R], pa[:, :], pa[:, :], start=True, stop=False)
            mm(pst[0][0:R, 0, 0:R], pbm[:, :], pbm[:, :], start=False, stop=True).then_inc(s("gram_filled"), 1)
            pe.wait_ge(s("pT_ready"), 1)

            def siluT():
                pe.wait_ge(s("ones_ready"), 1)
                pe.wait_ge(s("silu_ready"), 1)
                tr(ps[0][:, 0:B], silu[:, 0:128], ident[0:B, 0:B])
                tr(ps[0][0:CB + 1, B:2 * B], silu[:, 128:C + 1], ident[0:B, 0:B]).then_inc(s("siluT_filled"), 1)

            def quarters(bank, weights, n, part):
                a, w = (siluT_a, siluT_b)[part], weights[part]
                for i in range(4):
                    last = mm(bank[32 * i:32 * i + B, 0:n], a[:, :], w[:, n * i:n * i + n], start=(part == 0), stop=(part == 1))
                return last

            def conditioning(part):
                if part == 0:
                    pe.wait_ge(s("siluT_ready"), 2)
                    pe.wait_ge(s("wada_loaded"), 48)
                last = quarters(ps[1], (wada_a, wada_b), 6 * C // 4, part)
                if part == 1:
                    last.then_inc(s("ada_filled"), 1)

            def wrT(i, a):
                def transposes():
                    if i == 0:
                        pe.wait_ge(s("wr_loaded"), 32)
                        pe.wait_ge(s("ada_copied"), 4)
                    if i >= 2:
                        pe.wait_ge(s("wrTa_ready" if a else "wrTb_ready"), i - 1)
                    bank, lo, hi = (misc[6 + i % 2], 0, 128) if a else (ps[i % 2], 128, C)
                    for r in range(4):
                        last = tr(bank[0:hi - lo, VP * r:VP * r + VP], wr[:, 4 * i + r, lo:hi], ident[0:VP, 0:VP])
                    last.then_inc(s("wrTa_filled" if a else "wrTb_filled"), 1)
                return transposes

            def entries(part):
                if part == 0:
                    pe.wait_ge(s("wrTa_ready"), 4)
                    pe.wait_ge(s("wrTb_ready"), 4)
                last = quarters(m6, (wrT_a, wrT_b), NV // 4, part)
                if part == 1:
                    last.then_inc(s("v_filled"), 1)

            def eliminate(i, u):
                k = i * 8 + u
                pe.wait_ge(s("ew_set"), k + 1)
                settled(pe, "pe")
                mm(pst[0][0:R, 0, 0:left(i) + 1], ew[:, u % 2, :], gm[:, 0:left(i) + 1], start=True, stop=True).then_inc(s("elim_filled"), 1)
                pe.wait_ge(s("inv_step"), k + 1)
                settled(pe, "pe")
                mm(pst[1][0:R, 0, 0:R], ew[:, u % 2, :], gm[:, R + 1:2 * R + 1], start=True, stop=True).then_inc(s("inv_filled"), 1)

            def transpose_upper():
                pe.wait_ge(s("values_used"), 1)
                pe.wait_ge(s("ub_ready"), 2)
                for p in range(BP):
                    last = tr(blocks(pst[0])[:, p, :], ub[:, p, :], ident[:, :])
                last.then_inc(s("upT_filled"), 1)

            def square_matrix():
                pe.wait_ge(s("aa_ready"), 2)
                for p in range(BP):
                    last = mm(blocks(pst[1])[:, p, :], aa[:, p, 1, :], aa[:, p, 0, :], start=True, stop=True)
                last.then_inc(s("a2_filled"), 1)

            def times_square():
                pe.wait_ge(s("qq_ready"), 2)
                o = pst[0][:, :, :].rearrange("p a (e n) -> p a e n", e=2)
                for p in range(BP):
                    for e in range(2):
                        last = mm(o[:, p, e, :], a2[:, p, :], qq[:, p, e, :], start=True, stop=True)
                last.then_inc(s("e0_filled"), 1)

            def rotate_basis():
                pe.wait_ge(s("efs_ready"), 2)
                for b0, n, bank in ROTATED:
                    for b in range(b0, b0 + n):
                        last = mm(bank[:, C * (b - b0):C * (b - b0) + C], efs[:, b, :], qt[:, :], start=True, stop=True)
                    last.then_inc(s("fq_filled"), 1)
                pe.wait_ge(s("fq_ready"), len(ROTATED))

            def two_chunks(m, src):
                for lt in range(LT):
                    tr(m[:, 128 * lt:128 * lt + 128], src[:, lt, 0:128], ident[:, :])
                    k = src.shape[2] - 128
                    last = tr(m[0:k, L + 128 * lt:L + 128 * lt + 128], src[:, lt, 128:128 + k], ident[:, :])
                return last

            def project(o, a, b, wa, wb):
                mm(o, a, wa, start=True, stop=False)
                return mm(o, b, wb, start=False, stop=True)

            def transpose_h(u, b, n):
                pe.wait_ge(s("h_step"), n * 5 + 5)
                m = u.claim(pe, "hT", b)
                for lt in range(LT):
                    tr(m[:, 128 * lt:128 * lt + 128], h[:, lt, 0:128], ident[:, :])
                    last = tr(m[0:SR, L + 64 * lt:L + 64 * lt + 64].bitcast(BF16), hr[:, lt, :], identb[:, :])
                u.filled(last, "hT")

            def turn_a(t, par, parts_of_turn="ABCD"):
                def use(name, b, make):
                    if real(b):
                        make(b)
                    else:
                        UA.skip(pe, name, b)

                def qk(name, chunks):
                    def make(b):
                        UA.await_drain(pe, "hT", b)
                        m = UA.claim(pe, name, b)
                        for c in chunks:
                            cols = slice(QC * c, QC * c + QC)
                            last = project(m[0:QC, (c % 2) * L:(c % 2) * L + L], wqk_a[:, cols], wqk_r[:, cols],
                                           hTa[:, par, :], hTr[:, par, :])
                        UA.filled(last, name)
                    use(name, t + 2, make)

                def by_token(lt):
                    def make(b):
                        UA.await_drain(pe, "oT3", b)
                        m = UA.claim(pe, f"tt{lt}", b)
                        for g in range(G):
                            last = tr(m[:, 128 * g:128 * g + 128], oT[:, g, 128 * lt:128 * lt + 128], ident[:, :])
                        UA.filled(last, f"tt{lt}")
                    use(f"tt{lt}", t, make)

                def max_scores(us):
                    if not real(t + 1):
                        return
                    slot = (par + 1) % 2
                    if us[0] == 0:
                        pe.wait_ge(s("stacks_loaded"), (t + 1) * 96 + 96)
                    for u in us:
                        k, lt = u // 2, u % 2
                        pe.wait_ge(s("max_done"), (t + 1) * 16 + u + 1)
                        if u < 2 and later(t) and squares(t - 1):
                            pe.wait_ge(s(f"sq1{u}_drained"), t)
                        for i in range(2):
                            hd = 2 * k + i
                            last = mm(ps[u % 2][:, L * i:L * i + L], qs[0:KS, slot, hd, 128 * lt:128 * lt + 128],
                                      ks[0:KS, slot, hd, :], start=True, stop=True)
                        last.then_inc(s("max_filled"), 1)

                def values(b):
                    if real(t):
                        pe.wait_ge(s("exp_done"), t * 8 + 9)
                    elif t == -1:
                        pe.wait_ge(s("ef_ready"), 1)
                    for lt in range(LT):
                        rows = slice(128 * lt, 128 * lt + 128)
                        last = project(values_psum[:, C * lt:C * lt + C], hTa[:, par, rows], hTr[:, par, rows],
                                       wqkv_a[:, 2 * C:3 * C], wqkv_r[:, 2 * C:3 * C])
                    last.then_inc(s("values_filled"), 1)

                def channels(b):
                    UA.await_drain(pe, "tt1", b)
                    m = UA.claim(pe, "oc", b)
                    UA.filled(two_chunks(m, otok), "oc")

                def projection(b):
                    UA.await_drain(pe, "oc", b)
                    m = UA.claim(pe, "proj", b)
                    for lt in range(LT):
                        rows = slice(128 * lt, 128 * lt + 128)
                        last = project(m[:, C * lt:C * lt + C], oTa[:, rows], oTb[:, rows], wp_a[:, :], wp_b[:, :])
                    UA.filled(last, "proj")

                def scores(g):
                    if not real(t):
                        return
                    if g == 0:
                        pe.wait_ge(s("shift_loaded"), t * 16 + 16)
                        if real(t + 1):
                            pe.wait_ge(s("values_used"), t + 2)
                        if not later(t):
                            pe.wait_ge(s("ef_ready"), 1)
                    for mt in range(LT):
                        n = 2 * g + mt
                        pe.wait_ge(s("exp_done"), t * 8 + n + 1)
                        for j in range(4):
                            last = mm(pst[n % 2][:, j, :], ks[0:KS + 2, par, 4 * g + j, 128 * mt:128 * mt + 128],
                                      qs[0:KS + 2, par, 4 * g + j, :], start=True, stop=True)
                        last.then_inc(s("scores_filled"), 1)

                def weighted(g):
                    def make(b):
                        m = UA.claim(pe, f"oT{g}", b)
                        for mt in range(LT):
                            pe.wait_ge(s("exp_done"), b * 8 + 2 * g + mt + 3)
                            for j in range(4):
                                last = mm(m[32 * j:32 * j + 32, 0:L], ve[:, par, mt, 4 * g + j, :], pex[:, (2 * g + mt) % 4, j, :],
                                          start=(mt == 0), stop=(mt == LT - 1))
                        UA.filled(last, f"oT{g}")
                    use(f"oT{g}", t, make)

                def shift(b):
                    pe.wait_ge(s("shift_ready"), b + 1)
                    m = UA.claim(pe, "nmT", b)
                    for lt in range(LT):
                        last = tr(m[0:2 * H, 64 * lt:64 * lt + 64].bitcast(BF16), nmb[:, lt, :, :].rearrange("p a h -> p (a h)"), identb[:, :])
                    UA.filled(last, "nmT")

                def square(level, i):
                    if not squares(t):
                        if level == 0:
                            UA.skip(pe, f"sq0{i}", t)
                        return
                    if level == 1:
                        UA.await_drain(pe, f"sq0{i}", t)
                        pe.wait_ge(s("max_done"), (t + 1) * 16 + 17 + i)
                        m = ps[i]
                    else:
                        if later(t):
                            pe.wait_ge(s(f"sq1{i}_drained"), t)
                        else:
                            pe.wait_ge(s("ef_ready"), 1)
                        m = UA.claim(pe, f"sq0{i}", t)
                    o = m[:, :].rearrange("p (b e n) -> p b e n", b=2, e=2)
                    for b in range(2):
                        for e in range(2):
                            last = mm(o[:, b, e, :], ef[:, 2 * i + b, 1 - e, :], ef[:, 2 * i + b, e, :], start=True, stop=True)
                    if level == 0:
                        UA.filled(last, f"sq0{i}")
                    else:
                        last.then_inc(s(f"sq1{i}_filled"), 1)

                def next_hT(b):
                    transpose_h(UA, b, b)

                if "A" in parts_of_turn:
                    scores(0)
                    square(0, 0)
                    scores(1)
                    weighted(0)
                    scores(2)
                    weighted(1)
                    use("hT", t + 2, next_hT)
                    if isinstance(t, int) and t == -1:
                        square_matrix()
                if "B" in parts_of_turn:
                    max_scores(range(0, 4))
                    if isinstance(t, int) and t == -1:
                        times_square()
                    scores(3)
                    max_scores(range(4, 6))
                    weighted(2)
                    max_scores(range(6, 8))
                    square(0, 1)
                    max_scores(range(8, 10))
                    weighted(3)
                    max_scores(range(10, 12))
                    qk("qk01", (0, 1))
                if "C" in parts_of_turn:
                    max_scores(range(12, 14))
                    qk("qk2", (2,))
                if "D" in parts_of_turn:
                    max_scores(range(14, 16))
                    square(1, 0)
                    use("nmT", t + 1, shift)
                    square(1, 1)
                    by_token(0)
                    by_token(1)
                    use("oc", t, channels)
                    if real(t + 2):
                        values(t + 2)
                    use("proj", t, projection)
                    if isinstance(t, int) and t == -2:
                        transpose_upper()

            def first_hT():
                pe.wait_ge(s("h_one"), 2)
                pe.wait_ge(s("identb_ready"), 1)
                turn_a(A_FIRST, 0, "A")

            def first_qk01():
                pe.wait_ge(s("wqk_ready"), 4)
                turn_a(A_FIRST, 0, "B")

            between = {1: [siluT]}
            between |= {3 + i: [lambda i=i: conditioning(i)] for i in range(2)}
            between |= {7 + 2 * i + (1 - a): [wrT(i, a)] for i in range(4) for a in range(2)}
            between |= {16 + i: [lambda i=i: entries(i)] for i in range(2)}
            between |= {58: [first_hT], 59: [first_qk01], 60: [lambda: turn_a(A_FIRST, 0, "C")]}
            eliminations(pe, eliminate, between)
            pe.wait_ge(s("inv_step"), R + 1)
            tr(pst[1][0:R, 0, 0:R], gm[:, R + 1:2 * R + 1], ident[0:R, 0:R]).then_inc(s("linvT_filled"), 1)
            pe.wait_ge(s("linvT_ready"), 1)
            mm(pst[0][0:R, 0, 0:C], linvT[:, :], pT[:, :], start=True, stop=True).then_inc(s("qtu_filled"), 1)
            pe.wait_ge(s("qt_ready"), 1)
            tr(pst[1][:, 0, 0:R], qt[0:R, 0:128], ident[0:R, 0:R])
            tr(pst[1][0:CB, 0, R:2 * R], qt[0:R, 128:C], ident[0:R, 0:R]).then_inc(s("q_filled"), 1)
            pe.wait_ge(s("stacks_zeroed"), 3)
            pe.wait_ge(s("wp_loaded"), 48)

            turn_a(A_FIRST, 0, "D")
            run(pe, *A_TURNS, turn_a)

            pe.wait_ge(s("mlp_loaded"), 96)
            pe.wait_ge(s("gT_one"), 1)
            pe.wait_ge(s("exp_done"), 8 * B + 2)

            def turn_b(t, par):
                def use(name, b, make):
                    if real(b):
                        make(b)
                    else:
                        UB.skip(pe, name, b)

                def up_projection(chunks):
                    b, slot = t + 1, (par + 1) % 2
                    if not real(b):
                        return
                    if chunks[0] == 0:
                        UB.await_drain(pe, "hT", b)
                        if not isinstance(b, int) or b >= 2:
                            pe.wait_ge(s("gelu_done"), b - 1)
                    for c in chunks:
                        o = pst[slot][:, c, :] if c < FC else ps[slot][0:FL, 0:L]
                        cols = slice(128 * c, min(128 * c + 128, FF))
                        last = project(o, wfc1_a[:, cols], wfc1_r[:, cols], hTa[:, slot, :], hTr[:, slot, :])
                    if chunks[-1] == FC:
                        last.then_inc(s("fc1_filled"), 1)

                def x2_channels(b):
                    pe.wait_ge(s("x2_ready"), b + 1)
                    m = UB.claim(pe, "x2T", b)
                    UB.filled(two_chunks(m, x2c[:, par, :, :]), "x2T")

                def down_projection(b):
                    pe.wait_ge(s("gelu_done"), b + 1)
                    m = UB.claim(pe, "fc2", b)
                    for lt in range(LT):
                        for c in range(FC + 1):
                            k = 128 if c < FC else FL + 1
                            last = mm(m[:, C * lt:C * lt + C], gT[0:k, par, c, 128 * lt:128 * lt + 128], wfc2[0:k, c, :],
                                      start=(c == 0), stop=(c == FC))
                    UB.filled(last, "fc2")

                def coordinates(b):
                    UB.await_drain(pe, "x2T", b)
                    m = UB.claim(pe, "z", b)
                    UB.filled(project(m[0:R, 0:L], qa[:, :], qb[:, :], x2Ta[:, :], x2Tb[:, :]), "z")

                def rotation(b):
                    UB.await_drain(pe, "z", b)
                    m = UB.claim(pe, "w", b)
                    for lt in range(LT):
                        last = mm(m[:, C * lt:C * lt + C], zT[:, 128 * lt:128 * lt + 128],
                                  fq[:, bass.ds(b, 1), :].rearrange("p a n -> p (a n)"), start=True, stop=True)
                    UB.filled(last, "w")

                use("x2T", t - 2, x2_channels)
                up_projection(range(0, 3))
                use("z", t - 2, coordinates)
                up_projection(range(3, FC + 1))
                use("w", t - 2, rotation)
                use("hT", t + 2, lambda b: transpose_h(UB, b, b + B))
                use("fc2", t, down_projection)
                if isinstance(t, int) and t == 1:
                    rotate_basis()

            run(pe, *B_TURNS, turn_b)


_INS = ['x', 'cond_1152', 'L0_cond_W_qkv', 'L0_cond_b_qkv', 'L0_cond_W_proj', 'L0_cond_b_proj', 'L0_cond_W_fc1',
        'L0_cond_b_fc1', 'L0_cond_W_fc2', 'L0_cond_b_fc2', 'L0_cond_W_ada', 'L0_cond_b_ada', 'L1_cond_P',
        'L1_cond_W', 'L1_cond_b']
_OUTS = [((8, 256, 144), 'float32')]


def kernel(**inputs):
    import numpy as _np
    import concourse.bacc as _bacc
    from concourse import mybir as _mybir
    from concourse.bass_utils import run_bass_kernel_spmd as _run

    nc = _bacc.Bacc("TRN2", target_bir_lowering=False, num_devices=1)
    arrays, args = {}, []
    for name in _INS:
        a = _np.ascontiguousarray(inputs[name])
        arrays[f"in_{name}_dram"] = a
        args.append(nc.dram_tensor(f"in_{name}_dram", a.shape, _mybir.dt.from_np(a.dtype), kind="ExternalInput").ap())
    for i, (shape, dtype) in enumerate(_OUTS):
        dt = _mybir.dt.from_np(_np.dtype(dtype))
        args.append(nc.dram_tensor(f"out_{i}_dram", shape, dt, kind="ExternalOutput").ap())
    cond_seq_program(nc, *args)
    r = _run(nc, [arrays], core_ids=[0])
    return r.results[0]["out_0_dram"]
```
